# Optimizing a Trainium2 kernel written in Bass

```python
import numpy as np
import jax
import jax.numpy as jnp

def _softmax(x, axis=-1):
    return jax.nn.softmax(x, axis=axis)

def _gelu(x):
    return jax.nn.gelu(x, approximate=True)

def _silu(x):
    return jax.nn.silu(x)

def _sigmoid(x):
    return jax.nn.sigmoid(x)

def _layernorm(x, axis=-1, eps=1e-05):
    m = jnp.mean(x, axis=axis, keepdims=True)
    v = jnp.var(x, axis=axis, keepdims=True)
    return (x - m) / jnp.sqrt(v + eps)

def _scatter_add(tgt, idx, src, axis=0):
    return tgt.at[idx].add(src)

def _segment_sum(src, seg, n):
    return jax.ops.segment_sum(src, seg, n)
kernel_name = 'mk_audio_tower_d1_tok_audfeat768_r4_6ced37'

def setup_inputs(seed: int=0):
    np.random.seed(seed)
    _w = jnp.asarray

    def _rec_inputs():
        import jax
        import jax.numpy as jnp
        _rk = jax.random.key(seed)
        x = -0.000392918 + 0.999932 * jax.random.normal(jax.random.fold_in(_rk, 1), (64, 256, 128), jnp.float32)
        return x
    x = _rec_inputs()

    def _L0_tok_setup():
        import jax, jax.numpy as jnp
        import numpy as np
        PATCH_LEN = 16
        STRIDE = 8
        EPS = 1e-05
        key = jax.random.key(seed)
        k1, k2, k3 = jax.random.split(key, 3)
        B, S, F = (32, 1024, 128)
        d_model = 192
        patch_dim = PATCH_LEN * F
        x = jax.random.normal(k1, (B, S, F), dtype=jnp.float32)
        W = jax.random.normal(k2, (d_model, patch_dim), dtype=jnp.float32) * (1.0 / np.sqrt(patch_dim))
        b = jax.random.normal(k3, (d_model,), dtype=jnp.float32) * 0.01
        gamma = jnp.ones((d_model,), dtype=jnp.float32)
        beta = jnp.zeros((d_model,), dtype=jnpp.float32) if False else jnp.zeros((d_model,), dtype=jnp.float32)
        return {'x': x, 'W': W, 'b': b, 'gamma': gamma, 'beta': beta}
    _L0_tok_all = _L0_tok_setup()
    _L0_tok_in = {k: v for k, v in _L0_tok_all.items() if k in ('W', 'b', 'gamma', 'beta')}
    del _L0_tok_all

    def _L0_attn_setup():
        import jax, jax.numpy as jnp
        import numpy as np
        D_MODEL = 192
        D_STATE = 64
        D_CONV = 4
        EXPAND = 2
        HEADDIM = 64
        D_INNER = EXPAND * D_MODEL
        NHEADS = D_INNER // HEADDIM
        CONV_DIM = D_INNER + 2 * D_STATE
        D_IN_PROJ = 2 * D_INNER + 2 * D_STATE + NHEADS
        BATCH, SEQLEN = (2, 256)
        EPS = 1e-05

        def _forward(x, ln_w, ln_b, W_in, conv_w, conv_b, dt_bias, A_log, D, rms_w, W_out):
            b, l, _ = x.shape
            mu = jnp.mean(x, -1, keepdims=True)
            var = jnp.mean((x - mu) ** 2, -1, keepdims=True)
            xn = (x - mu) * jax.lax.rsqrt(var + EPS) * ln_w + ln_b
            zxbcdt = xn @ W_in
            z = zxbcdt[..., :D_INNER]
            xBC = zxbcdt[..., D_INNER:D_INNER + CONV_DIM]
            dt_raw = zxbcdt[..., -NHEADS:]
            xp = jnp.pad(xBC, ((0, 0), (D_CONV - 1, 0), (0, 0)))
            xBC = sum((xp[:, k:k + l, :] * conv_w[:, k] for k in range(D_CONV))) + conv_b
            xBC = jax.nn.silu(xBC)
            xh = xBC[..., :D_INNER].reshape(b, l, NHEADS, HEADDIM)
            Bm = xBC[..., D_INNER:D_INNER + D_STATE]
            Cm = xBC[..., D_INNER + D_STATE:]
            dt = jax.nn.softplus(dt_raw + dt_bias)
            A = -jnp.exp(A_log)
            decay = jnp.exp(dt * A)

            def step(h, inp):
                dec_t, dt_t, x_t, B_t, C_t = inp
                h = h * dec_t[..., None, None] + (dt_t[..., None] * x_t)[..., None] * B_t[:, None, None, :]
                y = jnp.einsum('bhpn,bn->bhp', h, C_t)
                return (h, y)
            h0 = jnp.zeros((b, NHEADS, HEADDIM, D_STATE), x.dtype)
            seq = (decay.transpose(1, 0, 2), dt.transpose(1, 0, 2), xh.transpose(1, 0, 2, 3), Bm.transpose(1, 0, 2), Cm.transpose(1, 0, 2))
            _, ys = jax.lax.scan(step, h0, seq)
            y = ys.transpose(1, 0, 2, 3) + D[None, None, :, None] * xh
            y = y.reshape(b, l, D_INNER)
            g = y * jax.nn.silu(z)
            g = g * jax.lax.rsqrt(jnp.mean(g * g, -1, keepdims=True) + EPS) * rms_w
            return g @ W_out + x
        key = jax.random.key(seed)
        ks = jax.random.split(key, 8)
        n = lambda i, shape, s: jax.random.normal(ks[i], shape, jnp.float32) * s
        return {'x': n(0, (BATCH, SEQLEN, D_MODEL), 1.0), 'ln_w': jnp.ones((D_MODEL,), jnp.float32), 'ln_b': jnp.zeros((D_MODEL,), jnp.float32), 'W_in': n(1, (D_MODEL, D_IN_PROJ), 0.02), 'conv_w': n(2, (CONV_DIM, D_CONV), 0.2), 'conv_b': jnp.zeros((CONV_DIM,), jnp.float32), 'dt_bias': n(3, (NHEADS,), 0.5), 'A_log': jnp.log(jnp.linspace(1.0, 16.0, NHEADS, dtype=jnp.float32)), 'D': jnp.ones((NHEADS,), jnp.float32), 'rms_w': jnp.ones((D_INNER,), jnp.float32), 'W_out': n(4, (D_INNER, D_MODEL), 0.02)}
    _L0_attn_all = _L0_attn_setup()
    _L0_attn_in = {k: v for k, v in _L0_attn_all.items() if k in ('ln_w', 'ln_b', 'W_in', 'conv_w', 'conv_b', 'dt_bias', 'A_log', 'D', 'rms_w', 'W_out')}
    del _L0_attn_all

    def _L0_ffn_setup():
        import jax, jax.numpy as jnp
        import numpy as np
        B, T, H, F, E = (128, 32, 192, 768, 3)
        key = jax.random.key(seed)
        ks = jax.random.split(key, 4)
        s = 0.02
        return {'x': jax.random.normal(ks[0], (B, T, H), jnp.float32), 'Wg': jax.random.normal(ks[1], (E, H), jnp.float32) * s, 'W1': jax.random.normal(ks[2], (E, H, F), jnp.float32) * s, 'b1': jnp.zeros((E, F), jnp.float32), 'W2': jax.random.normal(ks[3], (E, F, H), jnp.float32) * s, 'b2': jnp.zeros((E, H), jnp.float32)}
    _L0_ffn_all = _L0_ffn_setup()
    _L0_ffn_in = {k: v for k, v in _L0_ffn_all.items() if k in ('Wg', 'W1', 'b1', 'W2', 'b2')}
    del _L0_ffn_all
    return {'x': x, 'L0_tok_W': _L0_tok_in['W'], 'L0_tok_b': _L0_tok_in['b'], 'L0_tok_gamma': _L0_tok_in['gamma'], 'L0_tok_beta': _L0_tok_in['beta'], 'L0_attn_ln_w': _L0_attn_in['ln_w'], 'L0_attn_ln_b': _L0_attn_in['ln_b'], 'L0_attn_W_in': _L0_attn_in['W_in'], 'L0_attn_conv_w': _L0_attn_in['conv_w'], 'L0_attn_conv_b': _L0_attn_in['conv_b'], 'L0_attn_dt_bias': _L0_attn_in['dt_bias'], 'L0_attn_A_log': _L0_attn_in['A_log'], 'L0_attn_D': _L0_attn_in['D'], 'L0_attn_rms_w': _L0_attn_in['rms_w'], 'L0_attn_W_out': _L0_attn_in['W_out'], 'L0_ffn_Wg': _L0_ffn_in['Wg'], 'L0_ffn_W1': _L0_ffn_in['W1'], 'L0_ffn_b1': _L0_ffn_in['b1'], 'L0_ffn_W2': _L0_ffn_in['W2'], 'L0_ffn_b2': _L0_ffn_in['b2']}

def reference(x, L0_tok_W, L0_tok_b, L0_tok_gamma, L0_tok_beta, L0_attn_ln_w, L0_attn_ln_b, L0_attn_W_in, L0_attn_conv_w, L0_attn_conv_b, L0_attn_dt_bias, L0_attn_A_log, L0_attn_D, L0_attn_rms_w, L0_attn_W_out, L0_ffn_Wg, L0_ffn_W1, L0_ffn_b1, L0_ffn_W2, L0_ffn_b2):
    import jax
    import jax.numpy as jnp

    def _L0_tok_ref(x, W, b, gamma, beta):
        import jax, jax.numpy as jnp
        import numpy as np
        PATCH_LEN = 16
        STRIDE = 8
        EPS = 1e-05
        B, S, F = x.shape
        n_patches = (S - PATCH_LEN) // STRIDE + 1
        idx = jnp.arange(n_patches)[:, None] * STRIDE + jnp.arange(PATCH_LEN)[None, :]
        patches = x[:, idx, :]
        patches = patches.transpose(0, 1, 3, 2).reshape(B, n_patches, F * PATCH_LEN)
        y = jnp.einsum('bnk,dk->bnd', patches, W) + b
        mu = jnp.mean(y, axis=-1, keepdims=True)
        var = jnp.mean(jnp.square(y - mu), axis=-1, keepdims=True)
        y = (y - mu) * jax.lax.rsqrt(var + EPS) * gamma + beta
        return y

    def _L0_attn_ref(x, ln_w, ln_b, W_in, conv_w, conv_b, dt_bias, A_log, D, rms_w, W_out):
        import jax, jax.numpy as jnp
        import numpy as np
        D_MODEL = 192
        D_STATE = 64
        D_CONV = 4
        EXPAND = 2
        HEADDIM = 64
        D_INNER = EXPAND * D_MODEL
        NHEADS = D_INNER // HEADDIM
        CONV_DIM = D_INNER + 2 * D_STATE
        D_IN_PROJ = 2 * D_INNER + 2 * D_STATE + NHEADS
        BATCH, SEQLEN = (2, 256)
        EPS = 1e-05

        def _forward(x, ln_w, ln_b, W_in, conv_w, conv_b, dt_bias, A_log, D, rms_w, W_out):
            b, l, _ = x.shape
            mu = jnp.mean(x, -1, keepdims=True)
            var = jnp.mean((x - mu) ** 2, -1, keepdims=True)
            xn = (x - mu) * jax.lax.rsqrt(var + EPS) * ln_w + ln_b
            zxbcdt = xn @ W_in
            z = zxbcdt[..., :D_INNER]
            xBC = zxbcdt[..., D_INNER:D_INNER + CONV_DIM]
            dt_raw = zxbcdt[..., -NHEADS:]
            xp = jnp.pad(xBC, ((0, 0), (D_CONV - 1, 0), (0, 0)))
            xBC = sum((xp[:, k:k + l, :] * conv_w[:, k] for k in range(D_CONV))) + conv_b
            xBC = jax.nn.silu(xBC)
            xh = xBC[..., :D_INNER].reshape(b, l, NHEADS, HEADDIM)
            Bm = xBC[..., D_INNER:D_INNER + D_STATE]
            Cm = xBC[..., D_INNER + D_STATE:]
            dt = jax.nn.softplus(dt_raw + dt_bias)
            A = -jnp.exp(A_log)
            decay = jnp.exp(dt * A)

            def step(h, inp):
                dec_t, dt_t, x_t, B_t, C_t = inp
                h = h * dec_t[..., None, None] + (dt_t[..., None] * x_t)[..., None] * B_t[:, None, None, :]
                y = jnp.einsum('bhpn,bn->bhp', h, C_t)
                return (h, y)
            h0 = jnp.zeros((b, NHEADS, HEADDIM, D_STATE), x.dtype)
            seq = (decay.transpose(1, 0, 2), dt.transpose(1, 0, 2), xh.transpose(1, 0, 2, 3), Bm.transpose(1, 0, 2), Cm.transpose(1, 0, 2))
            _, ys = jax.lax.scan(step, h0, seq)
            y = ys.transpose(1, 0, 2, 3) + D[None, None, :, None] * xh
            y = y.reshape(b, l, D_INNER)
            g = y * jax.nn.silu(z)
            g = g * jax.lax.rsqrt(jnp.mean(g * g, -1, keepdims=True) + EPS) * rms_w
            return g @ W_out + x
        return _forward(x, ln_w, ln_b, W_in, conv_w, conv_b, dt_bias, A_log, D, rms_w, W_out)

    def _L0_ffn_ref(x, Wg, W1, b1, W2, b2):
        import jax, jax.numpy as jnp
        import numpy as np
        B, T, H, F, E = (128, 32, 192, 768, 3)
        scores = jax.nn.softmax(jnp.mean(x, axis=1) @ Wg.T, axis=-1)
        _, idx = jax.lax.top_k(scores, 1)
        sel = idx[:, 0]
        h = jax.nn.gelu(jnp.einsum('bth,ehf->betf', x, W1) + b1[None, :, None, :], approximate=False)
        y = jnp.einsum('betf,efh->beth', h, W2) + b2[None, :, None, :]
        w = scores * jax.nn.one_hot(sel, E, dtype=scores.dtype)
        out = jnp.einsum('beth,be->bth', y, w)
        return out
    h = _L0_tok_ref(x, L0_tok_W, L0_tok_b, L0_tok_gamma, L0_tok_beta)
    h = h + _L0_attn_ref(_layernorm(h, axis=-1), L0_attn_ln_w, L0_attn_ln_b, L0_attn_W_in, L0_attn_conv_w, L0_attn_conv_b, L0_attn_dt_bias, L0_attn_A_log, L0_attn_D, L0_attn_rms_w, L0_attn_W_out)
    h = h + _L0_ffn_ref(_layernorm(h, axis=-1), L0_ffn_Wg, L0_ffn_W1, L0_ffn_b1, L0_ffn_W2, L0_ffn_b2)
    return h

_drawn_inputs = setup_inputs


def setup_inputs(seed=0):
    import zlib

    import numpy as np

    out = dict(_drawn_inputs(seed))
    spreads = {'L0_tok_gamma': (1.0, 0.2),
     'L0_tok_beta': (0.0, 0.1),
     'L0_attn_ln_w': (1.0, 0.2),
     'L0_attn_ln_b': (0.0, 0.329),
     'L0_attn_conv_b': (0.0, 0.1),
     'L0_attn_D': (1.0, 0.6),
     'L0_attn_rms_w': (1.0, 0.2),
     'L0_ffn_b1': (0.0, 0.8),
     'L0_ffn_b2': (0.0, 0.473)}
    factors = {'L0_tok_b': 5.425,
     'L0_attn_dt_bias': 33.25,
     'L0_attn_A_log': 64.0,
     'L0_ffn_Wg': 2.843,
     'L0_ffn_W1': 4.143,
     'L0_ffn_W2': 3.807}
    for name, (base, spread) in spreads.items():
        noise = np.random.default_rng([zlib.crc32(name.encode()), seed]).standard_normal(out[name].shape)
        drawn = base * np.exp(spread * noise) if base else spread * noise
        out[name] = jnp.asarray(drawn.astype(out[name].dtype))
    for name, factor in factors.items():
        out[name] = (out[name] * factor).astype(out[name].dtype)
    return out
```

```python
from contextlib import ExitStack

import concourse.bass as bass
from concourse import mybir

F32 = mybir.dt.float32
F32R = mybir.dt.float32r
I32 = mybir.dt.int32
U32 = mybir.dt.uint32
ALU = mybir.AluOpType
ACT = mybir.ActivationFunctionType
AX = mybir.AxisListType
ds = bass.ds

EPS = 1e-5
LOG_MAX = 88.6
RATE_UNIT = 2.0 ** 64
DECAY_MAX = 1024.0
LOG1P_TERMS = [1 / 17, 1 / 15, 1 / 13, 1 / 11, 1 / 9, 1 / 7, 1 / 5, 1 / 3]


def need(eng, s, n):
    if isinstance(n, int) and n <= 0:
        return
    eng.wait_ge(s, n)


class Steps:

    def __init__(self, eng, s, per, index):
        self.eng, self.s, self.per, self.base, self.n = eng, s, per, index * per, 0

    def did(self, ins):
        self.n += 1
        assert self.n <= self.per
        ins.then_inc(self.s, 1)

    def settle(self):
        self.eng.wait_ge(self.s, self.base + self.n)

    def then(self, ins):
        self.did(ins)
        self.settle()


def audio_tower(nc, x, tok_W, tok_b, tok_gamma, tok_beta, ln_w, ln_b, W_in, conv_w, conv_b, dt_bias,
                A_log, D, rms_w, W_out, Wg, W1, b1, W2, b2, out):
    NSEQ, S, F = x.shape
    DM, KP = tok_W.shape
    PL = KP // F
    ST = PL // 2
    NP = (S - PL) // ST + 1
    BLK = S // ST
    SB = 128 // BLK
    T = SB * NP
    NG = NSEQ // (2 * SB)
    T2 = 2 * T
    DH = DM // 2
    DI = W_out.shape[0]
    NC = DI // 128
    H = D.shape[0]
    HD = DI // H
    NS = (conv_w.shape[0] - DI) // 2
    WI = W_in.shape[1]
    TAPS = conv_w.shape[1]
    NE, _, FF = W1.shape
    FC = FF // 128
    FH = FF // 2
    NTOK = NSEQ * NP
    NT = NSEQ // SB + NE - 1
    SLOTS = NT * SB
    ROW = DM + 2
    MISS = 4096
    CH = NC + 1
    NCH = CH + NC
    assert F == 128 and BLK * SB == 128 and 2 * NS == 128 and H == 2 * NC and HD == 64
    assert MISS > NTOK and NT % 2 == 0 and TAPS == 4

    hid = nc.dram_tensor("hid", (NTOK, ROW), F32, kind="Internal").ap()
    out_rows = out.rearrange("b n d -> (b n) d")

    ctx = ExitStack()
    with ctx:
        def sb(name, shape, dt=F32, stack=ctx):
            return stack.enter_context(nc.sbuf_tensor(name, shape, dt))

        def sem(name):
            return ctx.enter_context(nc.semaphore(name))

        bank = [ctx.enter_context(nc.psum_tensor(f"bank{i}", [128, 512], F32)) for i in range(8)]

        ident = sb("ident", [128, 128])
        same = sb("same", [T, T])
        eye = sb("eye", [T, NP])
        later = sb("later", [T, NP])
        seq_of = sb("seq_of", [T, SB])
        mean_of = sb("mean_of", [T, SB])
        ones = sb("ones", [128, 128])
        idle = sb("idle", [1, 2])
        neg_half = sb("neg_half", [128, 2])
        tokb = sb("tokb", [T, DM])
        gamma = sb("gamma", [T, DM])
        beta = sb("beta", [T, DM])
        dtb = sb("dtb", [T, H])
        alog = sb("alog", [T, H])
        expa = sb("expa", [T, H])
        alogc = sb("alogc", [T, H])
        rate = sb("rate", [T, H])
        lnw = sb("lnw", [DH, 2])
        lnb = sb("lnb", [DH, 2])
        cw = sb("cw", [128, CH, TAPS])
        cb = sb("cb", [128, CH])
        Dc = sb("Dc", [128, NC])
        rmsw = sb("rmsw", [128, NC])
        woraw = sb("woraw", [128, NC, DM])
        WO = sb("WO", [128, NC, DM])
        WT = sb("WT", [128, PL, 2 * DM], F32R)
        WIh = sb("WIh", [DH, 2, WI], F32R)
        WIl = sb("WIl", [DH, 2, WI], F32R)
        W1h = sb("W1h", [DH + 1, NE * 2 * FF], F32R)
        W1l = sb("W1l", [DH + 1, NE * 2 * FF], F32R)
        W2s = sb("W2s", [128, NE * FC, 2 * DM], F32R)
        w1raw = sb("w1raw", [DH, FF])
        w2raw = sb("w2raw", [128, NE, DM])
        WgT = sb("WgT", [DH, 2, NE])
        b2c = sb("b2c", [T, NE * DM])
        skip = sb("skip", [T, 2 * NG, DM])
        means = sb("means", [DH, 2, NSEQ])

        tri = sb("tri", [NSEQ, NSEQ])
        k4 = sb("k4", [NSEQ, NSEQ // SB])
        iota_s = sb("iota_s", [NSEQ, SLOTS])
        iota_t = sb("iota_t", [T, NP])
        rowid = sb("rowid", [NSEQ, T])

        one = ExitStack()
        xraw = sb("xraw", [128, 2, ST * F], stack=one)
        xTh = sb("xTh", [128, 2, ST * 128], F32R, one)
        xTl = sb("xTl", [128, 2, ST * 128], F32R, one)
        raw = ExitStack()
        wtraw = sb("wtraw", [DH, 2, KP], stack=raw)
        wiraw = sb("wiraw", [DH, 2, WI], stack=raw)
        b1raw = sb("b1raw", [DH + 1, NE * FF], stack=raw)
        raw.close()
        emb = sb("emb", [T, 2, DM], stack=one)
        h0 = sb("h0", [T, 2, DM], stack=one)
        xc = sb("xc", [T, 2, DM], stack=one)
        an = sb("an", [T, 2, DM], stack=one)
        st0 = sb("st0", [T, 2, 6], stack=one)
        mv0 = sb("mv0", [T, 2, 2], stack=one)
        st1 = sb("st1", [T, 2, 6], stack=one)
        mv1 = sb("mv1", [T, 2, 2], stack=one)
        rs0 = sb("rs0", [T, 2, 2], stack=one)
        rs1 = sb("rs1", [T, 2, 4], stack=one)
        xnf = sb("xnf", [DH, 2, T2], stack=one)
        xnh = sb("xnh", [DH, 2, T2], F32R, one)
        xnl = sb("xnl", [DH, 2, T2], F32R, one)
        acc = sb("acc", [128, CH, T2], stack=one)
        xs = sb("xs", [128, NC, T2], stack=one)
        zs = sb("zs", [128, NC, T2], stack=one)
        BC = sb("BC", [128, T2], stack=one)
        CT = sb("CT", [NS, T2], stack=one)
        dtv = sb("dtv", [T, 2, H], stack=one)
        dtw = sb("dtw", [T, 9, 2 * H], stack=one)
        dt = sb("dt", [T, 2 * H], stack=one)
        dtA = sb("dtA", [T, 2, H], stack=one)
        dec = sb("dec", [T, 2 * H], stack=one)
        dteye = sb("dteye", [T, 2 * H, NP], stack=one)
        deceye = sb("deceye", [T, 2 * H, NP], stack=one)
        fade = sb("fade", [T, 2 * H, NP], stack=one)
        prod = sb("prod", [T, 2 * H, NP], stack=one)
        score = sb("score", [T, 2, T], stack=one)
        mix = sb("mix", [T, 2, H, T], stack=one)
        xtok = sb("xtok", [T, 2, DI], stack=one)
        gated = sb("gated", [128, NC, T2], stack=one)
        gsq = sb("gsq", [128, NC, T2], stack=one)
        msq = sb("msq", [T, 2], stack=one)
        rrms = sb("rrms", [T, 2], stack=one)
        hrow = sb("hrow", [T, 2, ROW], stack=one)
        st2 = sb("st2", [T, 2, 6], stack=one)
        mv2 = sb("mv2", [T, 2, 2], stack=one)
        var2 = sb("var2", [T, 2], stack=one)
        bn = sb("bn", [T, 2, DM], stack=one)
        one.close()

        rows = sb("rows", [T, 2, ROW])
        resid = sb("resid", [T, NT, DM])
        bb = sb("bb", [T, 2, DM])
        bTh = sb("bTh", [DH + 1, 2, 2 * T], F32R)
        bTl = sb("bTl", [DH + 1, 2, 2 * T], F32R)
        hg = sb("hg", [T, 2, FF])
        hTh = sb("hTh", [128, 2, FC * T], F32R)
        hTl = sb("hTl", [128, 2, FC * T], F32R)
        res = sb("res", [T, 2, DM])
        lgt = sb("lgt", [NSEQ, 4, NE])
        sm = sb("sm", [NSEQ, 8])
        oh = sb("oh", [NSEQ, 6, NE])
        over = sb("over", [NSEQ, NE, NSEQ // SB])
        tpos = sb("tpos", [T, NP])
        tcol = sb("tcol", [T, 2])
        slot = sb("slot", [NSEQ, SLOTS])
        wcol = sb("wcol", [NSEQ, T])
        pick = sb("pick", [T, NT, SB])
        pickw = sb("pickw", [T, NT, SB])
        idf = sb("idf", [T, NT])
        idx = sb("idx", [T, NT], U32)
        wt = sb("wt", [T, NT])
        ef = sb("ef", [NSEQ, 2, NT])
        ei = sb("ei", [NSEQ, NT], I32)
        idg = sb("idg", [T, 2], U32)
        ids = sb("ids", [T, 2], U32)

        bT = (bank[0], bank[1])
        bE = bank[2]
        bX = bank[3]
        bP = (bank[4], bank[5])
        bY = (bank[6], bank[7])
        MEANC = 2 * DM + 16

        c_const = sem("c_const")
        c_wt = sem("c_wt")
        c_wi = sem("c_wi")
        c_b1 = sem("c_b1")
        c_x = [sem("c_x0"), sem("c_x1")]
        c_C = sem("c_C")
        c_w1 = sem("c_w1")
        c_w2 = sem("c_w2")
        c_hid = sem("c_hid")
        p_ident = sem("p_ident")
        p_mask = sem("p_mask")
        p_idle = sem("p_idle")
        p_wi = sem("p_wi")
        v_mask = sem("v_mask")
        a_expa = sem("a_expa")
        t_wt = sem("t_wt")
        a_wt = sem("a_wt")
        v_wt = sem("v_wt")
        v_alog = sem("v_alog")
        v_wo = sem("v_wo")
        t_x = sem("t_x")
        a_xh = sem("a_xh")
        v_xl = sem("v_xl")
        t_emb = sem("t_emb")
        v_emb = sem("v_emb")
        v_ln = sem("v_ln")
        p_ln = sem("p_ln")
        t_xn = sem("t_xn")
        v_xn = sem("v_xn")
        t_dt = sem("t_dt")
        v_dtv = sem("v_dtv")
        t_in = sem("t_in")
        a_cv = sem("a_cv")
        v_cv = sem("v_cv")
        a_si = sem("a_si")
        a_z = sem("a_z")
        a_dt = sem("a_dt")
        v_sp = sem("v_sp")
        p_dt = sem("p_dt")
        t_sd = sem("t_sd")
        a_xt = sem("a_xt")
        v_mix = sem("v_mix")
        p_mix = sem("p_mix")
        t_y = sem("t_y")
        v_gate = sem("v_gate")
        a_sq = sem("a_sq")
        t_out = sem("t_out")
        v_o = sem("v_o")
        p_o = sem("p_o")
        t_mean = sem("t_mean")
        v_mean = sem("v_mean")
        p_w1 = sem("p_w1")
        t_r = sem("t_r")
        v_r = sem("v_r")
        a_r = sem("a_r")
        p_clear = sem("p_clear")
        c_g = [sem("c_g0"), sem("c_g1")]
        c_s = [sem("c_s0"), sem("c_s1")]
        p_id = sem("p_id")
        p_is = sem("p_is")
        v_b = sem("v_b")
        t_b = sem("t_b")
        a_b = sem("a_b")
        v_bl = sem("v_bl")
        t_up = sem("t_up")
        a_gelu = sem("a_gelu")
        t_h = sem("t_h")
        a_hh = sem("a_hh")
        v_hl = sem("v_hl")
        t_dn = sem("t_dn")
        v_fin = sem("v_fin")

        EMB, EMB_READ = 4, 2
        LNP, LNP_READ, LNP_H0, LNP_XC = 11, 3, 5, 9
        SP, SP_DT = 17, 15
        OV, OV_MS = 8, 1
        PO, PO_RR, PO_R = 5, 1, 3
        CONSTS = 18


        eB = bank[0]
        eU = (bank[1], bank[2])
        eH = (bank[3], bank[4])
        eD = (bank[5], bank[6])
        HT = FC // 2 * T
        R_SCORE, R_PICK, R_PLACE = 1, 2, 3
        VR_LOGIT = 3
        VR_CHOICE = VR_LOGIT + 4 + 2 * NE
        VR_PLACE = VR_CHOICE + NE + 7
        VR_TILE = VR_PLACE + NE
        VR_ALL = VR_TILE + 5 + 3

        def stage_one_done(eng):
            eng.wait_ge(c_hid, 32 * NG)
            eng.wait_ge(t_mean, NG)
            eng.wait_ge(v_mean, NG)

        def tiles(eng, at, first):
            for s in range(first, 3):
                at(s, s % 2)
            with eng.Fori(0, (NT - 6) // 2) as m:
                at(2 * m + 3, 1)
                at(2 * m + 4, 0)
            for s in range(NT - 3, NT + 1):
                at(s, s % 2)

        def tile(i):
            return not isinstance(i, int) or 0 <= i < NT

        def left_by(i, per=1):
            return per * (i - 1)

        def turns(i, par):
            return (i - par) // 2

        def stage_two_pool(pool):
            gp = nc.gpsimd
            stage_one_done(pool)
            st = Steps(pool, p_clear, 3, 0)
            st.then(gp.memset(rows[:, :, :], 0.0))
            st.then(gp.memset(bTh[DH:DH + 1, :, T:2 * T].bitcast(F32), 1.0))
            st.then(gp.memset(bTl[DH:DH + 1, :, T:2 * T].bitcast(F32), 0.0))
            pool.wait_ge(v_r, VR_ALL)

            def at(s, par):
                if tile(s + 3):
                    i, p = s + 3, (par + 1) % 2
                    need(pool, v_b, left_by(i, 2))
                    gp.tensor_copy(idg[:, p:p + 1], idx[:, ds(i, 1)]).then_inc(p_id, 1)
                    pool.wait_ge(p_id, i + 1)
                    apart(pool)
                    gp.indirect_dma_start(
                        out=rows[:, p, :], out_offset=None, in_=hid,
                        in_offset=bass.IndirectOffsetOnAxis(ap=idg[:, p:p + 1], axis=0),
                        bounds_check=NTOK - 1, oob_is_err=False).then_inc(c_g[p], 16)
                if tile(s - 1):
                    i, p = s - 1, (par + 1) % 2
                    need(pool, c_s[p], 16 * turns(i, p))
                    gp.tensor_copy(ids[:, p:p + 1], idx[:, ds(i, 1)]).then_inc(p_is, 1)
                    pool.wait_ge(p_is, i + 1)
                    pool.wait_ge(v_fin, 3 * i + 3)
                    apart(pool)
                    gp.indirect_dma_start(
                        out=out_rows, out_offset=bass.IndirectOffsetOnAxis(ap=ids[:, p:p + 1], axis=0),
                        in_=res[:, p, :], in_offset=None,
                        bounds_check=NTOK - 1, oob_is_err=False).then_inc(c_s[p], 16)

            tiles(pool, at, -3)

        def stage_two_act(act):
            ac = nc.scalar
            stage_one_done(act)
            act.wait_ge(v_r, VR_LOGIT)
            ac.activation(lgt[:, 1, :], lgt[:, 0, :], ACT.Exp, bias=sm[:, 1:2], accum_out=sm[:, 2:3])\
              .then_inc(a_r, 1)

            def at(s, par):
                def gelu(f):
                    act.wait_ge(t_up, 2 * s + f + 1)
                    need(act, t_h, left_by(s, 2))
                    ac.activation(hg[:, par, f * FH:(f + 1) * FH], eU[f][0:T, 0:FH], ACT.Gelu)\
                      .then_inc(a_gelu, 1)

                if tile(s + 1):
                    i, p = s + 1, (par + 1) % 2
                    act.wait_ge(t_b, i + 1)
                    need(act, t_up, left_by(i, 2))
                    ac.activation(bTh[0:DH, p, :], eB[0:DH, 0:2 * T], ACT.Copy).then_inc(a_b, 1)
                if tile(s):
                    gelu(0)
                if tile(s - 1):
                    i, p = s - 1, (par + 1) % 2
                    for f in range(2):
                        act.wait_ge(t_h, 2 * i + f + 1)
                        need(act, t_dn, left_by(i))
                        ac.activation(hTh[:, p, f * HT:(f + 1) * HT], eH[f][:, 0:HT], ACT.Copy)\
                          .then_inc(a_hh, 1)
                if tile(s):
                    gelu(1)

            tiles(act, at, -1)

        def stage_two_dve(dve):
            ve = nc.vector
            stage_one_done(dve)
            dve.wait_ge(p_mask, 8)
            st = Steps(dve, v_r, VR_ALL, 0)
            dve.wait_ge(t_r, R_SCORE)
            st.then(ve.tensor_copy(lgt[:, 0, :], bank[3][0:NSEQ, 0:NE]))
            st.then(ve.tensor_reduce(sm[:, 0:1], lgt[:, 0, :], AX.X, ALU.max))
            st.then(ve.tensor_scalar(sm[:, 1:2], sm[:, 0:1], -1.0, None, ALU.mult))
            dve.wait_ge(a_r, 1)
            st.then(ve.reciprocal(sm[:, 3:4], sm[:, 2:3]))
            st.then(ve.tensor_scalar(lgt[:, 2, :], lgt[:, 1, :], sm[:, 3:4], None, ALU.mult))
            st.then(ve.tensor_reduce(sm[:, 4:5], lgt[:, 2, :], AX.X, ALU.max))
            st.then(ve.tensor_scalar(oh[:, 0, :], lgt[:, 2, :], sm[:, 4:5], None, ALU.is_ge))
            left = ones[0:NSEQ, 0:1]
            for e in range(NE):
                st.then(ve.tensor_tensor(oh[:, 1, e:e + 1], oh[:, 0, e:e + 1], left, ALU.mult))
                st.then(ve.tensor_tensor(sm[:, 5:6], left, oh[:, 1, e:e + 1], ALU.subtract))
                left = sm[:, 5:6]
            dve.wait_ge(t_r, R_PICK)
            st.then(ve.tensor_tensor(over[:, :, :],
                                     bank[3][0:NSEQ, 16:16 + NE].unsqueeze(2).broadcast_to((NSEQ, NE, NSEQ // SB)),
                                     k4[:, :].unsqueeze(1).broadcast_to((NSEQ, NE, NSEQ // SB)), ALU.is_gt))
            st.did(ve.tensor_reduce(oh[:, 2, :], over[:, :, :], AX.X, ALU.add))
            st.then(ve.memset(oh[:, 3, 0:1], 0.0))
            for e in range(1, NE):
                st.then(ve.tensor_tensor(oh[:, 3, e:e + 1], oh[:, 3, e - 1:e], oh[:, 2, e - 1:e], ALU.add))
            st.then(ve.scalar_tensor_tensor(oh[:, 4, :], oh[:, 3, :], float(SB), bank[3][0:NSEQ, 8:8 + NE],
                                            ALU.mult, ALU.add))
            st.then(ve.tensor_tensor(oh[:, 5, :], oh[:, 4, :], oh[:, 1, :], ALU.mult))
            st.then(ve.tensor_reduce(sm[:, 6:7], oh[:, 5, :], AX.X, ALU.add))
            st.did(ve.tensor_scalar(slot[:, :], iota_s[:, :], sm[:, 6:7], None, ALU.is_equal))
            st.did(ve.tensor_scalar(wcol[:, :], ones[0:NSEQ, 0:T], sm[:, 4:5], None, ALU.mult))
            assert st.n == VR_PLACE
            st.then(ve.tensor_scalar(ef[:, 0, :], iota_s[:, 0:NT], oh[:, 3, 1:2], None, ALU.is_ge))
            for e in range(2, NE):
                st.then(ve.scalar_tensor_tensor(ef[:, 0, :], iota_s[:, 0:NT], oh[:, 3, e:e + 1], ef[:, 0, :],
                                                ALU.is_ge, ALU.add))
            st.did(ve.tensor_copy(ei[:, :], ef[:, 0, :]))
            assert st.n == VR_TILE
            st.then(ve.tensor_tensor(tpos[:, :], iota_t[:, :], eye[:, :], ALU.mult))
            st.then(ve.tensor_reduce(tcol[:, 0:1], tpos[:, :], AX.X, ALU.add))
            st.did(ve.tensor_scalar(tcol[:, 1:2], tcol[:, 0:1], float(MISS), None, ALU.add))
            dve.wait_ge(t_r, R_PLACE)
            spread = seq_of[:, :].unsqueeze(1).broadcast_to((T, NT, SB))
            st.did(ve.tensor_tensor(pick[:, :, :], bank[4][0:T, 0:SLOTS].rearrange("p (k q) -> p k q", q=SB),
                                    spread, ALU.mult))
            st.then(ve.tensor_tensor(pickw[:, :, :], bank[5][0:T, 0:SLOTS].rearrange("p (k q) -> p k q", q=SB),
                                     spread, ALU.mult))
            st.then(ve.tensor_reduce(idf[:, :], pick[:, :, :], AX.X, ALU.add))
            st.did(ve.tensor_scalar(idx[:, :], idf[:, :], tcol[:, 1:2], None, ALU.add))
            st.then(ve.tensor_reduce(wt[:, :], pickw[:, :, :], AX.X, ALU.add))
            assert st.n == VR_ALL

            def at(s, par):
                if tile(s + 1):
                    i, p = s + 1, (par + 1) % 2
                    dve.wait_ge(a_b, i + 1)
                    need(dve, t_up, left_by(i, 2))
                    ve.tensor_tensor(bTl[0:DH, p, :], eB[0:DH, 0:2 * T], bTh[0:DH, p, :].bitcast(F32),
                                     ALU.subtract).then_inc(v_bl, 1)
                if tile(s + 2):
                    i, p = s + 2, par
                    dve.wait_ge(c_g[p], 16 * (turns(i, p) + 1))
                    need(dve, t_b, left_by(i))
                    ve.tensor_scalar(bb[:, p, :], rows[:, p, 0:DM], rows[:, p, DM:DM + 1],
                                     rows[:, p, DM + 1:DM + 2], ALU.subtract, ALU.mult).then_inc(v_b, 1)
                    ve.tensor_copy(resid[:, ds(i, 1), :], rows[:, p:p + 1, 0:DM]).then_inc(v_b, 1)
                if tile(s - 1):
                    i, p = s - 1, (par + 1) % 2
                    for f in range(2):
                        dve.wait_ge(a_hh, 2 * i + f + 1)
                        need(dve, t_dn, left_by(i))
                        ve.tensor_tensor(hTl[:, p, f * HT:(f + 1) * HT], eH[f][:, 0:HT],
                                         hTh[:, p, f * HT:(f + 1) * HT].bitcast(F32), ALU.subtract)\
                          .then_inc(v_hl, 1)
                    st = Steps(dve, v_fin, 3, i)
                    e = dve.value_load(ei[0:1, ds(i, 1)], min_val=0, max_val=NE - 1)
                    dve.wait_ge(t_dn, i + 1)
                    need(dve, c_s[p], 16 * turns(i, p))
                    st.then(ve.tensor_tensor(res[:, p, :], eD[p][0:T, DM:2 * DM], b2c[:, ds(e * DM, DM)], ALU.add))
                    st.then(ve.tensor_tensor(res[:, p, :], eD[p][0:T, 0:DM], res[:, p, :], ALU.add))
                    st.did(ve.scalar_tensor_tensor(res[:, p:p + 1, :], res[:, p:p + 1, :], wt[:, ds(i, 1)],
                                                   resid[:, ds(i, 1), :], ALU.mult, ALU.add))

            tiles(dve, at, -2)

        def stage_two_pe(pe):
            te = nc.tensor
            stage_one_done(pe)
            pe.wait_ge(p_mask, 8)
            for c in range(2):
                last = te.matmul(bank[3][0:NSEQ, 0:NE], means[:, c, :], WgT[:, c, :], start=(c == 0), stop=(c == 1))
            last.then_inc(t_r, 1)
            pe.wait_ge(v_r, VR_CHOICE)
            te.matmul(bank[3][0:NSEQ, 8:8 + NE], tri[:, :], oh[:, 1, :], start=True, stop=True)
            te.matmul(bank[3][0:NSEQ, 16:16 + NE], ones[0:NSEQ, 0:NSEQ], oh[:, 1, :], start=True, stop=True)\
              .then_inc(t_r, 1)
            pe.wait_ge(v_r, VR_PLACE)
            te.matmul(bank[4][0:T, 0:SLOTS], rowid[:, :], slot[:, :], start=True, stop=True)
            te.matmul(bank[5][0:T, 0:SLOTS], wcol[:, :], slot[:, :], start=True, stop=True).then_inc(t_r, 1)
            pe.wait_ge(v_r, VR_ALL)
            pe.wait_ge(p_clear, 3)
            pe.wait_ge(p_w1, 4 * 2 * NE)

            def at(s, par):
                def up(f, e):
                    need(pe, a_gelu, 2 * (s - 1) + f + 1)
                    n = 0
                    for c in range(2):
                        k = DH + c
                        w = ds(e * (2 * FF) + (c * FF + f * FH), FH)
                        for a, b in ((bTh, W1h), (bTh, W1l), (bTl, W1h)):
                            last = te.matmul(eU[f][0:T, 0:FH], a[0:k, par, c * T:(c + 1) * T], b[0:k, w],
                                             start=(n == 0), stop=(n == 5))
                            n += 1
                    last.then_inc(t_up, 1)

                if tile(s + 1):
                    i, p = s + 1, (par + 1) % 2
                    pe.wait_ge(v_b, 2 * i + 1)
                    need(pe, v_bl, i)
                    for c in range(2):
                        last = te.transpose(eB[0:DH, c * T:(c + 1) * T], bb[:, p, c * DH:(c + 1) * DH],
                                            ident[0:T, 0:T])
                    last.then_inc(t_b, 1)
                if tile(s):
                    e = pe.value_load(ei[0:1, ds(s, 1)], min_val=0, max_val=NE - 1)
                    pe.wait_ge(v_bl, s + 1)
                    up(0, e)
                if tile(s - 1):
                    i, p = s - 1, (par + 1) % 2
                    for f in range(2):
                        pe.wait_ge(a_gelu, 2 * i + f + 1)
                        need(pe, v_hl, 2 * (i - 1) + f + 1)
                        for c in range(FC // 2):
                            last = te.transpose(eH[f][:, c * T:(c + 1) * T],
                                                hg[:, p, f * FH + c * 128:f * FH + (c + 1) * 128], ident[0:T, 0:T])
                        last.then_inc(t_h, 1)
                if tile(s):
                    up(1, e)
                if tile(s - 1):
                    e = pe.value_load(ei[0:1, ds(i, 1)], min_val=0, max_val=NE - 1)
                    pe.wait_ge(v_hl, 2 * i + 2)
                    need(pe, v_fin, 3 * (i - 2) + 2)
                    def rest(c):
                        te.matmul(eD[p][0:T, DM:2 * DM], hTl[:, p, c * T:(c + 1) * T],
                                  W2s[:, ds(e * FC + c, 1), 0:DM].rearrange("p a d -> p (a d)"),
                                  start=False, stop=False, skip_group_check=True)

                    for c in range(FC):
                        if c > 0:
                            rest(c)
                        last = te.matmul(eD[p][0:T, 0:2 * DM], hTh[:, p, c * T:(c + 1) * T],
                                         W2s[:, ds(e * FC + c, 1), :].rearrange("p a d -> p (a d)"),
                                         start=(c == 0), stop=(c == FC - 1), skip_group_check=True)
                        if c == 0:
                            rest(c)
                    last.then_inc(t_dn, 1)

            tiles(pe, at, -1)

        block = ctx.enter_context(nc.Block())

        def bodies(eng, body, first, end, last):
            for g in range(first):
                body(g)
            with eng.Fori(first, end) as g:
                body(g)
            for g in range(end, last + 1):
                body(g)

        def at_index(ap, k):
            return ap[k] if isinstance(k, int) else ap[ds(k, 1)].squeeze(0)

        def apart(eng):
            cell = idle[0:1, 0:1] if eng is nc.vector else idle[0:1, 1:2]
            eng.tensor_tensor(cell, cell, cell, ALU.mult)

        def live(g):
            return not isinstance(g, int) or 0 <= g < NG

        @block.sync
        def _(sp):
            x_t = x.rearrange("(k b) (m r) f -> k m b (r f)", b=SB, r=ST)

            def load_x(k, j):
                need(sp, t_x, 2 * (k - 1))
                sp.dma_start(xraw[:, j, :], at_index(x_t, k)).then_inc(c_x[j], 16)

            sp.dma_start(wtraw[:, :, :], tok_W.rearrange("(c p) k -> p c k", p=DH)).then_inc(c_wt, 16)
            load_x(0, 0)
            load_x(1, 1)
            sp.dma_start(wiraw[:, :, :], W_in.rearrange("(c p) k -> p c k", p=DH)).then_inc(c_wi, 16)
            sp.dma_start(b1raw[DH:DH + 1, :],
                         b1.rearrange("e f -> (e f)").rearrange("(a n) -> a n", a=1)).then_inc(c_b1, 16)
            for dst, src in ((tokb, tok_b), (gamma, tok_gamma), (beta, tok_beta), (dtb, dt_bias),
                             (alog, A_log)):
                sp.dma_start(dst[:, :], src.partition_broadcast(T)).then_inc(c_const, 16)
            sp.dma_start(b2c[:, :], b2.rearrange("e d -> (e d)").partition_broadcast(T)).then_inc(c_const, 16)
            sp.dma_start(woraw[:, :, :], W_out.rearrange("(c p) d -> p c d", p=128)).then_inc(c_const, 16)
            with nc.allow_non_contiguous_dma(reason="small constants by partition"):
                sp.dma_start(lnw[:, :], ln_w.rearrange("(c p) -> p c", p=DH)).then_inc(c_const, 16)
                sp.dma_start(lnb[:, :], ln_b.rearrange("(c p) -> p c", p=DH)).then_inc(c_const, 16)
                sp.dma_start(cw[:, 0, :], conv_w[DI:DI + 128, :]).then_inc(c_const, 16)
                sp.dma_start(cw[:, 1:CH, :], conv_w[0:DI, :].rearrange("(c p) k -> p c k", p=128))\
                  .then_inc(c_const, 16)
                sp.dma_start(cb[:, 0:1], conv_b[DI:DI + 128].rearrange("(p a) -> p a", a=1))\
                  .then_inc(c_const, 16)
                sp.dma_start(cb[:, 1:CH], conv_b[0:DI].rearrange("(c p) -> p c", p=128)).then_inc(c_const, 16)
                sp.dma_start(rmsw[:, :], rms_w.rearrange("(c p) -> p c", p=128)).then_inc(c_const, 16)
                for half in range(2):
                    sp.dma_start(Dc[half * HD:(half + 1) * HD, :],
                                 D.rearrange("(c a) -> a c", a=2)[half, :].partition_broadcast(HD))\
                      .then_inc(c_const, 16)
                for c in range(2):
                    sp.dma_start(WgT[:, c, :], Wg[:, c * DH:(c + 1) * DH].rearrange("e p -> p e"))\
                      .then_inc(c_const, 16)
            sp.dma_start(w1raw[:, :], W1.rearrange("e (c p) f -> (e c) p f", p=DH)[0, :, :]).then_inc(c_w1, 16)
            sp.dma_start(w2raw[:, :, :], W2.rearrange("e (c p) d -> p (e c) d", p=128)[:, 0:NE, :])\
              .then_inc(c_w2, 16)

            w1_t = W1.rearrange("e (c p) f -> (e c) p f", p=DH)
            w2_t = W2.rearrange("e (c p) d -> p (e c) d", p=128)

            hid_t = hid.rearrange("(k b n) r -> k n b r", b=SB, n=NP)

            def body(g):
                if not isinstance(g, int) or g < NG - 1:
                    load_x(2 * g + 2, 0)
                    load_x(2 * g + 3, 1)
                if not isinstance(g, int) or g == 2:
                    sp.wait_ge(p_w1, 4 * (g - 1))
                    sp.dma_start(w1raw[:, :], w1_t[ds(g - 1, 1), :, :].rearrange("a p f -> (a p) f")
                                 if not isinstance(g, int) else w1_t[g - 1, :, :]).then_inc(c_w1, 16)
                    sp.dma_start(w2raw[:, :, :], w2_t[:, ds((g - 1) * NE, NE), :]).then_inc(c_w2, 16)
                if live(g - 1):
                    q = g - 1
                    sp.wait_ge(a_si, CH * q + 1)
                    need(sp, t_sd, 4 * (q - 1) + 1)
                    sp.dma_start(CT[:, :], BC[NS:2 * NS, :]).then_inc(c_C, 16)
                if live(g - 2):
                    u = g - 2
                    sp.wait_ge(v_o, OV * u + OV)
                    sp.wait_ge(p_o, PO * u + PO_R)
                    for j in range(2):
                        sp.dma_start(at_index(hid_t, 2 * u + j), hrow[:, j, :]).then_inc(c_hid, 16)

            bodies(sp, body, 3, NG - 1, NG + 1)
            for p in range(2):
                sp.wait_ge(c_s[p], 16 * (NT // 2))

        @block.gpsimd
        def _(pool):
            gp = nc.gpsimd
            gp.memset(ident[:, :], 0.0).then_inc(p_ident, 1)
            gp.memset(ones[:, :], 1.0).then_inc(p_mask, 1)
            gp.memset(neg_half[:, :], -0.5).then_inc(p_mask, 1)
            gp.memset(idle[:, :], 0.0).then_inc(p_idle, 1)
            pool.wait_ge(p_idle, 1)
            pool.wait_ge(p_ident, 1)
            gp.affine_select(out=ident[:, :], in_=ident[:, :], compare_op=ALU.not_equal, fill=1.0, base=0,
                             pattern=[[-1, 128]], channel_multiplier=1).then_inc(p_ident, 1)
            pool.wait_ge(p_mask, 2)
            gp.affine_select(out=later[:, :], in_=ones[0:T, 0:NP], compare_op=ALU.is_gt, fill=0.0, base=0,
                             pattern=[[SB, NP]], channel_multiplier=-1).then_inc(p_mask, 1)
            gp.affine_select(out=tri[:, :], in_=ones[0:NSEQ, 0:NSEQ], compare_op=ALU.is_gt, fill=0.0, base=0,
                             pattern=[[1, NSEQ]], channel_multiplier=-1).then_inc(p_mask, 1)
            for dst, pattern, base, by_row in ((k4, [[SB, NSEQ // SB]], 0, 0), (iota_s, [[1, SLOTS]], 0, 0),
                                               (iota_t, [[1, NP]], 0, 0), (rowid, [[0, T]], -MISS, NP)):
                gp.iota(dst[:, :], pattern=pattern, base=base, channel_multiplier=by_row,
                        allow_small_or_imprecise_dtypes=True).then_inc(p_mask, 1)
            pool.wait_ge(c_wi, 16)
            st = Steps(pool, p_wi, 4, 0)
            st.then(gp.tensor_copy(WIh[:, :, :], wiraw[:, :, :]))
            st.did(gp.tensor_tensor(WIl[:, :, :], wiraw[:, :, :], WIh[:, :, :].bitcast(F32), ALU.subtract))
            pool.wait_ge(c_b1, 16)
            b1_in = b1raw[DH:DH + 1, :].rearrange("p (e f) -> p e f", f=FF)
            b1_h = W1h[DH:DH + 1, :].rearrange("p (e c f) -> p e c f", c=2, f=FF)[:, :, 1, :]
            b1_l = W1l[DH:DH + 1, :].rearrange("p (e c f) -> p e c f", c=2, f=FF)[:, :, 1, :]
            st.then(gp.tensor_copy(b1_h, b1_in))
            st.then(gp.tensor_tensor(b1_l, b1_in, b1_h.bitcast(F32), ALU.subtract))
            pool.wait_ge(c_const, 16 * CONSTS)
            pool.wait_ge(t_wt, PL // 2)

            def norms_a(k, j):
                st = Steps(pool, p_ln, LNP, k)
                pool.wait_ge(v_emb, EMB * k + EMB)
                apart(pool)
                st.then(gp.tensor_scalar(rs0[:, j, 0:1], mv0[:, j, 1:2], EPS, None, ALU.add))
                st.did(gp.tensor_tensor(rs0[:, j, 1:2], rs0[:, j, 0:1], neg_half[0:T, 0:1], ALU.pow))
                st.settle()
                apart(pool)
                st.then(gp.tensor_scalar(h0[:, j, :], emb[:, j, :], mv0[:, j, 0:1], rs0[:, j, 1:2],
                                         ALU.subtract, ALU.mult))
                st.then(gp.tensor_tensor(h0[:, j, :], h0[:, j, :], gamma[:, :], ALU.mult))
                st.did(gp.tensor_tensor(h0[:, j, :], h0[:, j, :], beta[:, :], ALU.add))

            def norms_b(k, j, g):
                st = Steps(pool, p_ln, LNP, k)
                st.n = LNP_H0
                st.settle()
                pool.wait_ge(v_ln, 2 * k + 2)
                apart(pool)
                st.did(gp.tensor_scalar(rs1[:, j, 0:1], mv1[:, j, 1:2], EPS, None, ALU.add))
                st.then(gp.tensor_scalar(rs1[:, j, 1:2], mv1[:, j, 1:2], 1.0 + EPS, EPS * EPS,
                                         ALU.mult, ALU.add))
                st.did(gp.tensor_tensor(rs1[:, j, 2:4], rs1[:, j, 0:2], neg_half[0:T, :], ALU.pow))
                st.settle()
                need(pool, t_xn, g)
                apart(pool)
                st.did(gp.tensor_scalar(xc[:, j, :], h0[:, j, :], mv1[:, j, 0:1], rs1[:, j, 3:4],
                                        ALU.subtract, ALU.mult))
                st.then(gp.tensor_scalar(an[:, j, :], h0[:, j, :], mv1[:, j, 0:1], rs1[:, j, 2:3],
                                         ALU.subtract, ALU.mult))
                st.did(gp.tensor_tensor(skip[:, ds(k, 1), :], h0[:, j:j + 1, :], an[:, j:j + 1, :], ALU.add))

            def split_experts(i):
                st = Steps(pool, p_w1, 4, i)
                pool.wait_ge(c_w1, 16 * (i + 1))
                pool.wait_ge(c_w2, 16 * (i + 1))
                st.did(gp.tensor_copy(W1h[0:DH, ds(i * FF, FF)], w1raw[:, :]))
                st.then(gp.tensor_copy(W2s[:, ds(i * NE, NE), 0:DM], w2raw[:, :, :]))
                st.did(gp.tensor_tensor(W1l[0:DH, ds(i * FF, FF)], w1raw[:, :],
                                        W1h[0:DH, ds(i * FF, FF)].bitcast(F32), ALU.subtract))
                st.then(gp.tensor_tensor(W2s[:, ds(i * NE, NE), DM:2 * DM], w2raw[:, :, :],
                                         W2s[:, ds(i * NE, NE), 0:DM].bitcast(F32), ALU.subtract))

            def body(g):
                if live(g - 2):
                    u = g - 2
                    pool.wait_ge(v_mix, 4 * u + 3)
                    need(pool, t_y, 2 * u)
                    gp.tensor_tensor(
                        mix[:, 1, :, :].rearrange("p h (n q) -> p h n q", q=SB),
                        score[:, 1, :].rearrange("p (n q) -> p n q", q=SB).unsqueeze(1)
                        .broadcast_to((T, H, NP, SB)),
                        prod[:, H:2 * H, :].unsqueeze(3).broadcast_to((T, H, NP, SB)),
                        ALU.mult).then_inc(p_mix, 1)
                if live(g):
                    norms_a(2 * g, 0)
                if not isinstance(g, int) or 2 <= g <= 7:
                    split_experts(g - 2)
                if live(g):
                    norms_b(2 * g, 0, g)
                if live(g - 1):
                    q = g - 1
                    st = Steps(pool, p_dt, 2, q)
                    pool.wait_ge(v_sp, SP * q + SP_DT)
                    need(pool, v_mix, 4 * (q - 1) + 3)
                    st.did(gp.tensor_tensor(dteye[:, :, :],
                                            eye[:, :].unsqueeze(1).broadcast_to((T, 2 * H, NP)),
                                            dt[:, :].unsqueeze(2).broadcast_to((T, 2 * H, NP)), ALU.mult))
                    pool.wait_ge(a_dt, 3 * q + 3)
                    need(pool, t_sd, 4 * (q - 1) + 2)
                    st.did(gp.tensor_tensor(deceye[:, :, :],
                                            eye[:, :].unsqueeze(1).broadcast_to((T, 2 * H, NP)),
                                            dec[:, :].unsqueeze(2).broadcast_to((T, 2 * H, NP)), ALU.mult))
                if live(g):
                    norms_a(2 * g + 1, 1)
                if live(g - 2):
                    st = Steps(pool, p_o, PO, g - 2)
                    pool.wait_ge(v_o, OV * (g - 2) + OV_MS)
                    st.did(gp.tensor_tensor(rrms[:, :], msq[:, :], neg_half[0:T, :], ALU.pow))
                if live(g):
                    norms_b(2 * g + 1, 1, g)
                if live(g - 2):
                    u = g - 2
                    pool.wait_ge(v_o, OV * u + OV)
                    apart(pool)
                    st = Steps(pool, p_o, PO, u)
                    st.n = PO_RR
                    st.then(gp.tensor_scalar(var2[:, :], mv2[:, :, 1], EPS, None, ALU.add))
                    st.did(gp.tensor_tensor(hrow[:, :, DM + 1], var2[:, :], neg_half[0:T, :], ALU.pow))
                    st.settle()
                    need(pool, t_mean, u)
                    apart(pool)
                    for j in range(2):
                        st.did(gp.tensor_scalar(bn[:, j, :], hrow[:, j, 0:DM], hrow[:, j, DM:DM + 1],
                                                hrow[:, j, DM + 1:DM + 2], ALU.subtract, ALU.mult))

            bodies(pool, body, 3, NG, NG + 1)
            stage_two_pool(pool)

        @block.scalar
        def _(act):
            ac = nc.scalar
            for r in range(PL // 2):
                act.wait_ge(t_wt, r + 1)
                ac.activation(WT[:, 2 * r:2 * r + 2, 0:DM],
                              bank[2 + r % 4][:, 0:2 * DM].rearrange("p (t d) -> p t d", t=2),
                              ACT.Copy).then_inc(a_wt, 1)
            act.wait_ge(c_const, 16 * CONSTS)
            act.wait_ge(v_alog, 1)
            ac.activation(expa[:, :], alogc[:, :], ACT.Exp).then_inc(a_expa, 1)
            act.wait_ge(p_wi, 4)
            act.wait_ge(t_wt, PL // 2)

            def high(k, j):
                for h in range(2):
                    act.wait_ge(t_x, 2 * k + h + 1)
                    need(act, t_emb, k - 1)
                    ac.activation(xTh[:, j, h * 512:(h + 1) * 512], bT[h][:, :], ACT.Copy).then_inc(a_xh, 1)

            def body(g):
                if live(g):
                    high(2 * g, 0)
                if live(g - 2):
                    u = g - 2
                    for j, b in enumerate((bP[1], bY[0])):
                        act.wait_ge(t_sd, 4 * u + 3 + j)
                        need(act, t_y, 2 * u)
                        ac.activation(xtok[:, j, :], b[0:T, 0:DI], ACT.Copy).then_inc(a_xt, 1)
                if live(g):
                    high(2 * g + 1, 1)
                if live(g - 1):
                    q = g - 1

                    def start(i):
                        act.wait_ge(t_in, NCH * q + i + 1)
                        need(act, a_si, CH * (q - 1) + i + 1)
                        ac.activation(acc[:, i, :], bP[i % 2][:, 0:T2], ACT.Identity, bias=cb[:, i:i + 1],
                                      scale=cw[:, i, TAPS - 1:TAPS]).then_inc(a_cv, 1)

                    def silu(i):
                        act.wait_ge(v_cv, 3 * CH * q + 3 * (i + 1))
                        if i == 0:
                            need(act, t_sd, 4 * (q - 1) + 1)
                            need(act, c_C, 16 * q)
                        else:
                            need(act, t_sd, 4 * q)
                            need(act, v_gate, 4 * (q - 1) + 3)
                        ac.activation(BC[:, :] if i == 0 else xs[:, i - 1, :], acc[:, i, :], ACT.Silu)\
                          .then_inc(a_si, 1)

                    def gate(i):
                        act.wait_ge(t_in, NCH * q + CH + i + 1)
                        need(act, v_gate, 4 * q)
                        ac.activation(zs[:, i, :], bP[(CH + i) % 2][:, 0:T2], ACT.Silu).then_inc(a_z, 1)

                    start(0)
                    start(1)
                    silu(0)
                    start(2)
                    silu(1)
                    start(3)
                    silu(2)
                    gate(0)
                    silu(3)
                    gate(1)
                    gate(2)
                if live(g - 2):
                    u = g - 2
                    act.wait_ge(v_gate, 4 * u + 4)
                    need(act, t_out, u)
                    ac.activation(gsq[:, :, :], gated[:, :, :], ACT.Square).then_inc(a_sq, 1)
                if live(g - 1):
                    q = g - 1
                    act.wait_ge(v_dtv, q + 1)
                    need(act, v_sp, SP * q)
                    ac.activation(dtw[:, 0, :], dtv[:, :, :].rearrange("p u h -> p (u h)"), ACT.Abs)\
                      .then_inc(a_dt, 1)
                    act.wait_ge(a_dt, 3 * q + 1)
                    ac.activation(dtw[:, 1, :], dtw[:, 0, :], ACT.Exp, scale=-1.0).then_inc(a_dt, 1)
                    act.wait_ge(v_sp, SP * q + SP)
                    need(act, p_dt, 2 * q)
                    ac.activation(dec[:, :], dtA[:, :, :].rearrange("p u h -> p (u h)"), ACT.Exp,
                                  scale=-RATE_UNIT).then_inc(a_dt, 1)

            bodies(act, body, 3, NG, NG + 1)
            stage_two_act(act)

        @block.vector
        def _(dve):
            ve = nc.vector
            dve.wait_ge(p_ident, 2)
            ve.tensor_reduce(eye[:, :], ident[0:T, 0:T].rearrange("p (n q) -> p n q", q=SB), AX.X, ALU.add)\
              .then_inc(v_mask, 1)
            ve.tensor_reduce(seq_of[:, :], ident[0:T, 0:T].rearrange("p (n q) -> p q n", q=SB), AX.X, ALU.add)\
              .then_inc(v_mask, 1)
            dve.wait_ge(v_mask, 2)
            ve.tensor_copy(same[:, :].rearrange("p (n q) -> p n q", q=SB),
                           seq_of[:, :].unsqueeze(1).broadcast_to((T, NP, SB))).then_inc(v_mask, 1)
            ve.tensor_scalar(mean_of[:, :], seq_of[:, :], 1.0 / NP, None, ALU.mult).then_inc(v_mask, 1)
            dve.wait_ge(v_mask, 4)
            dve.wait_ge(p_idle, 1)
            dve.wait_ge(p_mask, 3)
            for r in range(PL // 2):
                dve.wait_ge(a_wt, r + 1)
                ve.tensor_tensor(WT[:, 2 * r:2 * r + 2, DM:2 * DM],
                                 bank[2 + r % 4][:, 0:2 * DM].rearrange("p (t d) -> p t d", t=2),
                                 WT[:, 2 * r:2 * r + 2, 0:DM].bitcast(F32), ALU.subtract).then_inc(v_wt, 1)
            dve.wait_ge(c_const, 16 * CONSTS)
            ve.tensor_scalar(alogc[:, :], alog[:, :], LOG_MAX, None, ALU.min).then_inc(v_alog, 1)
            dve.wait_ge(a_expa, 1)
            ve.tensor_scalar(rate[:, :], expa[:, :], 1.0 / RATE_UNIT, None, ALU.mult).then_inc(v_wo, 1)
            for c in range(NC):
                ve.tensor_scalar(WO[:, c, :], woraw[:, c, :], rmsw[:, c:c + 1], None, ALU.mult)\
                  .then_inc(v_wo, 1)
            dve.wait_ge(v_wo, NC + 1)
            dve.wait_ge(p_wi, 4)
            dve.wait_ge(t_wt, PL // 2)

            def low(k, j):
                for h in range(2):
                    dve.wait_ge(a_xh, 2 * k + h + 1)
                    need(dve, t_emb, k - 1)
                    ve.tensor_tensor(xTl[:, j, h * 512:(h + 1) * 512], bT[h][:, :],
                                     xTh[:, j, h * 512:(h + 1) * 512].bitcast(F32), ALU.subtract)\
                      .then_inc(v_xl, 1)

            def embed_a(k, j):
                st = Steps(dve, v_emb, EMB, k)
                dve.wait_ge(t_emb, k + 1)
                need(dve, p_ln, LNP * (k - 2) + LNP_READ)
                st.then(ve.tensor_tensor(emb[:, j, :], bE[0:T, DM:2 * DM], tokb[:, :], ALU.add))
                st.then(ve.tensor_tensor(emb[:, j, :], bE[0:T, 0:DM], emb[:, j, :], ALU.add))
                st.did(ve.bn_stats(st0[:, j, :], emb[:, j, :]))
                st.settle()
                apart(dve)
                st.did(ve.bn_aggr(mv0[:, j, :], st0[:, j, :]))

            def embed_b(k, j):
                st = Steps(dve, v_ln, 2, k)
                dve.wait_ge(p_ln, LNP * k + LNP_H0)
                st.did(ve.bn_stats(st1[:, j, :], h0[:, j, :]))
                st.settle()
                apart(dve)
                st.did(ve.bn_aggr(mv1[:, j, :], st1[:, j, :]))

            def mixing(u):
                st = Steps(dve, v_mix, 4, u)
                dve.wait_ge(t_sd, 4 * u + 1)
                need(dve, p_mix, u)
                st.did(ve.tensor_tensor(score[:, :, :], bX[0:T, 0:T2].rearrange("p (u t) -> p u t", u=2),
                                        same[:, :].unsqueeze(1).broadcast_to((T, 2, T)), ALU.mult))
                dve.wait_ge(t_sd, 4 * u + 2)
                st.then(ve.tensor_tensor(fade[:, :, :],
                                         bY[1][0:T, 0:2 * H * NP].rearrange("p (a t) -> p a t", t=NP),
                                         later[:, :].unsqueeze(1).broadcast_to((T, 2 * H, NP)), ALU.mult))
                dve.wait_ge(p_dt, 2 * u + 1)
                st.then(ve.tensor_tensor_scan(prod[:, :, :].rearrange("p a t -> p (a t)"),
                                              fade[:, :, :].rearrange("p a t -> p (a t)"),
                                              dteye[:, :, :].rearrange("p a t -> p (a t)"), 0.0,
                                              ALU.mult, ALU.add))
                need(dve, t_y, 2 * u)
                st.did(ve.tensor_tensor(
                    mix[:, 0, :, :].rearrange("p h (n q) -> p h n q", q=SB),
                    score[:, 0, :].rearrange("p (n q) -> p n q", q=SB).unsqueeze(1)
                    .broadcast_to((T, H, NP, SB)),
                    prod[:, 0:H, :].unsqueeze(3).broadcast_to((T, H, NP, SB)), ALU.mult))

            def norm_x(q):
                st = Steps(dve, v_xn, 4, q)
                dve.wait_ge(t_xn, q + 1)
                for c in range(2):
                    st.did(ve.tensor_scalar(xnf[:, c, :], bX[0:DH, c * T2:(c + 1) * T2], lnw[:, c:c + 1],
                                            lnb[:, c:c + 1], ALU.mult, ALU.add))
                st.settle()
                need(dve, t_in, NCH * q)
                st.then(ve.tensor_copy(xnh[:, :, :], xnf[:, :, :]))
                st.did(ve.tensor_tensor(xnl[:, :, :], xnf[:, :, :], xnh[:, :, :].bitcast(F32), ALU.subtract))

            def average(u):
                dve.wait_ge(t_mean, u + 1)
                ve.tensor_copy(means[:, :, ds(2 * SB * u, 2 * SB)],
                               bP[0][0:DH, MEANC:MEANC + 4 * SB].rearrange("p (c s) -> p c s", c=2))\
                  .then_inc(v_mean, 1)

            def gating(u):
                st = Steps(dve, v_gate, 4, u)
                need(dve, t_out, u)
                need(dve, a_sq, u)
                for c in range(NC):
                    dve.wait_ge(t_y, 2 * u + (1 if c < 2 else 2))
                    y = bY[0][:, c * T2:(c + 1) * T2] if c < 2 else bY[1][:, 0:T2]
                    st.did(ve.scalar_tensor_tensor(gated[:, c, :], xs[:, c, :], Dc[:, c:c + 1], y,
                                                   ALU.mult, ALU.add))
                st.settle()
                dve.wait_ge(a_z, NC * u + NC)
                st.did(ve.tensor_tensor(gated[:, :, :], gated[:, :, :], zs[:, :, :], ALU.mult))

            def step_sizes(q):
                dve.wait_ge(t_dt, q + 1)
                need(dve, a_dt, 3 * q)
                need(dve, v_sp, SP * q)
                ve.tensor_tensor(dtv[:, :, :], bX[0:T, 2 * T2:2 * T2 + 2 * H].rearrange("p (u h) -> p u h", h=H),
                                 dtb[:, :].unsqueeze(1).broadcast_to((T, 2, H)), ALU.add).then_inc(v_dtv, 1)

            def convolve(q):
                st = Steps(dve, v_cv, 3 * CH, q)
                for i in range(CH):
                    dve.wait_ge(a_cv, CH * q + i + 1)
                    a = acc[:, i, :].rearrange("p (j t) -> p j t", t=T)
                    p = bP[i % 2][:, 0:T2].rearrange("p (j t) -> p j t", t=T)
                    for back in (1, 2, 3):
                        st.then(ve.scalar_tensor_tensor(
                            a[:, :, back * SB:T], p[:, :, 0:T - back * SB], cw[:, i, TAPS - 1 - back:TAPS - back],
                            a[:, :, back * SB:T], ALU.mult, ALU.add))

            def softplus(q):
                st = Steps(dve, v_sp, SP, q)
                u, w, rc, s, s2, p, lp, rl = (dtw[:, i, :] for i in range(1, 9))
                dve.wait_ge(a_dt, 3 * q + 2)
                st.then(ve.tensor_scalar(w, u, 2.0, None, ALU.add))
                st.then(ve.reciprocal(rc, w))
                st.then(ve.tensor_tensor(s, u, rc, ALU.mult))
                st.then(ve.tensor_tensor(s2, s, s, ALU.mult))
                st.then(ve.tensor_scalar(p, s2, LOG1P_TERMS[0], None, ALU.mult))
                for c in LOG1P_TERMS[1:]:
                    st.then(ve.scalar_tensor_tensor(p, p, c, s2, ALU.add, ALU.mult))
                st.did(ve.scalar_tensor_tensor(lp, p, 1.0, s, ALU.add, ALU.mult))
                st.then(ve.tensor_scalar(rl, dtv[:, :, :].rearrange("p u h -> p (u h)"), 0.0, None, ALU.max))
                need(dve, p_dt, 2 * (q - 1) + 1)
                st.then(ve.scalar_tensor_tensor(dt[:, :], lp, 2.0, rl, ALU.mult, ALU.add))
                st.then(ve.tensor_tensor(dtA[:, :, :], dt[:, :].rearrange("p (u h) -> p u h", u=2),
                                         rate[:, :].unsqueeze(1).broadcast_to((T, 2, H)), ALU.mult))
                st.did(ve.tensor_scalar(dtA[:, :, :], dtA[:, :, :], DECAY_MAX / RATE_UNIT, None, ALU.min))

            def body(g):
                if live(g):
                    low(2 * g, 0)
                if live(g - 2):
                    mixing(g - 2)
                if live(g):
                    low(2 * g + 1, 1)
                if live(g - 1):
                    norm_x(g - 1)
                if live(g - 3):
                    average(g - 3)
                if live(g):
                    embed_a(2 * g, 0)
                if live(g - 2):
                    gating(g - 2)
                if live(g):
                    embed_b(2 * g, 0)
                if live(g - 1):
                    step_sizes(g - 1)
                    convolve(g - 1)
                    softplus(g - 1)
                if live(g):
                    embed_a(2 * g + 1, 1)
                if live(g - 2):
                    u = g - 2
                    st = Steps(dve, v_o, OV, u)
                    dve.wait_ge(t_out, u + 1)
                    need(dve, p_o, PO * (u - 1) + PO)
                    st.did(ve.tensor_scalar(msq[:, :], bP[0][0:T, 2 * DM:2 * DM + 2], 1.0 / DI, EPS,
                                            ALU.mult, ALU.add))
                if live(g):
                    embed_b(2 * g + 1, 1)
                if live(g - 2):
                    dve.wait_ge(p_o, PO * u + PO_RR)
                    dve.wait_ge(p_ln, LNP * (2 * u + 2))
                    need(dve, c_hid, 32 * u)
                    for j in range(2):
                        st.did(ve.scalar_tensor_tensor(
                            hrow[:, j:j + 1, 0:DM],
                            bP[0][0:T, j * DM:(j + 1) * DM].rearrange("p (a d) -> p a d", a=1),
                            rrms[:, j:j + 1], skip[:, ds(2 * u + j, 1), :], ALU.mult, ALU.add))
                    st.settle()
                    for j in range(2):
                        st.did(ve.bn_stats(st2[:, j, :], hrow[:, j, 0:DM]))
                    st.settle()
                    apart(dve)
                    for j in range(2):
                        st.did(ve.bn_aggr(mv2[:, j, :], st2[:, j, :]))
                    st.settle()
                    st.did(ve.tensor_copy(hrow[:, :, DM], mv2[:, :, 0]))

            bodies(dve, body, 3, NG, NG + 2)
            stage_two_dve(dve)

        @block.tensor
        def _(pe):
            te = nc.tensor
            pe.wait_ge(p_ident, 2)
            pe.wait_ge(c_wt, 16)
            for r in range(PL // 2):
                need(pe, v_wt, r - 3)
                for t in range(2):
                    for c in range(2):
                        last = te.transpose(bank[2 + r % 4][:, (2 * t + c) * DH:(2 * t + c + 1) * DH],
                                            wtraw[:, c, :].rearrange("p (f t) -> p t f", t=PL)[:, 2 * r + t, :],
                                            ident[0:DH, 0:DH])
                last.then_inc(t_wt, 1)

            def turn_x(k, j, g):
                pe.wait_ge(c_x[j], 16 * (g + 1))
                for h in range(2):
                    need(pe, v_xl, 2 * (k - 1) + h + 1)
                    for r in range(4):
                        last = te.transpose(bT[h][:, r * 128:(r + 1) * 128],
                                            xraw[:, j, (4 * h + r) * F:(4 * h + r + 1) * F], ident[:, :])
                    last.then_inc(t_x, 1)

            def embed(k, j):
                if isinstance(k, int) and k == 0:
                    pe.wait_ge(v_wt, PL // 2)
                pe.wait_ge(v_xl, 2 * k + 2)
                need(pe, v_emb, EMB * (k - 1) + EMB_READ)
                hi = xTh[:, j, :].rearrange("p (r s) -> p r s", s=128)
                lo = xTl[:, j, :].rearrange("p (r s) -> p r s", s=128)
                for t in range(PL):
                    w = slice(t // ST * SB, t // ST * SB + T)
                    if t > 0:
                        te.matmul(bE[0:T, DM:2 * DM], lo[:, t % ST, w], WT[:, t, 0:DM],
                                  start=False, stop=False, skip_group_check=True)
                    last = te.matmul(bE[0:T, 0:2 * DM], hi[:, t % ST, w], WT[:, t, :],
                                     start=(t == 0), stop=(t == PL - 1), skip_group_check=True)
                    if t == 0:
                        te.matmul(bE[0:T, DM:2 * DM], lo[:, t % ST, w], WT[:, t, 0:DM],
                                  start=False, stop=False, skip_group_check=True)
                last.then_inc(t_emb, 1)

            def turn_norms(q):
                pe.wait_ge(p_ln, LNP * (2 * q + 1) + LNP_XC)
                need(pe, v_mix, 4 * (q - 1) + 1)
                need(pe, v_dtv, q)
                for j in range(2):
                    for c in range(2):
                        last = te.transpose(bX[0:DH, c * T2 + j * T:c * T2 + (j + 1) * T],
                                            xc[:, j, c * DH:(c + 1) * DH], ident[0:T, 0:T])
                last.then_inc(t_xn, 1)

            def project(q):
                if isinstance(q, int) and q == 0:
                    pe.wait_ge(p_wi, 2)
                pe.wait_ge(v_xn, 4 * q + 4)
                for j in range(2):
                    n = 0
                    for c in range(2):
                        for a, w in ((xnh, WIh), (xnh, WIl), (xnl, WIh)):
                            last = te.matmul(bX[0:T, 2 * T2 + j * H:2 * T2 + (j + 1) * H],
                                             a[:, c, j * T:(j + 1) * T], w[:, c, WI - H:WI],
                                             start=(n == 0), stop=(n == 5), skip_group_check=True)
                            n += 1
                last.then_inc(t_dt, 1)
                cols = [2 * DI] + [DI + 128 * i for i in range(NC)] + [128 * i for i in range(NC)]
                for i, col in enumerate(cols):
                    if i == 0:
                        need(pe, v_mean, q - 1)
                        need(pe, v_o, OV * (q - 1))
                    elif i == 1:
                        need(pe, a_xt, 2 * (q - 1) + 1)
                    elif i < CH + 2:
                        pe.wait_ge(v_cv, 3 * CH * q + 3 * (i - 1))
                    else:
                        pe.wait_ge(a_z, NC * q + i - CH - 1)
                    n = 0
                    for c in range(2):
                        for w, a in ((WIh, xnh), (WIh, xnl), (WIl, xnh)):
                            last = te.matmul(bP[i % 2][:, 0:T2], w[:, c, col:col + 128], a[:, c, :],
                                             start=(n == 0), stop=(n == 5))
                            n += 1
                    last.then_inc(t_in, 1)

            def prepare(u):
                pe.wait_ge(c_C, 16 * (u + 1))
                pe.wait_ge(v_dtv, u + 1)
                for j in range(2):
                    last = te.matmul(bX[0:T, j * T:(j + 1) * T], BC[0:NS, j * T:(j + 1) * T],
                                     CT[:, j * T:(j + 1) * T], start=True, stop=True)
                last.then_inc(t_sd, 1)
                if isinstance(u, int) and u == 0:
                    pe.wait_ge(v_mask, 4)
                pe.wait_ge(p_dt, 2 * u + 2)
                need(pe, v_gate, 4 * (u - 1) + 3)
                te.matmul(bY[1][0:T, 0:2 * H * NP], same[:, :],
                          deceye[:, :, :].rearrange("p a t -> p (a t)"), start=True, stop=True)\
                  .then_inc(t_sd, 1)
                pe.wait_ge(a_si, CH * u + CH)
                pe.wait_ge(a_z, NC * u + 2)
                for j, b in enumerate((bP[1], bY[0])):
                    for c in range(NC):
                        last = te.transpose(b[0:T, c * 128:(c + 1) * 128], xs[:, c, j * T:(j + 1) * T],
                                            ident[:, :])
                    last.then_inc(t_sd, 1)

            def blend(u):
                pe.wait_ge(v_mix, 4 * u + 4)
                pe.wait_ge(p_mix, u + 1)
                pe.wait_ge(a_xt, 2 * u + 2)
                for c in range(NC):
                    y = bY[0][:, c * T2:(c + 1) * T2] if c < 2 else bY[1][:, 0:T2]
                    for j in range(2):
                        for half in range(2):
                            h = 2 * c + half
                            last = te.matmul(y[half * HD:(half + 1) * HD, j * T:(j + 1) * T],
                                             xtok[:, j, h * HD:(h + 1) * HD], mix[:, j, h, :],
                                             start=True, stop=True)
                    if c > 0:
                        last.then_inc(t_y, 1)

            def average(u):
                if isinstance(u, int) and u == 0:
                    pe.wait_ge(v_mask, 4)
                pe.wait_ge(p_o, PO * u + PO)
                for j in range(2):
                    for c in range(2):
                        col = MEANC + c * 2 * SB + j * SB
                        last = te.matmul(bP[0][0:DH, col:col + SB], bn[:, j, c * DH:(c + 1) * DH],
                                         mean_of[:, :], start=True, stop=True)
                last.then_inc(t_mean, 1)

            def emit(u, g):
                if isinstance(u, int) and u == 0:
                    pe.wait_ge(v_wo, NC + 1)
                pe.wait_ge(a_z, NC * (min(g, NG) if isinstance(g, int) else g))
                pe.wait_ge(a_sq, u + 1)
                for j in range(2):
                    for c in range(NC):
                        te.matmul(bP[0][0:T, j * DM:(j + 1) * DM], gated[:, c, j * T:(j + 1) * T], WO[:, c, :],
                                  start=(c == 0), stop=(c == NC - 1))
                for j in range(2):
                    for c in range(NC):
                        last = te.matmul(bP[0][0:T, 2 * DM + j:2 * DM + j + 1], gsq[:, c, j * T:(j + 1) * T],
                                         ones[:, 0:1], start=(c == 0), stop=(c == NC - 1))
                last.then_inc(t_out, 1)

            def body(g):
                if live(g):
                    turn_x(2 * g, 0, g)
                if live(g - 2):
                    prepare(g - 2)
                if live(g):
                    embed(2 * g, 0)
                    turn_x(2 * g + 1, 1, g)
                if live(g - 1):
                    turn_norms(g - 1)
                if live(g - 3):
                    average(g - 3)
                if live(g - 2):
                    blend(g - 2)
                if live(g - 1):
                    project(g - 1)
                if live(g):
                    embed(2 * g + 1, 1)
                if live(g - 2):
                    emit(g - 2, g)

            bodies(pe, body, 3, NG, NG + 2)
            stage_two_pe(pe)


_INS = ['x', 'L0_tok_W', 'L0_tok_b', 'L0_tok_gamma', 'L0_tok_beta', 'L0_attn_ln_w', 'L0_attn_ln_b',
        'L0_attn_W_in', 'L0_attn_conv_w', 'L0_attn_conv_b', 'L0_attn_dt_bias', 'L0_attn_A_log', 'L0_attn_D',
        'L0_attn_rms_w', 'L0_attn_W_out', 'L0_ffn_Wg', 'L0_ffn_W1', 'L0_ffn_b1', 'L0_ffn_W2', 'L0_ffn_b2']


def kernel(**inputs):
    import numpy as _np
    import concourse.bacc as _bacc
    from concourse import mybir as _mybir
    from concourse.bass_utils import run_bass_kernel_spmd as _run

    nc = _bacc.Bacc("TRN2", target_bir_lowering=False, num_devices=1)
    arrays, args = {}, []
    for name in _INS:
        a = _np.ascontiguousarray(inputs[name])
        arrays[f"in_{name}"] = a
        args.append(nc.dram_tensor(f"in_{name}", a.shape, _mybir.dt.from_np(a.dtype), kind="ExternalInput").ap())
    nseq, samples, _ = inputs['x'].shape
    width = inputs['L0_tok_W'].shape[0]
    shape = (nseq, (samples - 16) // 8 + 1, width)
    args.append(nc.dram_tensor("out_0", shape, _mybir.dt.float32, kind="ExternalOutput").ap())
    audio_tower(nc, *args)
    r = _run(nc, [arrays], core_ids=[0])
    return r.results[0]["out_0"]
```

```python
from contextlib import ExitStack

import concourse.bass as bass
from concourse import mybir

F32 = mybir.dt.float32
F32R = mybir.dt.float32r
I32 = mybir.dt.int32
U32 = mybir.dt.uint32
ALU = mybir.AluOpType
ACT = mybir.ActivationFunctionType
AX = mybir.AxisListType
ds = bass.ds

EPS = 1e-5
LOG_MAX = 88.6
RATE_UNIT = 2.0 ** 64
DECAY_MAX = 1024.0
LOG1P_TERMS = [1 / 17, 1 / 15, 1 / 13, 1 / 11, 1 / 9, 1 / 7, 1 / 5, 1 / 3]


def need(eng, s, n):
    if isinstance(n, int) and n <= 0:
        return
    eng.wait_ge(s, n)


class Steps:

    def __init__(self, eng, s, per, index):
        self.eng, self.s, self.per, self.base, self.n = eng, s, per, index * per, 0

    def did(self, ins):
        self.n += 1
        assert self.n <= self.per
        ins.then_inc(self.s, 1)

    def settle(self):
        self.eng.wait_ge(self.s, self.base + self.n)

    def then(self, ins):
        self.did(ins)
        self.settle()


def audio_tower(nc, x, tok_W, tok_b, tok_gamma, tok_beta, ln_w, ln_b, W_in, conv_w, conv_b, dt_bias,
                A_log, D, rms_w, W_out, Wg, W1, b1, W2, b2, out):
    NSEQ, S, F = x.shape
    DM, KP = tok_W.shape
    PL = KP // F
    ST = PL // 2
    NP = (S - PL) // ST + 1
    BLK = S // ST
    SB = 128 // BLK
    T = SB * NP
    NG = NSEQ // (2 * SB)
    T2 = 2 * T
    DH = DM // 2
    DI = W_out.shape[0]
    NC = DI // 128
    H = D.shape[0]
    HD = DI // H
    NS = (conv_w.shape[0] - DI) // 2
    WI = W_in.shape[1]
    TAPS = conv_w.shape[1]
    NE, _, FF = W1.shape
    FC = FF // 128
    FH = FF // 2
    NTOK = NSEQ * NP
    NT = NSEQ // SB + NE - 1
    SLOTS = NT * SB
    ROW = DM + 2
    MISS = 4096
    CH = NC + 1
    NCH = CH + NC
    assert F == 128 and BLK * SB == 128 and 2 * NS == 128 and H == 2 * NC and HD == 64
    assert MISS > NTOK and NT % 2 == 0 and TAPS == 4

    hid = nc.dram_tensor("hid", (NTOK, ROW), F32, kind="Internal").ap()
    out_rows = out.rearrange("b n d -> (b n) d")

    ctx = ExitStack()
    with ctx:
        def sb(name, shape, dt=F32, stack=ctx):
            return stack.enter_context(nc.sbuf_tensor(name, shape, dt))

        def sem(name):
            return ctx.enter_context(nc.semaphore(name))

        bank = [ctx.enter_context(nc.psum_tensor(f"bank{i}", [128, 512], F32)) for i in range(8)]

        ident = sb("ident", [128, 128])
        same = sb("same", [T, T])
        eye = sb("eye", [T, NP])
        later = sb("later", [T, NP])
        seq_of = sb("seq_of", [T, SB])
        mean_of = sb("mean_of", [T, SB])
        ones = sb("ones", [128, 128])
        idle = sb("idle", [1, 2])
        neg_half = sb("neg_half", [128, 2])
        eps = sb("eps", [128, 2])
        var_k = sb("var_k", [128, 2])
        var_c = sb("var_c", [128, 2])
        WDT = sb("WDT", [DH, 2, H])
        tokb = sb("tokb", [T, DM])
        gamma = sb("gamma", [T, DM])
        beta = sb("beta", [T, DM])
        dtb = sb("dtb", [T, H])
        alog = sb("alog", [T, H])
        expa = sb("expa", [T, H])
        alogc = sb("alogc", [T, H])
        rate = sb("rate", [T, H])
        lnw = sb("lnw", [DH, 2])
        lnb = sb("lnb", [DH, 2])
        cw = sb("cw", [128, CH, TAPS])
        cb = sb("cb", [128, CH])
        Dc = sb("Dc", [128, NC])
        rmsw = sb("rmsw", [128, NC])
        WO = sb("WO", [128, NC, DM])
        WT = sb("WT", [128, PL, 2 * DM], F32R)
        WIh = sb("WIh", [DH, 2, WI], F32R)
        WIl = sb("WIl", [DH, 2, WI], F32R)
        W1h = sb("W1h", [DH + 1, NE * 2 * FF], F32R)
        W1l = sb("W1l", [DH + 1, NE * 2 * FF], F32R)
        W2s = sb("W2s", [128, NE * FC, 2 * DM], F32R)
        w1raw = sb("w1raw", [DH + 1, FF])
        w2raw = sb("w2raw", [128, NE, DM])
        WgT = sb("WgT", [DH, 2, NE])
        b2c = sb("b2c", [T, NE * DM])
        skip = sb("skip", [T, 2 * NG, DM])
        means = sb("means", [DH, 2, NSEQ])

        tri = sb("tri", [NSEQ, NSEQ])
        k4 = sb("k4", [NSEQ, NSEQ // SB])
        iota_s = sb("iota_s", [NSEQ, SLOTS])
        iota_t = sb("iota_t", [T, NP])
        rowid = sb("rowid", [NSEQ, T])

        one = ExitStack()
        xraw = sb("xraw", [128, 2, ST * F], stack=one)
        xTh = sb("xTh", [128, 2, ST * 128], F32R, one)
        xTl = sb("xTl", [128, 2, ST * 128], F32R, one)
        raw = ExitStack()
        wtraw = sb("wtraw", [DH, 2, KP], stack=raw)
        wiraw = sb("wiraw", [DH, 2, WI], stack=raw)
        woraw = sb("woraw", [128, NC, DM], stack=raw)
        raw.close()
        emb = sb("emb", [T, 2, DM], stack=one)
        h0 = sb("h0", [T, 2, DM], stack=one)
        xc = sb("xc", [T, 2, DM], stack=one)
        an = sb("an", [T, 2, DM], stack=one)
        st0 = sb("st0", [T, 2, 6], stack=one)
        mv0 = sb("mv0", [T, 2, 2], stack=one)
        st1 = sb("st1", [T, 2, 6], stack=one)
        mv1 = sb("mv1", [T, 2, 2], stack=one)
        rs0 = sb("rs0", [T, 2, 2], stack=one)
        rs1 = sb("rs1", [T, 2, 4], stack=one)
        xnf = sb("xnf", [DH, 2, T2], stack=one)
        xnh = sb("xnh", [DH, 2, T2], F32R, one)
        xnl = sb("xnl", [DH, 2, T2], F32R, one)
        taps = sb("taps", [128, CH, T2], stack=one)
        acc = sb("acc", [128, CH, T2], stack=one)
        xs = sb("xs", [128, NC, T2], stack=one)
        zs = sb("zs", [128, NC, T2], stack=one)
        BC = sb("BC", [128, T2], stack=one)
        CT = sb("CT", [NS, T2], stack=one)
        dtv = sb("dtv", [T, 2, H], stack=one)
        dtw = sb("dtw", [T, 9, 2 * H], stack=one)
        dt = sb("dt", [T, 2 * H], stack=one)
        dtA = sb("dtA", [T, 2, H], stack=one)
        dec = sb("dec", [T, 2 * H], stack=one)
        dteye = sb("dteye", [T, 2 * H, NP], stack=one)
        deceye = sb("deceye", [T, 2 * H, NP], stack=one)
        fade = sb("fade", [T, 2 * H, NP], stack=one)
        prod = sb("prod", [T, 2 * H, NP], stack=one)
        score = sb("score", [T, 2, T], stack=one)
        mix = sb("mix", [T, 2, H, T], stack=one)
        xtok = sb("xtok", [T, 2, DI], stack=one)
        gated = sb("gated", [128, NC, T2], stack=one)
        gsq = sb("gsq", [128, NC, T2], stack=one)
        msq = sb("msq", [T, 2], stack=one)
        rrms = sb("rrms", [T, 2], stack=one)
        hrow = sb("hrow", [T, 2, ROW], stack=one)
        st2 = sb("st2", [T, 2, 6], stack=one)
        mv2 = sb("mv2", [T, 2, 2], stack=one)
        var2 = sb("var2", [T, 2], stack=one)
        bn = sb("bn", [T, 2, DM], stack=one)
        one.close()

        rows = sb("rows", [T, 2, ROW])
        resid = sb("resid", [T, NT, DM])
        bb = sb("bb", [T, 2, DM])
        bTh = sb("bTh", [DH + 1, 2, 2 * T], F32R)
        bTl = sb("bTl", [DH + 1, 2, 2 * T], F32R)
        hg = sb("hg", [T, 2, FF])
        hTh = sb("hTh", [128, 2, FC * T], F32R)
        hTl = sb("hTl", [128, 2, FC * T], F32R)
        res = sb("res", [T, 2, DM])
        lgt = sb("lgt", [NSEQ, 4, NE])
        sm = sb("sm", [NSEQ, 8])
        oh = sb("oh", [NSEQ, 6, NE])
        over = sb("over", [NSEQ, NE, NSEQ // SB])
        tpos = sb("tpos", [T, NP])
        tcol = sb("tcol", [T, 2])
        slot = sb("slot", [NSEQ, SLOTS])
        wcol = sb("wcol", [NSEQ, T])
        pick = sb("pick", [T, NT, SB])
        pickw = sb("pickw", [T, NT, SB])
        idf = sb("idf", [T, NT])
        idx = sb("idx", [T, NT], U32)
        wt = sb("wt", [T, NT])
        ef = sb("ef", [NSEQ, 2, NT])
        ei = sb("ei", [NSEQ, NT], I32)
        idg = sb("idg", [T, 2], U32)
        ids = sb("ids", [T, 2], U32)

        bT = (bank[0], bank[1])
        bE = bank[2]
        bX = bank[3]
        bP = (bank[4], bank[5])
        bY = (bank[6], bank[7])
        bIn = (bP[0], bP[1], bP[0], bP[1], bY[0], bY[1], bP[0])

        c_const = sem("c_const")
        c_wt = sem("c_wt")
        c_wi = sem("c_wi")
        c_x = [sem("c_x0"), sem("c_x1")]
        c_C = sem("c_C")
        c_w1 = sem("c_w1")
        c_w2 = sem("c_w2")
        c_hid = sem("c_hid")
        p_ident = sem("p_ident")
        p_mask = sem("p_mask")
        p_idle = sem("p_idle")
        a_wi = sem("a_wi")
        v_wi = sem("v_wi")
        v_mask = sem("v_mask")
        a_expa = sem("a_expa")
        t_wt = sem("t_wt")
        a_wt = sem("a_wt")
        v_wt = sem("v_wt")
        v_alog = sem("v_alog")
        v_wo = sem("v_wo")
        t_x = sem("t_x")
        a_xh = sem("a_xh")
        v_xl = sem("v_xl")
        t_emb = sem("t_emb")
        v_emb = sem("v_emb")
        v_ln = sem("v_ln")
        p_ln = sem("p_ln")
        t_xn = sem("t_xn")
        a_xn = sem("a_xn")
        v_xn = sem("v_xn")
        t_dt = sem("t_dt")
        v_dtv = sem("v_dtv")
        t_in = sem("t_in")
        a_cv = sem("a_cv")
        v_cv = sem("v_cv")
        a_si = sem("a_si")
        a_z = sem("a_z")
        a_dt = sem("a_dt")
        v_sp = sem("v_sp")
        p_dt = sem("p_dt")
        t_sd = sem("t_sd")
        a_xt = sem("a_xt")
        v_mix = sem("v_mix")
        p_mix = sem("p_mix")
        t_y = sem("t_y")
        v_gate = sem("v_gate")
        a_sq = sem("a_sq")
        t_out = sem("t_out")
        v_o = sem("v_o")
        p_o = sem("p_o")
        t_mean = sem("t_mean")
        v_mean = sem("v_mean")
        a_w1 = sem("a_w1")
        p_w1 = sem("p_w1")
        t_r = sem("t_r")
        v_r = sem("v_r")
        a_r = sem("a_r")
        p_clear = sem("p_clear")
        c_g = [sem("c_g0"), sem("c_g1")]
        c_s = [sem("c_s0"), sem("c_s1")]
        p_id = sem("p_id")
        p_is = sem("p_is")
        v_b = sem("v_b")
        t_b = sem("t_b")
        a_b = sem("a_b")
        v_bl = sem("v_bl")
        t_up = sem("t_up")
        a_gelu = sem("a_gelu")
        t_h = sem("t_h")
        a_hh = sem("a_hh")
        v_hl = sem("v_hl")
        t_dn = sem("t_dn")
        v_fin = sem("v_fin")

        EMB, EMB_READ, EMB_STAT = 4, 2, 4
        VLN, VLN_H0, VLN_STAT, VLN_XC, VLN_AN = 5, 1, 3, 4, 5
        LNP, LNP_RS0, LNP_H0, LNP_RS1, LNP_SKIP = 8, 2, 4, 7, 8
        SP, SP_DT = 17, 15
        OV, OV_MS, OV_ROWS, OV_STAT = 10, 1, 8, 8
        PO, PO_RR, PO_R = 3, 1, 3
        CONSTS = 18


        eB = bank[0]
        eU = (bank[1], bank[2])
        eH = (bank[3], bank[4])
        eD = (bank[5], bank[6])
        HT = FC // 2 * T
        R_SCORE, R_PICK, R_PLACE = 1, 2, 3
        VR_LOGIT = 3 + 3
        VR_CHOICE = VR_LOGIT + 4 + 2 * NE
        VR_PLACE = VR_CHOICE + NE + 7
        VR_TILE = VR_PLACE + NE
        VR_ALL = VR_TILE + 5

        def stage_one_done(eng):
            eng.wait_ge(c_hid, 32 * NG)
            eng.wait_ge(t_mean, NG)
            eng.wait_ge(v_mean, NG)

        def tiles(eng, at, first):
            for s in range(first, 4):
                at(s, s % 2)
            with eng.Fori(0, (NT - 8) // 2) as m:
                at(2 * m + 4, 0)
                at(2 * m + 5, 1)
            for s in range(NT - 4, NT + 2):
                at(s, s % 2)

        def tile(i):
            return not isinstance(i, int) or 0 <= i < NT

        def left_by(i, per=1):
            return per * (i - 1)

        def turns(i, par):
            return (i - par) // 2

        def stage_two_pool(pool):
            gp = nc.gpsimd
            stage_one_done(pool)
            st = Steps(pool, p_clear, 3, 0)
            st.then(gp.memset(rows[:, :, :], 0.0))
            st.then(gp.memset(bTh[DH:DH + 1, :, T:2 * T].bitcast(F32), 1.0))
            st.then(gp.memset(bTl[DH:DH + 1, :, T:2 * T].bitcast(F32), 0.0))
            pool.wait_ge(v_r, VR_ALL)

            def at(s, par):
                if tile(s + 3):
                    i, p = s + 3, (par + 1) % 2
                    need(pool, v_b, left_by(i, 2))
                    gp.tensor_copy(idg[:, p:p + 1], idx[:, ds(i, 1)]).then_inc(p_id, 1)
                    pool.wait_ge(p_id, i + 1)
                    apart(pool)
                    gp.indirect_dma_start(
                        out=rows[:, p, :], out_offset=None, in_=hid,
                        in_offset=bass.IndirectOffsetOnAxis(ap=idg[:, p:p + 1], axis=0),
                        bounds_check=NTOK - 1, oob_is_err=False).then_inc(c_g[p], 16)
                if tile(s - 2):
                    i, p = s - 2, par
                    need(pool, c_s[p], 16 * turns(i, p))
                    gp.tensor_copy(ids[:, p:p + 1], idx[:, ds(i, 1)]).then_inc(p_is, 1)
                    pool.wait_ge(p_is, i + 1)
                    pool.wait_ge(v_fin, 3 * i + 3)
                    apart(pool)
                    gp.indirect_dma_start(
                        out=out_rows, out_offset=bass.IndirectOffsetOnAxis(ap=ids[:, p:p + 1], axis=0),
                        in_=res[:, p, :], in_offset=None,
                        bounds_check=NTOK - 1, oob_is_err=False).then_inc(c_s[p], 16)

            tiles(pool, at, -3)

        def stage_two_act(act):
            ac = nc.scalar
            stage_one_done(act)
            act.wait_ge(v_r, VR_LOGIT)
            ac.activation(lgt[:, 1, :], lgt[:, 0, :], ACT.Exp, bias=sm[:, 1:2], accum_out=sm[:, 2:3])\
              .then_inc(a_r, 1)

            def at(s, par):
                def gelu(f):
                    act.wait_ge(t_up, 2 * s + f + 1)
                    need(act, t_h, left_by(s, 2))
                    ac.activation(hg[:, par, f * FH:(f + 1) * FH], eU[f][0:T, 0:FH], ACT.Gelu)\
                      .then_inc(a_gelu, 1)

                if tile(s + 1):
                    i, p = s + 1, (par + 1) % 2
                    act.wait_ge(t_b, i + 1)
                    need(act, t_up, left_by(i, 2))
                    ac.activation(bTh[0:DH, p, :], eB[0:DH, 0:2 * T], ACT.Copy).then_inc(a_b, 1)
                if tile(s):
                    gelu(0)
                if tile(s - 1):
                    i, p = s - 1, (par + 1) % 2
                    for f in range(2):
                        act.wait_ge(t_h, 2 * i + f + 1)
                        need(act, t_dn, left_by(i))
                        ac.activation(hTh[:, p, f * HT:(f + 1) * HT], eH[f][:, 0:HT], ACT.Copy)\
                          .then_inc(a_hh, 1)
                if tile(s):
                    gelu(1)

            tiles(act, at, -1)

        def stage_two_dve(dve):
            ve = nc.vector
            stage_one_done(dve)
            dve.wait_ge(p_mask, 13)
            st = Steps(dve, v_r, VR_ALL, 0)
            st.then(ve.tensor_tensor(tpos[:, :], iota_t[:, :], eye[:, :], ALU.mult))
            st.then(ve.tensor_reduce(tcol[:, 0:1], tpos[:, :], AX.X, ALU.add))
            st.did(ve.tensor_scalar(tcol[:, 1:2], tcol[:, 0:1], float(MISS), None, ALU.add))
            dve.wait_ge(t_r, R_SCORE)
            st.then(ve.tensor_copy(lgt[:, 0, :], bank[3][0:NSEQ, 0:NE]))
            st.then(ve.tensor_reduce(sm[:, 0:1], lgt[:, 0, :], AX.X, ALU.max))
            st.then(ve.tensor_scalar(sm[:, 1:2], sm[:, 0:1], -1.0, None, ALU.mult))
            dve.wait_ge(a_r, 1)
            st.then(ve.reciprocal(sm[:, 3:4], sm[:, 2:3]))
            st.then(ve.tensor_scalar(lgt[:, 2, :], lgt[:, 1, :], sm[:, 3:4], None, ALU.mult))
            st.then(ve.tensor_reduce(sm[:, 4:5], lgt[:, 2, :], AX.X, ALU.max))
            st.then(ve.tensor_scalar(oh[:, 0, :], lgt[:, 2, :], sm[:, 4:5], None, ALU.is_ge))
            left = ones[0:NSEQ, 0:1]
            for e in range(NE):
                st.then(ve.tensor_tensor(oh[:, 1, e:e + 1], oh[:, 0, e:e + 1], left, ALU.mult))
                st.then(ve.tensor_tensor(sm[:, 5:6], left, oh[:, 1, e:e + 1], ALU.subtract))
                left = sm[:, 5:6]
            st.did(ve.tensor_scalar(wcol[:, :], ones[0:NSEQ, 0:T], sm[:, 4:5], None, ALU.mult))
            dve.wait_ge(t_r, R_PICK)
            st.then(ve.tensor_tensor(over[:, :, :],
                                     bank[3][0:NSEQ, 16:16 + NE].unsqueeze(2).broadcast_to((NSEQ, NE, NSEQ // SB)),
                                     k4[:, :].unsqueeze(1).broadcast_to((NSEQ, NE, NSEQ // SB)), ALU.is_gt))
            st.did(ve.tensor_reduce(oh[:, 2, :], over[:, :, :], AX.X, ALU.add))
            st.then(ve.memset(oh[:, 3, 0:1], 0.0))
            for e in range(1, NE):
                st.then(ve.tensor_tensor(oh[:, 3, e:e + 1], oh[:, 3, e - 1:e], oh[:, 2, e - 1:e], ALU.add))
            st.then(ve.scalar_tensor_tensor(oh[:, 4, :], oh[:, 3, :], float(SB), bank[3][0:NSEQ, 8:8 + NE],
                                            ALU.mult, ALU.add))
            st.then(ve.tensor_tensor(oh[:, 5, :], oh[:, 4, :], oh[:, 1, :], ALU.mult))
            st.then(ve.tensor_reduce(sm[:, 6:7], oh[:, 5, :], AX.X, ALU.add))
            st.did(ve.tensor_scalar(slot[:, :], iota_s[:, :], sm[:, 6:7], None, ALU.is_equal))
            assert st.n == VR_PLACE
            st.then(ve.tensor_scalar(ef[:, 0, :], iota_s[:, 0:NT], oh[:, 3, 1:2], None, ALU.is_ge))
            for e in range(2, NE):
                st.then(ve.scalar_tensor_tensor(ef[:, 0, :], iota_s[:, 0:NT], oh[:, 3, e:e + 1], ef[:, 0, :],
                                                ALU.is_ge, ALU.add))
            st.did(ve.tensor_copy(ei[:, :], ef[:, 0, :]))
            assert st.n == VR_TILE
            dve.wait_ge(t_r, R_PLACE)
            spread = seq_of[:, :].unsqueeze(1).broadcast_to((T, NT, SB))
            st.did(ve.tensor_tensor(pick[:, :, :], bank[4][0:T, 0:SLOTS].rearrange("p (k q) -> p k q", q=SB),
                                    spread, ALU.mult))
            st.then(ve.tensor_tensor(pickw[:, :, :], bank[5][0:T, 0:SLOTS].rearrange("p (k q) -> p k q", q=SB),
                                     spread, ALU.mult))
            st.then(ve.tensor_reduce(idf[:, :], pick[:, :, :], AX.X, ALU.add))
            st.did(ve.tensor_scalar(idx[:, :], idf[:, :], tcol[:, 1:2], None, ALU.add))
            st.then(ve.tensor_reduce(wt[:, :], pickw[:, :, :], AX.X, ALU.add))
            assert st.n == VR_ALL

            def fin(i, p):
                st = Steps(dve, v_fin, 3, i)
                e = dve.value_load(ei[0:1, ds(i, 1)], min_val=0, max_val=NE - 1)
                dve.wait_ge(t_dn, i + 1)
                need(dve, c_s[p], 16 * turns(i, p))
                st.then(ve.tensor_tensor(res[:, p, :], eD[p][0:T, DM:2 * DM], b2c[:, ds(e * DM, DM)], ALU.add))
                st.then(ve.tensor_tensor(res[:, p, :], eD[p][0:T, 0:DM], res[:, p, :], ALU.add))
                st.did(ve.scalar_tensor_tensor(res[:, p:p + 1, :], res[:, p:p + 1, :], wt[:, ds(i, 1)],
                                               resid[:, ds(i, 1), :], ALU.mult, ALU.add))

            def at(s, par):
                if tile(s + 1):
                    i, p = s + 1, (par + 1) % 2
                    dve.wait_ge(a_b, i + 1)
                    need(dve, t_up, left_by(i, 2))
                    ve.tensor_tensor(bTl[0:DH, p, :], eB[0:DH, 0:2 * T], bTh[0:DH, p, :].bitcast(F32),
                                     ALU.subtract).then_inc(v_bl, 1)
                if tile(s + 2):
                    i, p = s + 2, par
                    dve.wait_ge(c_g[p], 16 * (turns(i, p) + 1))
                    need(dve, t_b, left_by(i))
                    ve.tensor_scalar(bb[:, p, :], rows[:, p, 0:DM], rows[:, p, DM:DM + 1],
                                     rows[:, p, DM + 1:DM + 2], ALU.subtract, ALU.mult).then_inc(v_b, 1)
                    ve.tensor_copy(resid[:, ds(i, 1), :], rows[:, p:p + 1, 0:DM]).then_inc(v_b, 1)
                if tile(s - 2):
                    fin(s - 2, par)
                if tile(s - 1):
                    i, p = s - 1, (par + 1) % 2
                    for f in range(2):
                        dve.wait_ge(a_hh, 2 * i + f + 1)
                        need(dve, t_dn, left_by(i))
                        ve.tensor_tensor(hTl[:, p, f * HT:(f + 1) * HT], eH[f][:, 0:HT],
                                         hTh[:, p, f * HT:(f + 1) * HT].bitcast(F32), ALU.subtract)\
                          .then_inc(v_hl, 1)

            tiles(dve, at, -2)

        def stage_two_pe(pe):
            te = nc.tensor
            stage_one_done(pe)
            pe.wait_ge(p_mask, 13)
            for c in range(2):
                last = te.matmul(bank[3][0:NSEQ, 0:NE], means[:, c, :], WgT[:, c, :], start=(c == 0), stop=(c == 1))
            last.then_inc(t_r, 1)
            pe.wait_ge(v_r, VR_CHOICE)
            te.matmul(bank[3][0:NSEQ, 8:8 + NE], tri[:, :], oh[:, 1, :], start=True, stop=True)
            te.matmul(bank[3][0:NSEQ, 16:16 + NE], ones[0:NSEQ, 0:NSEQ], oh[:, 1, :], start=True, stop=True)\
              .then_inc(t_r, 1)
            pe.wait_ge(v_r, VR_PLACE)
            te.matmul(bank[4][0:T, 0:SLOTS], rowid[:, :], slot[:, :], start=True, stop=True)
            te.matmul(bank[5][0:T, 0:SLOTS], wcol[:, :], slot[:, :], start=True, stop=True).then_inc(t_r, 1)
            pe.wait_ge(v_r, VR_ALL)
            pe.wait_ge(p_clear, 3)
            pe.wait_ge(p_w1, 2 * 2 * NE)

            def at(s, par):
                def up(f, e):
                    need(pe, a_gelu, 2 * (s - 1) + f + 1)
                    n = 0
                    for c in range(2):
                        k = DH + c
                        w = ds(e * (2 * FF) + (c * FF + f * FH), FH)
                        for a, b in ((bTh, W1h), (bTh, W1l), (bTl, W1h)):
                            last = te.matmul(eU[f][0:T, 0:FH], a[0:k, par, c * T:(c + 1) * T], b[0:k, w],
                                             start=(n == 0), stop=(n == 5))
                            n += 1
                    last.then_inc(t_up, 1)

                if tile(s + 1):
                    i, p = s + 1, (par + 1) % 2
                    pe.wait_ge(v_b, 2 * i + 1)
                    need(pe, v_bl, i)
                    for c in range(2):
                        last = te.transpose(eB[0:DH, c * T:(c + 1) * T], bb[:, p, c * DH:(c + 1) * DH],
                                            ident[0:T, 0:T])
                    last.then_inc(t_b, 1)
                if tile(s):
                    e = pe.value_load(ei[0:1, ds(s, 1)], min_val=0, max_val=NE - 1)
                    pe.wait_ge(v_bl, s + 1)
                    up(0, e)
                if tile(s - 2):
                    i, p = s - 2, par
                    e_down = pe.value_load(ei[0:1, ds(i, 1)], min_val=0, max_val=NE - 1)
                    pe.wait_ge(v_hl, 2 * i + 2)
                    need(pe, v_fin, 3 * (i - 2) + 2)
                    def rest(c):
                        te.matmul(eD[p][0:T, DM:2 * DM], hTl[:, p, c * T:(c + 1) * T],
                                  W2s[:, ds(e_down * FC + c, 1), 0:DM].rearrange("p a d -> p (a d)"),
                                  start=False, stop=False, skip_group_check=True)

                    for c in range(FC):
                        if c > 0:
                            rest(c)
                        last = te.matmul(eD[p][0:T, 0:2 * DM], hTh[:, p, c * T:(c + 1) * T],
                                         W2s[:, ds(e_down * FC + c, 1), :].rearrange("p a d -> p (a d)"),
                                         start=(c == 0), stop=(c == FC - 1), skip_group_check=True)
                        if c == 0:
                            rest(c)
                    last.then_inc(t_dn, 1)
                if tile(s - 1):
                    i, p = s - 1, (par + 1) % 2
                    for f in range(2):
                        pe.wait_ge(a_gelu, 2 * i + f + 1)
                        need(pe, v_hl, 2 * (i - 1) + f + 1)
                        for c in range(FC // 2):
                            last = te.transpose(eH[f][:, c * T:(c + 1) * T],
                                                hg[:, p, f * FH + c * 128:f * FH + (c + 1) * 128], ident[0:T, 0:T])
                        last.then_inc(t_h, 1)
                if tile(s):
                    up(1, e)

            tiles(pe, at, -1)

        block = ctx.enter_context(nc.Block())

        def raw_weights_read(eng):
            eng.wait_ge(t_wt, PL // 2)
            eng.wait_ge(a_wi, 2)
            eng.wait_ge(v_wi, 1)
            eng.wait_ge(v_wo, NC + 1)

        def bodies(eng, body, first, end, last):
            for g in range(first):
                body(g)
            with eng.Fori(first, end) as g:
                body(g)
            for g in range(end, last + 1):
                body(g)

        def at_index(ap, k):
            return ap[k] if isinstance(k, int) else ap[ds(k, 1)].squeeze(0)

        def apart(eng):
            cell = idle[0:1, 0:1] if eng is nc.vector else idle[0:1, 1:2]
            eng.tensor_tensor(cell, cell, cell, ALU.mult)

        def live(g):
            return not isinstance(g, int) or 0 <= g < NG

        @block.sync
        def _(sp):
            x_t = x.rearrange("(k b) (m r) f -> k m b (r f)", b=SB, r=ST)

            def load_x(k, j):
                need(sp, t_x, 2 * (k - 1))
                sp.dma_start(xraw[:, j, :], at_index(x_t, k)).then_inc(c_x[j], 16)

            sp.dma_start(wtraw[:, :, :], tok_W.rearrange("(c p) k -> p c k", p=DH)).then_inc(c_wt, 16)
            load_x(0, 0)
            load_x(1, 1)
            sp.dma_start(wiraw[:, :, :], W_in.rearrange("(c p) k -> p c k", p=DH)).then_inc(c_wi, 16)
            for dst, src in ((tokb, tok_b), (gamma, tok_gamma), (beta, tok_beta), (dtb, dt_bias),
                             (alog, A_log)):
                sp.dma_start(dst[:, :], src.partition_broadcast(T)).then_inc(c_const, 16)
            sp.dma_start(b2c[:, :], b2.rearrange("e d -> (e d)").partition_broadcast(T)).then_inc(c_const, 16)
            sp.dma_start(woraw[:, :, :], W_out.rearrange("(c p) d -> p c d", p=128)).then_inc(c_const, 16)
            with nc.allow_non_contiguous_dma(reason="small constants by partition"):
                sp.dma_start(lnw[:, :], ln_w.rearrange("(c p) -> p c", p=DH)).then_inc(c_const, 16)
                sp.dma_start(lnb[:, :], ln_b.rearrange("(c p) -> p c", p=DH)).then_inc(c_const, 16)
                sp.dma_start(cw[:, 0, :], conv_w[DI:DI + 128, :]).then_inc(c_const, 16)
                sp.dma_start(cw[:, 1:CH, :], conv_w[0:DI, :].rearrange("(c p) k -> p c k", p=128))\
                  .then_inc(c_const, 16)
                sp.dma_start(cb[:, 0:1], conv_b[DI:DI + 128].rearrange("(p a) -> p a", a=1))\
                  .then_inc(c_const, 16)
                sp.dma_start(cb[:, 1:CH], conv_b[0:DI].rearrange("(c p) -> p c", p=128)).then_inc(c_const, 16)
                sp.dma_start(rmsw[:, :], rms_w.rearrange("(c p) -> p c", p=128)).then_inc(c_const, 16)
                for half in range(2):
                    sp.dma_start(Dc[half * HD:(half + 1) * HD, :],
                                 D.rearrange("(c a) -> a c", a=2)[half, :].partition_broadcast(HD))\
                      .then_inc(c_const, 16)
                for c in range(2):
                    sp.dma_start(WgT[:, c, :], Wg[:, c * DH:(c + 1) * DH].rearrange("e p -> p e"))\
                      .then_inc(c_const, 16)
            w1_t = W1.rearrange("e (c p) f -> (e c) p f", p=DH)
            w2_t = W2.rearrange("e (c p) d -> p (e c) d", p=128)

            def load_experts(i):
                sp.dma_start(w1raw[0:DH, :], at_index(w1_t, i)).then_inc(c_w1, 16)
                sp.dma_start(w1raw[DH:DH + 1, :], b1[ds(i // 2, 1), :]).then_inc(c_w1, 16)
                sp.dma_start(w2raw[:, :, :], w2_t[:, ds(i * NE, NE), :]).then_inc(c_w2, 16)

            load_experts(0)

            hid_t = hid.rearrange("(k b n) r -> k n b r", b=SB, n=NP)

            def body(g):
                if not isinstance(g, int) or g < NG - 1:
                    load_x(2 * g + 2, 0)
                    load_x(2 * g + 3, 1)
                if not isinstance(g, int) or g == 2:
                    sp.wait_ge(p_w1, 2 * (g - 1))
                    load_experts(g - 1)
                if live(g - 1):
                    q = g - 1
                    sp.wait_ge(a_si, CH * q + 1)
                    need(sp, t_sd, 4 * (q - 1) + 1)
                    sp.dma_start(CT[:, :], BC[NS:2 * NS, :]).then_inc(c_C, 16)
                if live(g - 3):
                    u = g - 3
                    sp.wait_ge(v_o, OV * u + OV_STAT)
                    sp.wait_ge(p_o, PO * u + PO_R)
                    for j in range(2):
                        sp.dma_start(at_index(hid_t, 2 * u + j), hrow[:, j, :]).then_inc(c_hid, 16)

            bodies(sp, body, 3, NG - 1, NG + 2)
            for p in range(2):
                sp.wait_ge(c_s[p], 16 * (NT // 2))

        @block.gpsimd
        def _(pool):
            gp = nc.gpsimd
            gp.memset(ident[:, :], 0.0).then_inc(p_ident, 1)
            gp.memset(ones[:, :], 1.0).then_inc(p_mask, 1)
            gp.memset(neg_half[:, :], -0.5).then_inc(p_mask, 1)
            for dst, value in ((eps[:, :], EPS), (var_k[:, 0:1], 1.0), (var_k[:, 1:2], 1.0 + EPS),
                               (var_c[:, 0:1], EPS), (var_c[:, 1:2], EPS * EPS)):
                gp.memset(dst, value).then_inc(p_mask, 1)
            gp.memset(idle[:, :], 0.0).then_inc(p_idle, 1)
            pool.wait_ge(p_idle, 1)
            pool.wait_ge(p_ident, 1)
            gp.affine_select(out=ident[:, :], in_=ident[:, :], compare_op=ALU.not_equal, fill=1.0, base=0,
                             pattern=[[-1, 128]], channel_multiplier=1).then_inc(p_ident, 1)
            pool.wait_ge(p_mask, 7)
            gp.affine_select(out=later[:, :], in_=ones[0:T, 0:NP], compare_op=ALU.is_gt, fill=0.0, base=0,
                             pattern=[[SB, NP]], channel_multiplier=-1).then_inc(p_mask, 1)
            gp.affine_select(out=tri[:, :], in_=ones[0:NSEQ, 0:NSEQ], compare_op=ALU.is_gt, fill=0.0, base=0,
                             pattern=[[1, NSEQ]], channel_multiplier=-1).then_inc(p_mask, 1)
            for dst, pattern, base, by_row in ((k4, [[SB, NSEQ // SB]], 0, 0), (iota_s, [[1, SLOTS]], 0, 0),
                                               (iota_t, [[1, NP]], 0, 0), (rowid, [[0, T]], -MISS, NP)):
                gp.iota(dst[:, :], pattern=pattern, base=base, channel_multiplier=by_row,
                        allow_small_or_imprecise_dtypes=True).then_inc(p_mask, 1)
            raw_weights_read(pool)

            def root_a(k, j):
                st = Steps(pool, p_ln, LNP, k)
                pool.wait_ge(v_emb, EMB * k + EMB_STAT)
                st.then(gp.tensor_tensor(rs0[:, j, 0:1], mv0[:, j, 1:2], eps[0:T, 0:1], ALU.add))
                st.did(gp.tensor_tensor(rs0[:, j, 1:2], rs0[:, j, 0:1], neg_half[0:T, 0:1], ALU.pow))
                assert st.n == LNP_RS0

            def scale(k, j):
                st = Steps(pool, p_ln, LNP, k)
                st.n = LNP_RS0
                pool.wait_ge(v_ln, VLN * k + VLN_H0)
                st.then(gp.tensor_tensor(h0[:, j, :], h0[:, j, :], gamma[:, :], ALU.mult))
                st.did(gp.tensor_tensor(h0[:, j, :], h0[:, j, :], beta[:, :], ALU.add))
                assert st.n == LNP_H0

            def root_b(k, j):
                st = Steps(pool, p_ln, LNP, k)
                st.n = LNP_H0
                pool.wait_ge(v_ln, VLN * k + VLN_STAT)
                st.then(gp.tensor_tensor(rs1[:, j, 0:2], mv1[:, j, 1:2].broadcast_to((T, 2)), var_k[0:T, :],
                                         ALU.mult))
                st.then(gp.tensor_tensor(rs1[:, j, 0:2], rs1[:, j, 0:2], var_c[0:T, :], ALU.add))
                st.did(gp.tensor_tensor(rs1[:, j, 2:4], rs1[:, j, 0:2], neg_half[0:T, :], ALU.pow))
                assert st.n == LNP_RS1

            def add_skip(k, j):
                st = Steps(pool, p_ln, LNP, k)
                st.n = LNP_RS1
                pool.wait_ge(v_ln, VLN * k + VLN_AN)
                st.did(gp.tensor_tensor(skip[:, ds(k, 1), :], h0[:, j:j + 1, :], an[:, j:j + 1, :], ALU.add))
                assert st.n == LNP_SKIP

            def split_experts(i):
                pool.wait_ge(a_w1, 2 * i + 2)
                gp.tensor_tensor(W1l[:, ds(i * FF, FF)], w1raw[:, :],
                                 W1h[:, ds(i * FF, FF)].bitcast(F32), ALU.subtract).then_inc(p_w1, 1)
                gp.tensor_tensor(W2s[:, ds(i * NE, NE), DM:2 * DM], w2raw[:, :, :],
                                 W2s[:, ds(i * NE, NE), 0:DM].bitcast(F32), ALU.subtract).then_inc(p_w1, 1)

            def body(g):
                if live(g - 1):
                    scale(2 * (g - 1) + 1, 1)
                if live(g - 3):
                    pool.wait_ge(v_o, OV * (g - 3) + OV_MS)
                    gp.tensor_tensor(rrms[:, :], msq[:, :], neg_half[0:T, :], ALU.pow).then_inc(p_o, 1)
                if live(g - 1):
                    root_b(2 * (g - 1) + 1, 1)
                if live(g - 2):
                    u = g - 2
                    pool.wait_ge(v_mix, 4 * u + 3)
                    need(pool, t_y, 2 * u)
                    gp.tensor_tensor(
                        mix[:, 1, :, :].rearrange("p h (n q) -> p h n q", q=SB),
                        score[:, 1, :].rearrange("p (n q) -> p n q", q=SB).unsqueeze(1)
                        .broadcast_to((T, H, NP, SB)),
                        prod[:, H:2 * H, :].unsqueeze(3).broadcast_to((T, H, NP, SB)),
                        ALU.mult).then_inc(p_mix, 1)
                if live(g - 1):
                    add_skip(2 * (g - 1) + 1, 1)
                if live(g - 3):
                    u = g - 3
                    st = Steps(pool, p_o, PO, u)
                    st.n = PO_RR
                    pool.wait_ge(v_o, OV * u + OV_STAT)
                    st.then(gp.tensor_tensor(var2[:, :], mv2[:, :, 1], eps[0:T, :], ALU.add))
                    st.did(gp.tensor_tensor(hrow[:, :, DM + 1], var2[:, :], neg_half[0:T, :], ALU.pow))
                if live(g):
                    root_a(2 * g, 0)
                    scale(2 * g, 0)
                    root_b(2 * g, 0)
                if not isinstance(g, int) or 2 <= g <= 7:
                    split_experts(g - 2)
                if live(g):
                    add_skip(2 * g, 0)
                if live(g - 1):
                    q = g - 1
                    st = Steps(pool, p_dt, 2, q)
                    pool.wait_ge(v_sp, SP * q + SP_DT)
                    need(pool, v_mix, 4 * (q - 1) + 3)
                    st.did(gp.tensor_tensor(dteye[:, :, :],
                                            eye[:, :].unsqueeze(1).broadcast_to((T, 2 * H, NP)),
                                            dt[:, :].unsqueeze(2).broadcast_to((T, 2 * H, NP)), ALU.mult))
                    pool.wait_ge(a_dt, 3 * q + 3)
                    need(pool, t_sd, 4 * (q - 1) + 2)
                    st.did(gp.tensor_tensor(deceye[:, :, :],
                                            eye[:, :].unsqueeze(1).broadcast_to((T, 2 * H, NP)),
                                            dec[:, :].unsqueeze(2).broadcast_to((T, 2 * H, NP)), ALU.mult))
                if live(g):
                    root_a(2 * g + 1, 1)

            bodies(pool, body, 3, NG, NG + 2)
            stage_two_pool(pool)

        @block.scalar
        def _(act):
            ac = nc.scalar
            for r in range(PL // 2):
                act.wait_ge(t_wt, r + 1)
                ac.activation(WT[:, 2 * r:2 * r + 2, 0:DM],
                              bank[2 + r % 4][:, 0:2 * DM].rearrange("p (t d) -> p t d", t=2),
                              ACT.Copy).then_inc(a_wt, 1)
            def high(k, j):
                for h in range(2):
                    act.wait_ge(t_x, 2 * k + h + 1)
                    need(act, t_emb, k - 1)
                    ac.activation(xTh[:, j, h * 512:(h + 1) * 512], bT[h][:, :], ACT.Copy).then_inc(a_xh, 1)

            def body(g):
                if live(g - 2):
                    u = g - 2
                    for j, b in enumerate((bP[1], bY[0])):
                        act.wait_ge(t_sd, 4 * u + 3 + j)
                        need(act, t_y, 2 * u)
                        ac.activation(xtok[:, j, :], b[0:T, 0:DI], ACT.Copy).then_inc(a_xt, 1)
                if not isinstance(g, int) or 2 <= g <= 7:
                    i = g - 2
                    act.wait_ge(c_w1, 32 * (i + 1))
                    ac.activation(W1h[:, ds(i * FF, FF)], w1raw[:, :], ACT.Copy).then_inc(a_w1, 1)
                    act.wait_ge(c_w2, 16 * (i + 1))
                    ac.activation(W2s[:, ds(i * NE, NE), 0:DM], w2raw[:, :, :], ACT.Copy).then_inc(a_w1, 1)
                if live(g - 1):
                    q = g - 1
                    act.wait_ge(t_xn, q + 1)
                    need(act, v_xn, q)
                    for c in range(2):
                        ac.activation(xnf[:, c, :], bX[0:DH, c * T2:(c + 1) * T2], ACT.Identity,
                                      bias=lnb[:, c:c + 1], scale=lnw[:, c:c + 1]).then_inc(a_xn, 1)
                    act.wait_ge(a_xn, 3 * q + 2)
                    need(act, t_in, NCH * q)
                    ac.activation(xnh[:, :, :], xnf[:, :, :], ACT.Copy).then_inc(a_xn, 1)
                if live(g + 1):
                    high(2 * g + 2, 0)
                if live(g - 1):
                    act.wait_ge(v_dtv, q + 1)
                    need(act, v_sp, SP * q)
                    ac.activation(dtw[:, 0, :], dtv[:, :, :].rearrange("p u h -> p (u h)"), ACT.Abs)\
                      .then_inc(a_dt, 1)
                    act.wait_ge(a_dt, 3 * q + 1)
                    ac.activation(dtw[:, 1, :], dtw[:, 0, :], ACT.Exp, scale=-1.0).then_inc(a_dt, 1)

                    def start(i):
                        act.wait_ge(t_in, NCH * q + i + 1)
                        need(act, v_cv, 3 * CH * (q - 1) + 3 * (i + 1))
                        ac.activation(taps[:, i, :], bP[i % 2][:, 0:T2], ACT.Copy).then_inc(a_cv, 1)
                        need(act, a_si, CH * (q - 1) + i + 1)
                        ac.activation(acc[:, i, :], bP[i % 2][:, 0:T2], ACT.Identity, bias=cb[:, i:i + 1],
                                      scale=cw[:, i, TAPS - 1:TAPS]).then_inc(a_cv, 1)

                    def silu(i):
                        act.wait_ge(v_cv, 3 * CH * q + 3 * (i + 1))
                        if i == 0:
                            need(act, t_sd, 4 * (q - 1) + 1)
                            need(act, c_C, 16 * q)
                        else:
                            need(act, t_sd, 4 * q)
                            need(act, v_gate, 4 * (q - 1) + 3)
                        ac.activation(BC[:, :] if i == 0 else xs[:, i - 1, :], acc[:, i, :], ACT.Silu)\
                          .then_inc(a_si, 1)

                    def gate(i):
                        act.wait_ge(t_in, NCH * q + CH + i + 1)
                        need(act, v_gate, 4 * q)
                        ac.activation(zs[:, i, :], bIn[CH + i][:, 0:T2], ACT.Silu).then_inc(a_z, 1)

                    start(0)
                    start(1)
                    start(2)
                    start(3)
                if live(g - 1):
                    silu(0)
                    gate(0)
                    silu(1)
                if live(g - 2):
                    u = g - 2
                    act.wait_ge(v_gate, 4 * u + 4)
                    need(act, t_out, u)
                    ac.activation(gsq[:, :, :], gated[:, :, :], ACT.Square).then_inc(a_sq, 1)
                if live(g - 1):
                    gate(1)
                    silu(2)
                    gate(2)
                    silu(3)
                    act.wait_ge(v_sp, SP * q + SP)
                    need(act, p_dt, 2 * q)
                    ac.activation(dec[:, :], dtA[:, :, :].rearrange("p u h -> p (u h)"), ACT.Exp,
                                  scale=-RATE_UNIT).then_inc(a_dt, 1)
                if live(g + 1):
                    high(2 * g + 3, 1)

            high(0, 0)
            act.wait_ge(c_wi, 16)
            ac.activation(WIh[:, :, :], wiraw[:, :, :], ACT.Copy).then_inc(a_wi, 1)
            high(1, 1)
            ac.activation(WDT[:, :, :], wiraw[:, :, WI - H:WI], ACT.Copy).then_inc(a_wi, 1)
            act.wait_ge(c_const, 16 * CONSTS)
            act.wait_ge(v_alog, 1)
            ac.activation(expa[:, :], alogc[:, :], ACT.Exp).then_inc(a_expa, 1)
            raw_weights_read(act)
            bodies(act, body, 3, NG - 1, NG + 1)
            stage_two_act(act)

        @block.vector
        def _(dve):
            ve = nc.vector
            dve.wait_ge(p_ident, 2)
            ve.tensor_reduce(eye[:, :], ident[0:T, 0:T].rearrange("p (n q) -> p n q", q=SB), AX.X, ALU.add)\
              .then_inc(v_mask, 1)
            ve.tensor_reduce(seq_of[:, :], ident[0:T, 0:T].rearrange("p (n q) -> p q n", q=SB), AX.X, ALU.add)\
              .then_inc(v_mask, 1)
            dve.wait_ge(v_mask, 2)
            ve.tensor_copy(same[:, :].rearrange("p (n q) -> p n q", q=SB),
                           seq_of[:, :].unsqueeze(1).broadcast_to((T, NP, SB))).then_inc(v_mask, 1)
            ve.tensor_scalar(mean_of[:, :], seq_of[:, :], 1.0 / NP, None, ALU.mult).then_inc(v_mask, 1)
            dve.wait_ge(v_mask, 4)
            dve.wait_ge(p_idle, 1)
            dve.wait_ge(p_mask, 8)
            for r in range(PL // 2):
                dve.wait_ge(a_wt, r + 1)
                ve.tensor_tensor(WT[:, 2 * r:2 * r + 2, DM:2 * DM],
                                 bank[2 + r % 4][:, 0:2 * DM].rearrange("p (t d) -> p t d", t=2),
                                 WT[:, 2 * r:2 * r + 2, 0:DM].bitcast(F32), ALU.subtract).then_inc(v_wt, 1)
            def low(k, j):
                for h in range(2):
                    dve.wait_ge(a_xh, 2 * k + h + 1)
                    need(dve, t_emb, k - 1)
                    ve.tensor_tensor(xTl[:, j, h * 512:(h + 1) * 512], bT[h][:, :],
                                     xTh[:, j, h * 512:(h + 1) * 512].bitcast(F32), ALU.subtract)\
                      .then_inc(v_xl, 1)

            def embed_a(k, j):
                st = Steps(dve, v_emb, EMB, k)
                dve.wait_ge(t_emb, k + 1)
                need(dve, p_ln, LNP * (k - 2) + LNP_RS0)
                st.then(ve.tensor_tensor(emb[:, j, :], bE[0:T, DM:2 * DM], tokb[:, :], ALU.add))
                st.then(ve.tensor_tensor(emb[:, j, :], bE[0:T, 0:DM], emb[:, j, :], ALU.add))
                st.did(ve.bn_stats(st0[:, j, :], emb[:, j, :]))
                st.settle()
                apart(dve)
                st.did(ve.bn_aggr(mv0[:, j, :], st0[:, j, :]))

            def norm_a(k, j):
                st = Steps(dve, v_ln, VLN, k)
                dve.wait_ge(p_ln, LNP * k + LNP_RS0)
                need(dve, p_ln, LNP * (k - 2) + LNP_SKIP)
                st.did(ve.tensor_scalar(h0[:, j, :], emb[:, j, :], mv0[:, j, 0:1], rs0[:, j, 1:2],
                                        ALU.subtract, ALU.mult))
                assert st.n == VLN_H0

            def statistics_b(k, j):
                st = Steps(dve, v_ln, VLN, k)
                st.n = VLN_H0
                dve.wait_ge(p_ln, LNP * k + LNP_H0)
                st.did(ve.bn_stats(st1[:, j, :], h0[:, j, :]))
                st.settle()
                apart(dve)
                st.did(ve.bn_aggr(mv1[:, j, :], st1[:, j, :]))
                assert st.n == VLN_STAT

            def norm_b(k, j, g):
                st = Steps(dve, v_ln, VLN, k)
                st.n = VLN_STAT
                dve.wait_ge(p_ln, LNP * k + LNP_RS1)
                need(dve, t_xn, g)
                st.did(ve.tensor_scalar(xc[:, j, :], h0[:, j, :], mv1[:, j, 0:1], rs1[:, j, 3:4],
                                        ALU.subtract, ALU.mult))
                st.did(ve.tensor_scalar(an[:, j, :], h0[:, j, :], mv1[:, j, 0:1], rs1[:, j, 2:3],
                                        ALU.subtract, ALU.mult))

            def mixing_a(u):
                st = Steps(dve, v_mix, 4, u)
                dve.wait_ge(t_sd, 4 * u + 1)
                need(dve, p_mix, u)
                st.did(ve.tensor_tensor(score[:, :, :], bX[0:T, 0:T2].rearrange("p (u t) -> p u t", u=2),
                                        same[:, :].unsqueeze(1).broadcast_to((T, 2, T)), ALU.mult))
                dve.wait_ge(t_sd, 4 * u + 2)
                st.then(ve.tensor_tensor(fade[:, :, :],
                                         bY[1][0:T, 0:2 * H * NP].rearrange("p (a t) -> p a t", t=NP),
                                         later[:, :].unsqueeze(1).broadcast_to((T, 2 * H, NP)), ALU.mult))
                dve.wait_ge(p_dt, 2 * u + 1)
                st.did(ve.tensor_tensor_scan(prod[:, :, :].rearrange("p a t -> p (a t)"),
                                              fade[:, :, :].rearrange("p a t -> p (a t)"),
                                              dteye[:, :, :].rearrange("p a t -> p (a t)"), 0.0,
                                              ALU.mult, ALU.add))

            def mixing_b(u):
                st = Steps(dve, v_mix, 4, u)
                st.n = 3
                st.settle()
                need(dve, t_y, 2 * u)
                st.did(ve.tensor_tensor(
                    mix[:, 0, :, :].rearrange("p h (n q) -> p h n q", q=SB),
                    score[:, 0, :].rearrange("p (n q) -> p n q", q=SB).unsqueeze(1)
                    .broadcast_to((T, H, NP, SB)),
                    prod[:, 0:H, :].unsqueeze(3).broadcast_to((T, H, NP, SB)), ALU.mult))

            def low_x(q):
                dve.wait_ge(a_xn, 3 * q + 3)
                need(dve, t_in, NCH * q)
                ve.tensor_tensor(xnl[:, :, :], xnf[:, :, :], xnh[:, :, :].bitcast(F32), ALU.subtract)\
                  .then_inc(v_xn, 1)

            def average(u):
                dve.wait_ge(t_mean, u + 1)
                ve.tensor_copy(means[:, :, ds(2 * SB * u, 2 * SB)],
                               bX[0:DH, 0:4 * SB].rearrange("p (c s) -> p c s", c=2))\
                  .then_inc(v_mean, 1)

            def gating_y(u):
                st = Steps(dve, v_gate, 4, u)
                need(dve, t_out, u)
                need(dve, a_sq, u)
                for c in range(NC):
                    dve.wait_ge(t_y, 2 * u + (1 if c < 2 else 2))
                    y = bY[0][:, c * T2:(c + 1) * T2] if c < 2 else bY[1][:, 0:T2]
                    st.did(ve.scalar_tensor_tensor(gated[:, c, :], xs[:, c, :], Dc[:, c:c + 1], y,
                                                   ALU.mult, ALU.add))

            def gating_z(u):
                st = Steps(dve, v_gate, 4, u)
                st.n = NC
                st.settle()
                dve.wait_ge(a_z, NC * u + NC)
                st.did(ve.tensor_tensor(gated[:, :, :], gated[:, :, :], zs[:, :, :], ALU.mult))

            def step_sizes(q):
                dve.wait_ge(t_dt, q + 1)
                need(dve, a_dt, 3 * q)
                need(dve, v_sp, SP * q)
                ve.tensor_tensor(dtv[:, :, :], bX[0:T, 2 * T2:2 * T2 + 2 * H].rearrange("p (u h) -> p u h", h=H),
                                 dtb[:, :].unsqueeze(1).broadcast_to((T, 2, H)), ALU.add).then_inc(v_dtv, 1)

            def softplus(q, n):
                st = Steps(dve, v_sp, SP, q)
                st.n = n
                u, w, rc, s, s2, p, lp, rl = (dtw[:, i, :] for i in range(1, 9))
                terms = len(LOG1P_TERMS)
                if n == 0:
                    dve.wait_ge(a_dt, 3 * q + 2)
                    st.did(ve.tensor_scalar(w, u, 2.0, None, ALU.add))
                    return
                st.settle()
                if n == 1:
                    st.did(ve.reciprocal(rc, w))
                elif n == 2:
                    st.did(ve.tensor_tensor(s, u, rc, ALU.mult))
                elif n == 3:
                    st.did(ve.tensor_tensor(s2, s, s, ALU.mult))
                elif n == 4:
                    st.did(ve.tensor_scalar(p, s2, LOG1P_TERMS[0], None, ALU.mult))
                elif n < 4 + terms:
                    st.did(ve.scalar_tensor_tensor(p, p, LOG1P_TERMS[n - 4], s2, ALU.add, ALU.mult))
                elif n == 4 + terms:
                    st.did(ve.scalar_tensor_tensor(lp, p, 1.0, s, ALU.add, ALU.mult))
                elif n == 5 + terms:
                    st.did(ve.tensor_scalar(rl, dtv[:, :, :].rearrange("p u h -> p (u h)"), 0.0, None, ALU.max))
                elif n == 6 + terms:
                    need(dve, p_dt, 2 * (q - 1) + 1)
                    st.did(ve.scalar_tensor_tensor(dt[:, :], lp, 2.0, rl, ALU.mult, ALU.add))
                    assert st.n == SP_DT
                elif n == 7 + terms:
                    st.did(ve.tensor_tensor(dtA[:, :, :], dt[:, :].rearrange("p (u h) -> p u h", u=2),
                                            rate[:, :].unsqueeze(1).broadcast_to((T, 2, H)), ALU.mult))
                else:
                    st.did(ve.tensor_scalar(dtA[:, :, :], dtA[:, :, :], DECAY_MAX / RATE_UNIT, None, ALU.min))

            def convolve(q, i):
                st = Steps(dve, v_cv, 3 * CH, q)
                st.n = 3 * i
                a = acc[:, i, :].rearrange("p (j t) -> p j t", t=T)
                p = taps[:, i, :].rearrange("p (j t) -> p j t", t=T)
                dve.wait_ge(a_cv, 2 * CH * q + 2 * (i + 1))
                for back in (1, 2, 3):
                    if back > 1:
                        st.settle()
                    st.did(ve.scalar_tensor_tensor(
                        a[:, :, back * SB:T], p[:, :, 0:T - back * SB], cw[:, i, TAPS - 1 - back:TAPS - back],
                        a[:, :, back * SB:T], ALU.mult, ALU.add))
                    softplus(q, 3 * i + back - 1)

            def mean_square(u):
                st = Steps(dve, v_o, OV, u)
                dve.wait_ge(t_out, u + 1)
                need(dve, p_o, PO * (u - 1) + PO_RR)
                st.did(ve.tensor_scalar(msq[:, :], bP[0][0:T, 2 * DM:2 * DM + 2], 1.0 / DI, EPS,
                                        ALU.mult, ALU.add))

            def mixed_rows(u):
                st = Steps(dve, v_o, OV, u)
                st.n = OV_MS
                dve.wait_ge(p_o, PO * u + PO_RR)
                need(dve, c_hid, 32 * u)
                for j in range(2):
                    st.did(ve.scalar_tensor_tensor(
                        hrow[:, j:j + 1, 0:DM],
                        bP[0][0:T, j * DM:(j + 1) * DM].rearrange("p (a d) -> p a d", a=1),
                        rrms[:, j:j + 1], skip[:, ds(2 * u + j, 1), :], ALU.mult, ALU.add))
                st.settle()
                for j in range(2):
                    st.did(ve.bn_stats(st2[:, j, :], hrow[:, j, 0:DM]))
                st.settle()
                apart(dve)
                for j in range(2):
                    st.did(ve.bn_aggr(mv2[:, j, :], st2[:, j, :]))
                st.settle()
                st.did(ve.tensor_copy(hrow[:, :, DM], mv2[:, :, 0]))
                assert st.n == OV_STAT

            def normed_rows(u):
                st = Steps(dve, v_o, OV, u)
                st.n = OV_STAT
                dve.wait_ge(p_o, PO * u + PO_R)
                need(dve, t_mean, u)
                for j in range(2):
                    st.did(ve.tensor_scalar(bn[:, j, :], hrow[:, j, 0:DM], hrow[:, j, DM:DM + 1],
                                            hrow[:, j, DM + 1:DM + 2], ALU.subtract, ALU.mult))

            def body(g):
                if live(g - 3):
                    mean_square(g - 3)
                if live(g - 1):
                    statistics_b(2 * (g - 1) + 1, 1)
                if live(g - 2):
                    mixing_a(g - 2)
                if live(g - 1):
                    norm_b(2 * (g - 1) + 1, 1, g - 1)
                if live(g - 2):
                    mixing_b(g - 2)
                if live(g):
                    low(2 * g + 1, 1)
                if live(g - 3):
                    mixed_rows(g - 3)
                if live(g):
                    embed_a(2 * g, 0)
                if live(g - 1):
                    low_x(g - 1)
                if live(g - 2):
                    gating_y(g - 2)
                if live(g - 1):
                    step_sizes(g - 1)
                if live(g - 3):
                    normed_rows(g - 3)
                if live(g + 1):
                    low(2 * g + 2, 0)
                if live(g):
                    norm_a(2 * g, 0)
                if live(g - 1):
                    convolve(g - 1, 0)
                if live(g - 2):
                    gating_z(g - 2)
                if live(g):
                    statistics_b(2 * g, 0)
                if live(g - 1):
                    convolve(g - 1, 1)
                if live(g):
                    norm_b(2 * g, 0, g)
                if live(g - 1):
                    convolve(g - 1, 2)
                    convolve(g - 1, 3)
                    for n in range(3 * CH, SP):
                        softplus(g - 1, n)
                if live(g - 3):
                    average(g - 3)
                if live(g):
                    embed_a(2 * g + 1, 1)
                    norm_a(2 * g + 1, 1)

            low(0, 0)
            dve.wait_ge(a_wi, 1)
            ve.tensor_tensor(WIl[:, :, :], wiraw[:, :, :], WIh[:, :, :].bitcast(F32), ALU.subtract)\
              .then_inc(v_wi, 1)
            dve.wait_ge(c_const, 16 * CONSTS)
            ve.tensor_scalar(alogc[:, :], alog[:, :], LOG_MAX, None, ALU.min).then_inc(v_alog, 1)
            for c in range(NC):
                ve.tensor_scalar(WO[:, c, :], woraw[:, c, :], rmsw[:, c:c + 1], None, ALU.mult)\
                  .then_inc(v_wo, 1)
            dve.wait_ge(a_expa, 1)
            ve.tensor_scalar(rate[:, :], expa[:, :], 1.0 / RATE_UNIT, None, ALU.mult).then_inc(v_wo, 1)
            raw_weights_read(dve)
            bodies(dve, body, 4, NG - 1, NG + 2)
            stage_two_dve(dve)

        @block.tensor
        def _(pe):
            te = nc.tensor
            pe.wait_ge(p_ident, 2)
            pe.wait_ge(c_wt, 16)
            for r in range(PL // 2):
                need(pe, v_wt, r - 3)
                for t in range(2):
                    for c in range(2):
                        last = te.transpose(bank[2 + r % 4][:, (2 * t + c) * DH:(2 * t + c + 1) * DH],
                                            wtraw[:, c, :].rearrange("p (f t) -> p t f", t=PL)[:, 2 * r + t, :],
                                            ident[0:DH, 0:DH])
                last.then_inc(t_wt, 1)

            def turn_x(k, j, g):
                pe.wait_ge(c_x[j], 16 * (g + 1))
                for h in range(2):
                    need(pe, v_xl, 2 * (k - 1) + h + 1)
                    for r in range(4):
                        last = te.transpose(bT[h][:, r * 128:(r + 1) * 128],
                                            xraw[:, j, (4 * h + r) * F:(4 * h + r + 1) * F], ident[:, :])
                    last.then_inc(t_x, 1)

            def embed(k, j, taps=(0, PL)):
                if isinstance(k, int) and k == 0:
                    pe.wait_ge(v_wt, PL // 2)
                if taps[0] == 0:
                    pe.wait_ge(v_xl, 2 * k + 2)
                    need(pe, v_emb, EMB * (k - 1) + EMB_READ)
                hi = xTh[:, j, :].rearrange("p (r s) -> p r s", s=128)
                lo = xTl[:, j, :].rearrange("p (r s) -> p r s", s=128)
                for t in range(*taps):
                    w = slice(t // ST * SB, t // ST * SB + T)
                    if t > 0:
                        te.matmul(bE[0:T, DM:2 * DM], lo[:, t % ST, w], WT[:, t, 0:DM],
                                  start=False, stop=False, skip_group_check=True)
                    last = te.matmul(bE[0:T, 0:2 * DM], hi[:, t % ST, w], WT[:, t, :],
                                     start=(t == 0), stop=(t == PL - 1), skip_group_check=True)
                    if t == 0:
                        te.matmul(bE[0:T, DM:2 * DM], lo[:, t % ST, w], WT[:, t, 0:DM],
                                  start=False, stop=False, skip_group_check=True)
                if taps[1] == PL:
                    last.then_inc(t_emb, 1)

            def turn_norms(q):
                pe.wait_ge(v_ln, VLN * (2 * q + 1) + VLN_XC)
                need(pe, v_mix, 4 * (q - 1) + 1)
                need(pe, v_dtv, q)
                for j in range(2):
                    for c in range(2):
                        last = te.transpose(bX[0:DH, c * T2 + j * T:c * T2 + (j + 1) * T],
                                            xc[:, j, c * DH:(c + 1) * DH], ident[0:T, 0:T])
                last.then_inc(t_xn, 1)

            def step_size_inputs(q):
                if isinstance(q, int) and q == 0:
                    pe.wait_ge(a_wi, 2)
                    pe.wait_ge(v_wi, 1)
                pe.wait_ge(a_xn, 3 * q + 3)
                for j in range(2):
                    for c in range(2):
                        last = te.matmul(bX[0:T, 2 * T2 + j * H:2 * T2 + (j + 1) * H],
                                         xnf[:, c, j * T:(j + 1) * T], WDT[:, c, :],
                                         start=(c == 0), stop=(c == 1))
                last.then_inc(t_dt, 1)

            def project(q, chunks):
                pe.wait_ge(v_xn, q + 1)
                cols = [2 * DI] + [DI + 128 * i for i in range(NC)] + [128 * i for i in range(NC)]
                for i in chunks:
                    col = cols[i]
                    if i == 0:
                        need(pe, v_o, OV * (q - 2) + 3)
                    elif i == 1:
                        need(pe, a_xt, 2 * (q - 1) + 1)
                    elif i < CH or i == CH + 2:
                        pe.wait_ge(a_cv, 2 * CH * q + 2 * ((2 if i > CH else i - 2) + 1))
                    else:
                        need(pe, v_gate, 4 * (q - 1) + 3)
                    n = 0
                    for c in range(2):
                        for w, a in ((WIh, xnh), (WIh, xnl), (WIl, xnh)):
                            last = te.matmul(bIn[i][:, 0:T2], w[:, c, col:col + 128], a[:, c, :],
                                             start=(n == 0), stop=(n == 5))
                            n += 1
                    last.then_inc(t_in, 1)

            def prepare(u):
                pe.wait_ge(c_C, 16 * (u + 1))
                pe.wait_ge(v_dtv, u + 1)
                need(pe, v_mean, u - 1)
                for j in range(2):
                    last = te.matmul(bX[0:T, j * T:(j + 1) * T], BC[0:NS, j * T:(j + 1) * T],
                                     CT[:, j * T:(j + 1) * T], start=True, stop=True)
                last.then_inc(t_sd, 1)
                if isinstance(u, int) and u == 0:
                    pe.wait_ge(v_mask, 4)
                pe.wait_ge(p_dt, 2 * u + 2)
                need(pe, v_gate, 4 * (u - 1) + 3)
                te.matmul(bY[1][0:T, 0:2 * H * NP], same[:, :],
                          deceye[:, :, :].rearrange("p a t -> p (a t)"), start=True, stop=True)\
                  .then_inc(t_sd, 1)
                pe.wait_ge(a_si, CH * u + CH)
                pe.wait_ge(a_z, NC * u + 2)
                for j, b in enumerate((bP[1], bY[0])):
                    for c in range(NC):
                        last = te.transpose(b[0:T, c * 128:(c + 1) * 128], xs[:, c, j * T:(j + 1) * T],
                                            ident[:, :])
                    last.then_inc(t_sd, 1)

            def blend(u):
                pe.wait_ge(v_mix, 4 * u + 4)
                pe.wait_ge(p_mix, u + 1)
                pe.wait_ge(a_xt, 2 * u + 2)
                for c in range(NC):
                    y = bY[0][:, c * T2:(c + 1) * T2] if c < 2 else bY[1][:, 0:T2]
                    for j in range(2):
                        for half in range(2):
                            h = 2 * c + half
                            last = te.matmul(y[half * HD:(half + 1) * HD, j * T:(j + 1) * T],
                                             xtok[:, j, h * HD:(h + 1) * HD], mix[:, j, h, :],
                                             start=True, stop=True)
                    if c > 0:
                        last.then_inc(t_y, 1)

            def average(u):
                if isinstance(u, int) and u == 0:
                    pe.wait_ge(v_mask, 4)
                pe.wait_ge(v_o, OV * u + OV)
                pe.wait_ge(v_dtv, min(u + 3, NG) if isinstance(u, int) else u + 3)
                need(pe, v_mean, u)
                for j in range(2):
                    for c in range(2):
                        col = c * 2 * SB + j * SB
                        last = te.matmul(bX[0:DH, col:col + SB], bn[:, j, c * DH:(c + 1) * DH],
                                         mean_of[:, :], start=True, stop=True)
                last.then_inc(t_mean, 1)

            def emit(u):
                if isinstance(u, int) and u == 0:
                    pe.wait_ge(v_wo, NC + 1)
                pe.wait_ge(a_sq, u + 1)
                for j in range(2):
                    for c in range(NC):
                        te.matmul(bP[0][0:T, j * DM:(j + 1) * DM], gated[:, c, j * T:(j + 1) * T], WO[:, c, :],
                                  start=(c == 0), stop=(c == NC - 1))
                for j in range(2):
                    for c in range(NC):
                        last = te.matmul(bP[0][0:T, 2 * DM + j:2 * DM + j + 1], gsq[:, c, j * T:(j + 1) * T],
                                         ones[:, 0:1], start=(c == 0), stop=(c == NC - 1))
                last.then_inc(t_out, 1)

            def body(g):
                if live(g - 2):
                    prepare(g - 2)
                if live(g):
                    embed(2 * g, 0)
                if live(g - 1):
                    turn_norms(g - 1)
                if live(g + 1):
                    turn_x(2 * g + 2, 0, g + 1)
                if live(g - 2):
                    blend(g - 2)
                if live(g - 1):
                    step_size_inputs(g - 1)
                    project(g - 1, (0, 1))
                if live(g):
                    embed(2 * g + 1, 1, (0, 6))
                if live(g - 1):
                    project(g - 1, (2, 3))
                if live(g - 3):
                    average(g - 3)
                if live(g):
                    embed(2 * g + 1, 1, (6, 11))
                if live(g - 1):
                    project(g - 1, (4, 5, 6))
                if live(g):
                    embed(2 * g + 1, 1, (11, PL))
                if live(g - 2):
                    pe.wait_ge(a_z, NC * (min(g, NG) if isinstance(g, int) else g))
                if live(g - 2):
                    emit(g - 2)
                if live(g + 1):
                    turn_x(2 * g + 3, 1, g + 1)

            turn_x(0, 0, 0)
            turn_x(1, 1, 0)
            bodies(pe, body, 4, NG - 1, NG + 2)
            stage_two_pe(pe)


_INS = ['x', 'L0_tok_W', 'L0_tok_b', 'L0_tok_gamma', 'L0_tok_beta', 'L0_attn_ln_w', 'L0_attn_ln_b',
        'L0_attn_W_in', 'L0_attn_conv_w', 'L0_attn_conv_b', 'L0_attn_dt_bias', 'L0_attn_A_log', 'L0_attn_D',
        'L0_attn_rms_w', 'L0_attn_W_out', 'L0_ffn_Wg', 'L0_ffn_W1', 'L0_ffn_b1', 'L0_ffn_W2', 'L0_ffn_b2']


def kernel(**inputs):
    import numpy as _np
    import concourse.bacc as _bacc
    from concourse import mybir as _mybir
    from concourse.bass_utils import run_bass_kernel_spmd as _run

    nc = _bacc.Bacc("TRN2", target_bir_lowering=False, num_devices=1)
    arrays, args = {}, []
    for name in _INS:
        a = _np.ascontiguousarray(inputs[name])
        arrays[f"in_{name}"] = a
        args.append(nc.dram_tensor(f"in_{name}", a.shape, _mybir.dt.from_np(a.dtype), kind="ExternalInput").ap())
    nseq, samples, _ = inputs['x'].shape
    width = inputs['L0_tok_W'].shape[0]
    shape = (nseq, (samples - 16) // 8 + 1, width)
    args.append(nc.dram_tensor("out_0", shape, _mybir.dt.float32, kind="ExternalOutput").ap())
    audio_tower(nc, *args)
    r = _run(nc, [arrays], core_ids=[0])
    return r.results[0]["out_0"]
```

```python
from contextlib import ExitStack

import concourse.bass as bass
from concourse import mybir

F32 = mybir.dt.float32
F32R = mybir.dt.float32r
I32 = mybir.dt.int32
U32 = mybir.dt.uint32
ALU = mybir.AluOpType
ACT = mybir.ActivationFunctionType
AX = mybir.AxisListType
ds = bass.ds

EPS = 1e-5
LOG_MAX = 88.6
RATE_UNIT = 2.0 ** 64
DECAY_MAX = 1024.0
LOG1P_TERMS = [1 / 13, 1 / 11, 1 / 9, 1 / 7, 1 / 5, 1 / 3]


def need(eng, s, n):
    if isinstance(n, int) and n <= 0:
        return
    eng.wait_ge(s, n)


class Steps:

    def __init__(self, eng, s, per, index):
        self.eng, self.s, self.per, self.base, self.n = eng, s, per, index * per, 0

    def did(self, ins):
        self.n += 1
        assert self.n <= self.per
        ins.then_inc(self.s, 1)

    def settle(self):
        self.eng.wait_ge(self.s, self.base + self.n)

    def then(self, ins):
        self.did(ins)
        self.settle()


def audio_tower(nc, x, tok_W, tok_b, tok_gamma, tok_beta, ln_w, ln_b, W_in, conv_w, conv_b, dt_bias,
                A_log, D, rms_w, W_out, Wg, W1, b1, W2, b2, out):
    NSEQ, S, F = x.shape
    DM, KP = tok_W.shape
    PL = KP // F
    ST = PL // 2
    NP = (S - PL) // ST + 1
    BLK = S // ST
    SB = 128 // BLK
    T = SB * NP
    NG = NSEQ // (2 * SB)
    T2 = 2 * T
    DH = DM // 2
    DI = W_out.shape[0]
    NC = DI // 128
    H = D.shape[0]
    HD = DI // H
    NS = (conv_w.shape[0] - DI) // 2
    WI = W_in.shape[1]
    TAPS = conv_w.shape[1]
    NE, _, FF = W1.shape
    FC = FF // 128
    FH = FF // 2
    NTOK = NSEQ * NP
    NT = NSEQ // SB + NE - 1
    SLOTS = NT * SB
    ROW = DM + 2
    MISS = 4096
    CH = NC + 1
    NCH = CH + NC
    assert F == 128 and BLK * SB == 128 and 2 * NS == 128 and H == 2 * NC and HD == 64
    assert MISS > NTOK and NT % 2 == 0 and TAPS == 4

    hid = nc.dram_tensor("hid", (NTOK, ROW), F32, kind="Internal").ap()
    out_rows = out.rearrange("b n d -> (b n) d")

    ctx = ExitStack()
    with ctx:
        def sb(name, shape, dt=F32, stack=ctx):
            return stack.enter_context(nc.sbuf_tensor(name, shape, dt))

        def sem(name):
            return ctx.enter_context(nc.semaphore(name))

        bank = [ctx.enter_context(nc.psum_tensor(f"bank{i}", [128, 512], F32)) for i in range(8)]

        ident = sb("ident", [128, 128])
        same = sb("same", [T, T])
        eye = sb("eye", [T, NP])
        later = sb("later", [T, NP])
        seq_of = sb("seq_of", [T, SB])
        mean_of = sb("mean_of", [T, SB])
        ones = sb("ones", [128, 128])
        idle = sb("idle", [1, 2])
        neg_half = sb("neg_half", [128, 2])
        eps = sb("eps", [128, 2])
        minus_one = sb("minus_one", [128, 1])
        var_k = sb("var_k", [128, 2])
        var_c = sb("var_c", [128, 2])
        WDT = sb("WDT", [DH, 2, H])
        tokb = sb("tokb", [T, DM])
        gamma = sb("gamma", [T, DM])
        beta = sb("beta", [T, DM])
        dtb = sb("dtb", [T, H])
        alog = sb("alog", [T, H])
        expa = sb("expa", [T, H])
        alogc = sb("alogc", [T, H])
        rate = sb("rate", [T, H])
        lnw = sb("lnw", [DH, 2])
        lnb = sb("lnb", [DH, 2])
        cw = sb("cw", [128, CH, TAPS])
        cb = sb("cb", [128, CH])
        Dc = sb("Dc", [128, NC])
        rmsw = sb("rmsw", [128, NC])
        WO = sb("WO", [128, NC, DM])
        WT = sb("WT", [128, PL, 2 * DM], F32R)
        WIh = sb("WIh", [DH, 2, WI], F32R)
        WIl = sb("WIl", [DH, 2, WI], F32R)
        W1h = sb("W1h", [DH + 1, NE * 2 * FF], F32R)
        W1l = sb("W1l", [DH + 1, NE * 2 * FF], F32R)
        W2s = sb("W2s", [128, NE * FC, 2 * DM], F32R)
        w1raw = sb("w1raw", [DH + 1, FF])
        w2raw = sb("w2raw", [128, FC // 2, DM])
        WgT = sb("WgT", [DH, 2, NE])
        skip = sb("skip", [T, 2 * NG, DM])
        means = sb("means", [DH, 2, NSEQ])

        tri = sb("tri", [NSEQ, NSEQ])
        k4 = sb("k4", [NSEQ, NSEQ // SB])
        rank = sb("rank", [NSEQ, NE])
        iota_s = sb("iota_s", [NSEQ, SLOTS])
        iota_t = sb("iota_t", [T, NP])
        rowid = sb("rowid", [NSEQ, T])

        neg_logit = sb("neg_logit", [NSEQ, NE])
        score_exp = sb("score_exp", [NSEQ, NE])
        expert_score = sb("expert_score", [NSEQ, NE])
        neg_max = sb("neg_max", [NSEQ, 1])
        exp_sum = sb("exp_sum", [NSEQ, 1])
        exp_sum_inv = sb("exp_sum_inv", [NSEQ, 1])
        weight = sb("weight", [NSEQ, 1])
        best_rank = sb("best_rank", [NSEQ, 1])
        slot_no = sb("slot_no", [NSEQ, 1])
        ranked = sb("ranked", [NSEQ, NE])
        choice = sb("choice", [NSEQ, NE])
        n_tiles = sb("n_tiles", [NSEQ, NE])
        first_tile = sb("first_tile", [NSEQ, NE])
        place = sb("place", [NSEQ, NE])
        own_place = sb("own_place", [NSEQ, NE])
        over = sb("over", [NSEQ, NE, NSEQ // SB])
        tpos = sb("tpos", [T, NP])
        tcol = sb("tcol", [T, 2])
        slot = sb("slot", [NSEQ, SLOTS])
        wcol = sb("wcol", [NSEQ, T])
        pick = sb("pick", [T, NT, SB])
        pickw = sb("pickw", [T, NT, SB])
        idf = sb("idf", [T, NT])
        idx = sb("idx", [T, NT], U32)
        wt = sb("wt", [T, NT])
        tile_expert = sb("tile_expert", [NSEQ, NT])
        ei = sb("ei", [NSEQ, NT], I32)

        one = ExitStack()
        xraw = sb("xraw", [128, 2, ST * F], stack=one)
        xTh = sb("xTh", [128, 2, ST * 128], F32R, one)
        xTl = sb("xTl", [128, 2, ST * 128], F32R, one)
        raw = ExitStack()
        wtraw = sb("wtraw", [DH, 2, KP], stack=raw)
        wiraw = sb("wiraw", [DH, 2, WI], stack=raw)
        woraw = sb("woraw", [128, NC, DM], stack=raw)
        raw.close()
        emb = sb("emb", [T, 2, DM], stack=one)
        h0 = sb("h0", [T, 2, DM], stack=one)
        xc = sb("xc", [T, 2, DM], stack=one)
        st0 = sb("st0", [T, 2, 6], stack=one)
        mv0 = sb("mv0", [T, 2, 2], stack=one)
        st1 = sb("st1", [T, 2, 6], stack=one)
        mv1 = sb("mv1", [T, 2, 2], stack=one)
        rs0 = sb("rs0", [T, 2, 2], stack=one)
        rs1 = sb("rs1", [T, 2, 6], stack=one)
        xnf = sb("xnf", [DH, 2, T2], stack=one)
        xnh = sb("xnh", [DH, 2, T2], F32R, one)
        xnl = sb("xnl", [DH, 2, T2], F32R, one)
        taps = sb("taps", [128, CH, T2], stack=one)
        acc = sb("acc", [128, CH, T2], stack=one)
        xs = sb("xs", [128, NC, T2], stack=one)
        zs = sb("zs", [128, NC, T2], stack=one)
        BC = sb("BC", [128, T2], stack=one)
        CT = sb("CT", [NS, T2], stack=one)
        dtv = sb("dtv", [T, 2, H], stack=one)
        dtw = sb("dtw", [T, 9, 2 * H], stack=one)
        dt = sb("dt", [T, 2 * H], stack=one)
        dtA = sb("dtA", [T, 2, H], stack=one)
        dec = sb("dec", [T, 2 * H], stack=one)
        dteye = sb("dteye", [T, 2 * H, NP], stack=one)
        deceye = sb("deceye", [T, 2 * H, NP], stack=one)
        fade = sb("fade", [T, 2 * H, NP], stack=one)
        prod = sb("prod", [T, 2 * H, NP], stack=one)
        score = sb("score", [T, 2, T], stack=one)
        mix = sb("mix", [T, 2, H, T], stack=one)
        xtok = sb("xtok", [T, 2, DI], stack=one)
        gated = sb("gated", [128, NC, T2], stack=one)
        gsq = sb("gsq", [128, NC, T2], stack=one)
        msq = sb("msq", [T, 2], stack=one)
        rrms = sb("rrms", [T, 2], stack=one)
        hrow = sb("hrow", [T, 2, ROW], stack=one)
        st2 = sb("st2", [T, 2, 6], stack=one)
        mv2 = sb("mv2", [T, 2, 2], stack=one)
        var2 = sb("var2", [T, 2], stack=one)
        bn = sb("bn", [T, 2, DM], stack=one)
        one.close()

        b2c = sb("b2c", [T, NE * DM])
        rows = sb("rows", [T, 2, ROW])
        resid = sb("resid", [T, NT, DM])
        bb = sb("bb", [T, 2, DM])
        bTh = sb("bTh", [DH + 1, 2, 2 * T], F32R)
        bTl = sb("bTl", [DH + 1, 2, 2 * T], F32R)
        hg = sb("hg", [T, 2, FF])
        hTh = sb("hTh", [128, 2, FC * T], F32R)
        hTl = sb("hTl", [128, 2, FC * T], F32R)
        res = sb("res", [T, 2, DM])
        idg = sb("idg", [T, 2], U32)
        ids = sb("ids", [T, 2], U32)

        bT = (bank[0], bank[1])
        bE = bank[2]
        bX = bank[3]
        bP = (bank[4], bank[5])
        bY = (bank[6], bank[7])
        bIn = (bP[0], bP[1], bP[0], bP[1], bY[0], bY[1], bP[0])

        c_const = sem("c_const")
        c_wt = [sem("c_wt0"), sem("c_wt1")]
        c_wi = sem("c_wi")
        c_x = [sem("c_x0"), sem("c_x1")]
        c_C = sem("c_C")
        c_w1 = sem("c_w1")
        c_b2 = sem("c_b2")
        c_w2 = sem("c_w2")
        c_hid = sem("c_hid")
        p_ident = sem("p_ident")
        p_mask = sem("p_mask")
        p_idle = sem("p_idle")
        a_wi = sem("a_wi")
        v_wi = sem("v_wi")
        v_mask = sem("v_mask")
        a_expa = sem("a_expa")
        t_wt = sem("t_wt")
        a_wt = sem("a_wt")
        v_wt = sem("v_wt")
        v_alog = sem("v_alog")
        v_wo = sem("v_wo")
        t_x = sem("t_x")
        a_xh = sem("a_xh")
        v_xl = sem("v_xl")
        t_emb = sem("t_emb")
        v_emb = sem("v_emb")
        v_ln = [sem("v_ln0"), sem("v_ln1")]
        p_ln = [sem("p_ln0"), sem("p_ln1")]
        t_xn = sem("t_xn")
        a_xn = sem("a_xn")
        a_skip = sem("a_skip")
        v_xn = sem("v_xn")
        t_dt = sem("t_dt")
        v_dtv = sem("v_dtv")
        t_in = sem("t_in")
        a_cv = sem("a_cv")
        v_cv = sem("v_cv")
        a_si = sem("a_si")
        a_z = sem("a_z")
        a_dt = sem("a_dt")
        v_sp = sem("v_sp")
        p_dt = sem("p_dt")
        t_sd = sem("t_sd")
        a_xt = sem("a_xt")
        v_mix = sem("v_mix")
        p_mix = sem("p_mix")
        t_y = sem("t_y")
        v_gate = sem("v_gate")
        a_sq = sem("a_sq")
        t_out = sem("t_out")
        v_o = sem("v_o")
        p_o = sem("p_o")
        t_mean = sem("t_mean")
        v_mean = sem("v_mean")
        a_w1 = sem("a_w1")
        p_w1 = sem("p_w1")
        t_r = sem("t_r")
        v_r = sem("v_r")
        a_r = sem("a_r")
        p_clear = sem("p_clear")
        c_g = [sem("c_g0"), sem("c_g1")]
        c_s = [sem("c_s0"), sem("c_s1")]
        p_id = sem("p_id")
        p_is = sem("p_is")
        v_b = sem("v_b")
        t_b = sem("t_b")
        a_b = sem("a_b")
        v_bl = sem("v_bl")
        t_up = sem("t_up")
        a_gelu = sem("a_gelu")
        t_h = sem("t_h")
        a_hh = sem("a_hh")
        v_hl = sem("v_hl")
        t_dn = sem("t_dn")
        v_fin = sem("v_fin")

        EMB, EMB_READ, EMB_STAT = 4, 2, 4
        VLN, VLN_H0, VLN_STAT, VLN_XC = 4, 1, 3, 4
        LNP, LNP_RS0, LNP_H0, LNP_RS1, LNP_SKIP = 10, 2, 4, 7, 10
        SP, SP_DT = 15, 13
        OV, OV_MS, OV_STAT = 10, 1, 8
        PO, PO_RR, PO_R = 3, 1, 3
        CONSTS = 17
        PIECES = 2 * NE
        assert NG == PIECES + 2


        eB = bank[0]
        eU = (bank[1], bank[2])
        eH = (bank[3], bank[4])
        eD = (bank[5], bank[6])
        HT = FC // 2 * T
        R_SCORE, R_PICK, R_PLACE = 1, 2, 3
        VR_LOGIT = 3 + 2
        VR_CHOICE = VR_LOGIT + 6
        VR_PLACE = VR_CHOICE + NE + 7
        VR_TILE = VR_PLACE + NE
        VR_ROWS = VR_TILE + 4
        VR_ALL = VR_ROWS + 1

        def averages_done(eng):
            eng.wait_ge(t_mean, NG)
            eng.wait_ge(v_mean, NG)

        def stage_one_done(eng):
            eng.wait_ge(c_hid, 32 * NG)
            eng.wait_ge(t_mean, NG)
            eng.wait_ge(v_mean, NG)

        def tiles(eng, at, first):
            for s in range(first, 4):
                at(s, s % 2)
            with eng.Fori(0, (NT - 8) // 2) as m:
                at(2 * m + 4, 0)
                at(2 * m + 5, 1)
            for s in range(NT - 4, NT + 2):
                at(s, s % 2)

        def tile(i):
            return not isinstance(i, int) or 0 <= i < NT

        def left_by(i, per=1):
            return per * (i - 1)

        def turns(i, par):
            return (i - par) // 2

        def stage_two_pool(pool):
            gp = nc.gpsimd
            stage_one_done(pool)
            st = Steps(pool, p_clear, 3, 0)
            st.then(gp.memset(rows[:, :, :], 0.0))
            st.then(gp.memset(bTh[DH:DH + 1, :, T:2 * T].bitcast(F32), 1.0))
            st.then(gp.memset(bTl[DH:DH + 1, :, T:2 * T].bitcast(F32), 0.0))
            pool.wait_ge(v_r, VR_ROWS)

            def at(s, par):
                if tile(s + 3):
                    i, p = s + 3, (par + 1) % 2
                    need(pool, v_b, left_by(i, 2))
                    gp.tensor_copy(idg[:, p:p + 1], idx[:, ds(i, 1)]).then_inc(p_id, 1)
                    pool.wait_ge(p_id, i + 1)
                    apart(pool)
                    gp.indirect_dma_start(
                        out=rows[:, p, :], out_offset=None, in_=hid,
                        in_offset=bass.IndirectOffsetOnAxis(ap=idg[:, p:p + 1], axis=0),
                        bounds_check=NTOK - 1, oob_is_err=False).then_inc(c_g[p], 16)
                if tile(s - 2):
                    i, p = s - 2, par
                    need(pool, c_s[p], 16 * turns(i, p))
                    gp.tensor_copy(ids[:, p:p + 1], idx[:, ds(i, 1)]).then_inc(p_is, 1)
                    pool.wait_ge(p_is, i + 1)
                    pool.wait_ge(v_fin, 3 * i + 3)
                    apart(pool)
                    gp.indirect_dma_start(
                        out=out_rows, out_offset=bass.IndirectOffsetOnAxis(ap=ids[:, p:p + 1], axis=0),
                        in_=res[:, p, :], in_offset=None,
                        bounds_check=NTOK - 1, oob_is_err=False).then_inc(c_s[p], 16)

            tiles(pool, at, -3)

        def stage_two_act(act):
            ac = nc.scalar
            averages_done(act)
            act.wait_ge(v_r, VR_LOGIT)
            ac.activation(score_exp[:, :], neg_logit[:, :], ACT.Exp, bias=neg_max[:, :], scale=-1.0,
                          accum_out=exp_sum[:, :]).then_inc(a_r, 1)
            stage_one_done(act)

            def at(s, par):
                def gelu(f):
                    act.wait_ge(t_up, 2 * s + f + 1)
                    need(act, t_h, left_by(s, 2))
                    ac.activation(hg[:, par, f * FH:(f + 1) * FH], eU[f][0:T, 0:FH], ACT.Gelu)\
                      .then_inc(a_gelu, 1)

                if tile(s + 1):
                    i, p = s + 1, (par + 1) % 2
                    act.wait_ge(t_b, i + 1)
                    need(act, t_up, left_by(i, 2))
                    ac.activation(bTh[0:DH, p, :], eB[0:DH, 0:2 * T], ACT.Copy).then_inc(a_b, 1)
                if tile(s):
                    gelu(0)
                if tile(s - 1):
                    i, p = s - 1, (par + 1) % 2
                    for f in range(2):
                        act.wait_ge(t_h, 2 * i + f + 1)
                        need(act, t_dn, left_by(i))
                        ac.activation(hTh[:, p, f * HT:(f + 1) * HT], eH[f][:, 0:HT], ACT.Copy)\
                          .then_inc(a_hh, 1)
                if tile(s):
                    gelu(1)

            tiles(act, at, -1)

        def stage_two_dve(dve):
            ve = nc.vector
            averages_done(dve)
            dve.wait_ge(p_mask, 15)
            st = Steps(dve, v_r, VR_ALL, 0)
            st.then(ve.tensor_tensor(tpos[:, :], iota_t[:, :], eye[:, :], ALU.mult))
            st.then(ve.tensor_reduce(tcol[:, 0:1], tpos[:, :], AX.X, ALU.add))
            st.did(ve.tensor_scalar(tcol[:, 1:2], tcol[:, 0:1], float(MISS), None, ALU.add))
            dve.wait_ge(t_r, R_SCORE)
            st.then(ve.tensor_scalar(neg_logit[:, :], bank[3][0:NSEQ, 0:NE], -1.0, None, ALU.mult))
            st.did(ve.tensor_reduce(neg_max[:, :], neg_logit[:, :], AX.X, ALU.min))
            assert st.n == VR_LOGIT
            dve.wait_ge(a_r, 1)
            st.then(ve.reciprocal(exp_sum_inv[:, :], exp_sum[:, :]))
            st.then(ve.tensor_scalar(expert_score[:, :], score_exp[:, :], exp_sum_inv[:, :], None, ALU.mult))
            st.then(ve.tensor_reduce(weight[:, :], expert_score[:, :], AX.X, ALU.max))
            st.then(ve.scalar_tensor_tensor(ranked[:, :], expert_score[:, :], weight[:, :], rank[:, :],
                                            ALU.is_ge, ALU.mult))
            st.then(ve.tensor_reduce(best_rank[:, :], ranked[:, :], AX.X, ALU.max))
            st.did(ve.tensor_scalar(choice[:, :], ranked[:, :], best_rank[:, :], None, ALU.is_equal))
            assert st.n == VR_CHOICE
            st.did(ve.tensor_scalar(wcol[:, :], ones[0:NSEQ, 0:T], weight[:, :], None, ALU.mult))
            dve.wait_ge(t_r, R_PICK)
            st.then(ve.tensor_tensor(over[:, :, :],
                                     bank[3][0:NSEQ, 16:16 + NE].unsqueeze(2)
                                     .broadcast_to((NSEQ, NE, NSEQ // SB)),
                                     k4[:, :].unsqueeze(1).broadcast_to((NSEQ, NE, NSEQ // SB)), ALU.is_gt))
            st.did(ve.tensor_reduce(n_tiles[:, :], over[:, :, :], AX.X, ALU.add))
            st.then(ve.memset(first_tile[:, 0:1], 0.0))
            for e in range(1, NE):
                st.then(ve.tensor_tensor(first_tile[:, e:e + 1], first_tile[:, e - 1:e], n_tiles[:, e - 1:e],
                                         ALU.add))
            st.then(ve.scalar_tensor_tensor(place[:, :], first_tile[:, :], float(SB),
                                            bank[3][0:NSEQ, 8:8 + NE], ALU.mult, ALU.add))
            st.then(ve.tensor_tensor(own_place[:, :], place[:, :], choice[:, :], ALU.mult))
            st.then(ve.tensor_reduce(slot_no[:, :], own_place[:, :], AX.X, ALU.add))
            st.did(ve.tensor_scalar(slot[:, :], iota_s[:, :], slot_no[:, :], None, ALU.is_equal))
            assert st.n == VR_PLACE
            st.then(ve.tensor_scalar(tile_expert[:, :], iota_s[:, 0:NT], first_tile[:, 1:2], None, ALU.is_ge))
            for e in range(2, NE):
                st.then(ve.scalar_tensor_tensor(tile_expert[:, :], iota_s[:, 0:NT], first_tile[:, e:e + 1],
                                                tile_expert[:, :], ALU.is_ge, ALU.add))
            st.did(ve.tensor_copy(ei[:, :], tile_expert[:, :]))
            assert st.n == VR_TILE
            dve.wait_ge(t_r, R_PLACE)
            spread = seq_of[:, :].unsqueeze(1).broadcast_to((T, NT, SB))
            st.then(ve.tensor_tensor(pick[:, :, :], bank[4][0:T, 0:SLOTS].rearrange("p (k q) -> p k q", q=SB),
                                     spread, ALU.mult))
            st.did(ve.tensor_reduce(idf[:, :], pick[:, :, :], AX.X, ALU.add))
            st.then(ve.tensor_tensor(pickw[:, :, :],
                                     bank[5][0:T, 0:SLOTS].rearrange("p (k q) -> p k q", q=SB),
                                     spread, ALU.mult))
            st.did(ve.tensor_scalar(idx[:, :], idf[:, :], tcol[:, 1:2], None, ALU.add))
            assert st.n == VR_ROWS
            st.then(ve.tensor_reduce(wt[:, :], pickw[:, :, :], AX.X, ALU.add))
            assert st.n == VR_ALL
            stage_one_done(dve)
            dve.wait_ge(c_b2, 16)

            def fin(i, p):
                st = Steps(dve, v_fin, 3, i)
                e = dve.value_load(ei[0:1, ds(i, 1)], min_val=0, max_val=NE - 1)
                dve.wait_ge(t_dn, i + 1)
                need(dve, c_s[p], 16 * turns(i, p))
                st.then(ve.tensor_tensor(res[:, p, :], eD[p][0:T, DM:2 * DM], b2c[:, ds(e * DM, DM)],
                                         ALU.add))
                st.then(ve.tensor_tensor(res[:, p, :], eD[p][0:T, 0:DM], res[:, p, :], ALU.add))
                st.did(ve.scalar_tensor_tensor(res[:, p:p + 1, :], res[:, p:p + 1, :], wt[:, ds(i, 1)],
                                               resid[:, ds(i, 1), :], ALU.mult, ALU.add))

            def at(s, par):
                if tile(s + 1):
                    i, p = s + 1, (par + 1) % 2
                    dve.wait_ge(a_b, i + 1)
                    need(dve, t_up, left_by(i, 2))
                    ve.tensor_tensor(bTl[0:DH, p, :], eB[0:DH, 0:2 * T], bTh[0:DH, p, :].bitcast(F32),
                                     ALU.subtract).then_inc(v_bl, 1)
                if tile(s + 2):
                    i, p = s + 2, par
                    dve.wait_ge(c_g[p], 16 * (turns(i, p) + 1))
                    need(dve, t_b, left_by(i))
                    ve.tensor_scalar(bb[:, p, :], rows[:, p, 0:DM], rows[:, p, DM:DM + 1],
                                     rows[:, p, DM + 1:DM + 2], ALU.subtract, ALU.mult).then_inc(v_b, 1)
                    ve.tensor_copy(resid[:, ds(i, 1), :], rows[:, p:p + 1, 0:DM]).then_inc(v_b, 1)
                if tile(s - 2):
                    fin(s - 2, par)
                if tile(s - 1):
                    i, p = s - 1, (par + 1) % 2
                    for f in range(2):
                        dve.wait_ge(a_hh, 2 * i + f + 1)
                        need(dve, t_dn, left_by(i))
                        ve.tensor_tensor(hTl[:, p, f * HT:(f + 1) * HT], eH[f][:, 0:HT],
                                         hTh[:, p, f * HT:(f + 1) * HT].bitcast(F32), ALU.subtract)\
                          .then_inc(v_hl, 1)

            tiles(dve, at, -2)

        def stage_two_pe(pe):
            te = nc.tensor
            averages_done(pe)
            pe.wait_ge(p_mask, 15)
            for c in range(2):
                last = te.matmul(bank[3][0:NSEQ, 0:NE], means[:, c, :], WgT[:, c, :],
                                 start=(c == 0), stop=(c == 1))
            last.then_inc(t_r, 1)
            pe.wait_ge(v_r, VR_CHOICE)
            te.matmul(bank[3][0:NSEQ, 8:8 + NE], tri[:, :], choice[:, :], start=True, stop=True)
            te.matmul(bank[3][0:NSEQ, 16:16 + NE], ones[0:NSEQ, 0:NSEQ], choice[:, :], start=True, stop=True)\
              .then_inc(t_r, 1)
            pe.wait_ge(v_r, VR_PLACE)
            te.matmul(bank[4][0:T, 0:SLOTS], rowid[:, :], slot[:, :], start=True, stop=True)
            te.matmul(bank[5][0:T, 0:SLOTS], wcol[:, :], slot[:, :], start=True, stop=True).then_inc(t_r, 1)
            pe.wait_ge(v_r, VR_ALL)
            pe.wait_ge(p_clear, 3)
            pe.wait_ge(p_w1, 2 * PIECES)

            def at(s, par):
                def up(f, e):
                    need(pe, a_gelu, 2 * (s - 1) + f + 1)
                    n = 0
                    for c in range(2):
                        k = DH + c
                        w = ds(e * (2 * FF) + (c * FF + f * FH), FH)
                        for a, b in ((bTh, W1h), (bTh, W1l), (bTl, W1h)):
                            last = te.matmul(eU[f][0:T, 0:FH], a[0:k, par, c * T:(c + 1) * T], b[0:k, w],
                                             start=(n == 0), stop=(n == 5))
                            n += 1
                    last.then_inc(t_up, 1)

                if tile(s + 1):
                    i, p = s + 1, (par + 1) % 2
                    pe.wait_ge(v_b, 2 * i + 1)
                    need(pe, v_bl, i)
                    for c in range(2):
                        last = te.transpose(eB[0:DH, c * T:(c + 1) * T], bb[:, p, c * DH:(c + 1) * DH],
                                            ident[0:T, 0:T])
                    last.then_inc(t_b, 1)
                if tile(s):
                    e = pe.value_load(ei[0:1, ds(s, 1)], min_val=0, max_val=NE - 1)
                    pe.wait_ge(v_bl, s + 1)
                    up(0, e)
                if tile(s - 2):
                    i, p = s - 2, par
                    e_down = pe.value_load(ei[0:1, ds(i, 1)], min_val=0, max_val=NE - 1)
                    pe.wait_ge(v_hl, 2 * i + 2)
                    need(pe, v_fin, 3 * (i - 2) + 2)
                    def rest(c):
                        te.matmul(eD[p][0:T, DM:2 * DM], hTl[:, p, c * T:(c + 1) * T],
                                  W2s[:, ds(e_down * FC + c, 1), 0:DM].rearrange("p a d -> p (a d)"),
                                  start=False, stop=False, skip_group_check=True)

                    for c in range(FC):
                        if c > 0:
                            rest(c)
                        last = te.matmul(eD[p][0:T, 0:2 * DM], hTh[:, p, c * T:(c + 1) * T],
                                         W2s[:, ds(e_down * FC + c, 1), :].rearrange("p a d -> p (a d)"),
                                         start=(c == 0), stop=(c == FC - 1), skip_group_check=True)
                        if c == 0:
                            rest(c)
                    last.then_inc(t_dn, 1)
                if tile(s - 1):
                    i, p = s - 1, (par + 1) % 2
                    for f in range(2):
                        pe.wait_ge(a_gelu, 2 * i + f + 1)
                        need(pe, v_hl, 2 * (i - 1) + f + 1)
                        for c in range(FC // 2):
                            col = f * FH + c * 128
                            last = te.transpose(eH[f][:, c * T:(c + 1) * T], hg[:, p, col:col + 128],
                                                ident[0:T, 0:T])
                        last.then_inc(t_h, 1)
                if tile(s):
                    up(1, e)

            tiles(pe, at, -1)

        block = ctx.enter_context(nc.Block())

        def raw_weights_read(eng):
            eng.wait_ge(t_wt, PL // 2)
            eng.wait_ge(a_wi, 2)
            eng.wait_ge(v_wi, 1)
            eng.wait_ge(v_wo, NC + 1)

        def bodies(eng, body, first, end, last):
            for g in range(first):
                body(g)
            with eng.Fori(first, end) as g:
                body(g)
            for g in range(end, last + 1):
                body(g)

        def at_index(ap, k):
            return ap[k] if isinstance(k, int) else ap[ds(k, 1)].squeeze(0)

        def apart(eng):
            cell = idle[0:1, 0:1] if eng is nc.vector else idle[0:1, 1:2]
            eng.tensor_tensor(cell, cell, cell, ALU.mult)

        def live(g):
            return not isinstance(g, int) or 0 <= g < NG

        def piece(i):
            return not isinstance(i, int) or 0 <= i < PIECES

        @block.sync
        def _(sp):
            x_t = x.rearrange("(k b) (m r) f -> k m b (r f)", b=SB, r=ST)

            def load_x(k, j):
                need(sp, t_x, 2 * (k - 1))
                sp.dma_start(xraw[:, j, :], at_index(x_t, k)).then_inc(c_x[j], 16)

            for c in range(2):
                sp.dma_start(wtraw[:, c, :], tok_W[c * DH:(c + 1) * DH, :]).then_inc(c_wt[c], 16)
            load_x(0, 0)
            load_x(1, 1)
            sp.dma_start(wiraw[:, :, :], W_in.rearrange("(c p) k -> p c k", p=DH)).then_inc(c_wi, 16)
            for dst, src in ((tokb, tok_b), (gamma, tok_gamma), (beta, tok_beta), (dtb, dt_bias),
                             (alog, A_log)):
                sp.dma_start(dst[:, :], src.partition_broadcast(T)).then_inc(c_const, 16)
            sp.dma_start(woraw[:, :, :], W_out.rearrange("(c p) d -> p c d", p=128)).then_inc(c_const, 16)
            with nc.allow_non_contiguous_dma(reason="small constants by partition"):
                sp.dma_start(lnw[:, :], ln_w.rearrange("(c p) -> p c", p=DH)).then_inc(c_const, 16)
                sp.dma_start(lnb[:, :], ln_b.rearrange("(c p) -> p c", p=DH)).then_inc(c_const, 16)
                sp.dma_start(cw[:, 0, :], conv_w[DI:DI + 128, :]).then_inc(c_const, 16)
                sp.dma_start(cw[:, 1:CH, :], conv_w[0:DI, :].rearrange("(c p) k -> p c k", p=128))\
                  .then_inc(c_const, 16)
                sp.dma_start(cb[:, 0:1], conv_b[DI:DI + 128].rearrange("(p a) -> p a", a=1))\
                  .then_inc(c_const, 16)
                sp.dma_start(cb[:, 1:CH], conv_b[0:DI].rearrange("(c p) -> p c", p=128)).then_inc(c_const, 16)
                sp.dma_start(rmsw[:, :], rms_w.rearrange("(c p) -> p c", p=128)).then_inc(c_const, 16)
                for half in range(2):
                    sp.dma_start(Dc[half * HD:(half + 1) * HD, :],
                                 D.rearrange("(c a) -> a c", a=2)[half, :].partition_broadcast(HD))\
                      .then_inc(c_const, 16)
                for c in range(2):
                    sp.dma_start(WgT[:, c, :], Wg[:, c * DH:(c + 1) * DH].rearrange("e p -> p e"))\
                      .then_inc(c_const, 16)
            w1_t = W1.rearrange("e (c p) f -> (e c) p f", p=DH)
            w2_t = W2.rearrange("e (c p) d -> p (e c) d", p=128)

            def load_experts(i):
                sp.dma_start(w1raw[0:DH, :], at_index(w1_t, i)).then_inc(c_w1, 16)
                sp.dma_start(w1raw[DH:DH + 1, :], b1[ds(i // 2, 1), :]).then_inc(c_w1, 16)
                sp.dma_start(w2raw[:, :, :], w2_t[:, ds(i * (FC // 2), FC // 2), :]).then_inc(c_w2, 16)

            hid_t = hid.rearrange("(k b n) r -> k n b r", b=SB, n=NP)

            def body(g):
                if not isinstance(g, int) or g < NG - 1:
                    load_x(2 * g + 2, 0)
                    load_x(2 * g + 3, 1)
                if live(g - 3):
                    u = g - 3
                    sp.wait_ge(v_o, OV * u + OV_STAT)
                    sp.wait_ge(p_o, PO * u + PO_R)
                    for j in range(2):
                        sp.dma_start(at_index(hid_t, 2 * u + j), hrow[:, j, :]).then_inc(c_hid, 16)
                if live(g - 1):
                    q = g - 1
                    sp.wait_ge(a_si, CH * q + 1)
                    need(sp, t_sd, 4 * (q - 1) + 1)
                    sp.dma_start(CT[:, :], BC[NS:2 * NS, :]).then_inc(c_C, 16)
                if piece(g - 1):
                    need(sp, p_w1, 2 * (g - 1))
                    load_experts(g - 1)

            bodies(sp, body, 3, NG - 1, NG + 2)
            stage_one_done(sp)
            sp.dma_start(b2c[:, :], b2.rearrange("e d -> (e d)").partition_broadcast(T)).then_inc(c_b2, 16)
            for p in range(2):
                sp.wait_ge(c_s[p], 16 * (NT // 2))

        @block.gpsimd
        def _(pool):
            gp = nc.gpsimd
            gp.memset(ident[:, :], 0.0).then_inc(p_ident, 1)
            gp.memset(ones[:, :], 1.0).then_inc(p_mask, 1)
            gp.memset(neg_half[:, :], -0.5).then_inc(p_mask, 1)
            for dst, value in ((eps[:, :], EPS), (minus_one[:, :], -1.0), (var_k[:, 0:1], 1.0),
                               (var_k[:, 1:2], 1.0 + EPS), (var_c[:, 0:1], EPS), (var_c[:, 1:2], EPS * EPS)):
                gp.memset(dst, value).then_inc(p_mask, 1)
            gp.memset(idle[:, :], 0.0).then_inc(p_idle, 1)
            pool.wait_ge(p_idle, 1)
            pool.wait_ge(p_ident, 1)
            gp.affine_select(out=ident[:, :], in_=ident[:, :], compare_op=ALU.not_equal, fill=1.0, base=0,
                             pattern=[[-1, 128]], channel_multiplier=1).then_inc(p_ident, 1)
            pool.wait_ge(p_mask, 8)
            gp.affine_select(out=later[:, :], in_=ones[0:T, 0:NP], compare_op=ALU.is_gt, fill=0.0, base=0,
                             pattern=[[SB, NP]], channel_multiplier=-1).then_inc(p_mask, 1)
            gp.affine_select(out=tri[:, :], in_=ones[0:NSEQ, 0:NSEQ], compare_op=ALU.is_gt, fill=0.0, base=0,
                             pattern=[[1, NSEQ]], channel_multiplier=-1).then_inc(p_mask, 1)
            for dst, pattern, base, by_row in ((k4, [[SB, NSEQ // SB]], 0, 0), (rank, [[-1, NE]], NE, 0),
                                               (iota_s, [[1, SLOTS]], 0, 0), (iota_t, [[1, NP]], 0, 0),
                                               (rowid, [[0, T]], -MISS, NP)):
                gp.iota(dst[:, :], pattern=pattern, base=base, channel_multiplier=by_row,
                        allow_small_or_imprecise_dtypes=True).then_inc(p_mask, 1)
            raw_weights_read(pool)

            def root_a(q, j):
                st = Steps(pool, p_ln[j], LNP, q)
                pool.wait_ge(v_emb, EMB * (2 * q + j) + EMB_STAT)
                st.then(gp.tensor_tensor(rs0[:, j, 0:1], mv0[:, j, 1:2], eps[0:T, 0:1], ALU.add))
                st.did(gp.tensor_tensor(rs0[:, j, 1:2], rs0[:, j, 0:1], neg_half[0:T, 0:1], ALU.pow))
                assert st.n == LNP_RS0

            def scale(q, j):
                st = Steps(pool, p_ln[j], LNP, q)
                st.n = LNP_RS0
                pool.wait_ge(v_ln[j], VLN * q + VLN_H0)
                st.then(gp.tensor_tensor(h0[:, j, :], h0[:, j, :], gamma[:, :], ALU.mult))
                st.did(gp.tensor_tensor(h0[:, j, :], h0[:, j, :], beta[:, :], ALU.add))
                assert st.n == LNP_H0

            def root_b(q, j):
                st = Steps(pool, p_ln[j], LNP, q)
                st.n = LNP_H0
                pool.wait_ge(v_ln[j], VLN * q + VLN_STAT)
                need(pool, a_skip, 2 * (q - 1) + j + 1)
                st.then(gp.tensor_tensor(rs1[:, j, 0:2], mv1[:, j, 1:2].broadcast_to((T, 2)), var_k[0:T, :],
                                         ALU.mult))
                st.then(gp.tensor_tensor(rs1[:, j, 0:2], rs1[:, j, 0:2], var_c[0:T, :], ALU.add))
                st.did(gp.tensor_tensor(rs1[:, j, 2:4], rs1[:, j, 0:2], neg_half[0:T, :], ALU.pow))
                assert st.n == LNP_RS1

            def skip_factors(q, j):
                st = Steps(pool, p_ln[j], LNP, q)
                st.n = LNP_RS1
                st.settle()
                st.did(gp.tensor_tensor(rs1[:, j, 4:5], rs1[:, j, 2:3], ones[0:T, 0:1], ALU.add))
                st.then(gp.tensor_tensor(rs1[:, j, 5:6], rs1[:, j, 2:3], mv1[:, j, 0:1], ALU.mult))
                st.did(gp.tensor_tensor(rs1[:, j, 5:6], rs1[:, j, 5:6], minus_one[0:T, :], ALU.mult))
                assert st.n == LNP_SKIP

            def split_experts(i):
                pool.wait_ge(a_w1, 2 * i + 2)
                gp.tensor_tensor(W1l[:, ds(i * FF, FF)], w1raw[:, :],
                                 W1h[:, ds(i * FF, FF)].bitcast(F32), ALU.subtract).then_inc(p_w1, 1)
                chunks = ds(i * (FC // 2), FC // 2)
                gp.tensor_tensor(W2s[:, chunks, DM:2 * DM], w2raw[:, :, :],
                                 W2s[:, chunks, 0:DM].bitcast(F32), ALU.subtract).then_inc(p_w1, 1)

            def body(g):
                if live(g - 1):
                    scale(g - 1, 1)
                    root_b(g - 1, 1)
                if live(g - 3):
                    pool.wait_ge(v_o, OV * (g - 3) + OV_MS)
                    gp.tensor_tensor(rrms[:, :], msq[:, :], neg_half[0:T, :], ALU.pow).then_inc(p_o, 1)
                if live(g - 2):
                    u = g - 2
                    pool.wait_ge(v_mix, 4 * u + 3)
                    need(pool, t_y, 2 * u)
                    gp.tensor_tensor(
                        mix[:, 1, :, :].rearrange("p h (n q) -> p h n q", q=SB),
                        score[:, 1, :].rearrange("p (n q) -> p n q", q=SB).unsqueeze(1)
                        .broadcast_to((T, H, NP, SB)),
                        prod[:, H:2 * H, :].unsqueeze(3).broadcast_to((T, H, NP, SB)),
                        ALU.mult).then_inc(p_mix, 1)
                if live(g - 1):
                    skip_factors(g - 1, 1)
                if live(g - 3):
                    u = g - 3
                    st = Steps(pool, p_o, PO, u)
                    st.n = PO_RR
                    pool.wait_ge(v_o, OV * u + OV_STAT)
                    st.then(gp.tensor_tensor(var2[:, :], mv2[:, :, 1], eps[0:T, :], ALU.add))
                    st.did(gp.tensor_tensor(hrow[:, :, DM + 1], var2[:, :], neg_half[0:T, :], ALU.pow))
                if live(g):
                    root_a(g, 0)
                    scale(g, 0)
                    root_b(g, 0)
                    skip_factors(g, 0)
                if not isinstance(g, int) or 2 <= g < NG - 1:
                    split_experts(g - 2)
                elif g == NG:
                    split_experts(PIECES - 1)
                if live(g - 1):
                    q = g - 1
                    st = Steps(pool, p_dt, 2, q)
                    pool.wait_ge(v_sp, SP * q + SP_DT)
                    need(pool, v_mix, 4 * (q - 1) + 3)
                    st.did(gp.tensor_tensor(dteye[:, :, :],
                                            eye[:, :].unsqueeze(1).broadcast_to((T, 2 * H, NP)),
                                            dt[:, :].unsqueeze(2).broadcast_to((T, 2 * H, NP)), ALU.mult))
                if live(g):
                    root_a(g, 1)
                if live(g - 1):
                    pool.wait_ge(a_dt, 3 * q + 3)
                    need(pool, t_sd, 4 * (q - 1) + 2)
                    st.did(gp.tensor_tensor(deceye[:, :, :],
                                            eye[:, :].unsqueeze(1).broadcast_to((T, 2 * H, NP)),
                                            dec[:, :].unsqueeze(2).broadcast_to((T, 2 * H, NP)), ALU.mult))
            bodies(pool, body, 3, NG - 1, NG + 2)
            stage_two_pool(pool)

        @block.scalar
        def _(act):
            ac = nc.scalar
            for r in range(PL // 2):
                act.wait_ge(t_wt, r + 1)
                ac.activation(WT[:, 2 * r:2 * r + 2, 0:DM],
                              bank[r][:, 0:2 * DM].rearrange("p (t d) -> p t d", t=2),
                              ACT.Copy).then_inc(a_wt, 1)
            def high(k, j):
                for h in range(2):
                    act.wait_ge(t_x, 2 * k + h + 1)
                    need(act, t_emb, k - 1)
                    ac.activation(xTh[:, j, h * 512:(h + 1) * 512], bT[h][:, :], ACT.Copy).then_inc(a_xh, 1)

            def add_skip(q, j):
                act.wait_ge(p_ln[j], LNP * q + LNP_SKIP)
                ac.activation(skip[:, ds(2 * q + j, 1), :], h0[:, j:j + 1, :], ACT.Identity,
                              bias=rs1[:, j, 5:6], scale=rs1[:, j, 4:5]).then_inc(a_skip, 1)

            def body(g):
                if live(g - 2):
                    u = g - 2
                    for j, b in enumerate((bP[1], bY[0])):
                        act.wait_ge(t_sd, 4 * u + 3 + j)
                        need(act, t_y, 2 * u)
                        ac.activation(xtok[:, j, :], b[0:T, 0:DI], ACT.Copy).then_inc(a_xt, 1)
                if piece(g - 2):
                    i = g - 2
                    act.wait_ge(c_w1, 32 * (i + 1))
                    ac.activation(W1h[:, ds(i * FF, FF)], w1raw[:, :], ACT.Copy).then_inc(a_w1, 1)
                    act.wait_ge(c_w2, 16 * (i + 1))
                    ac.activation(W2s[:, ds(i * (FC // 2), FC // 2), 0:DM], w2raw[:, :, :], ACT.Copy)\
                      .then_inc(a_w1, 1)
                if live(g - 1):
                    q = g - 1
                    act.wait_ge(t_xn, q + 1)
                    need(act, v_xn, q)
                    for c in range(2):
                        ac.activation(xnf[:, c, :], bX[0:DH, c * T2:(c + 1) * T2], ACT.Identity,
                                      bias=lnb[:, c:c + 1], scale=lnw[:, c:c + 1]).then_inc(a_xn, 1)
                    act.wait_ge(a_xn, 3 * q + 2)
                    need(act, t_in, NCH * q)
                    ac.activation(xnh[:, :, :], xnf[:, :, :], ACT.Copy).then_inc(a_xn, 1)
                if live(g + 1):
                    high(2 * g + 2, 0)
                if live(g - 1):
                    add_skip(g - 1, 1)
                if live(g - 1):
                    act.wait_ge(v_dtv, q + 1)
                    need(act, v_sp, SP * q)
                    ac.activation(dtw[:, 0, :], dtv[:, :, :].rearrange("p u h -> p (u h)"), ACT.Abs)\
                      .then_inc(a_dt, 1)
                    act.wait_ge(a_dt, 3 * q + 1)
                    ac.activation(dtw[:, 1, :], dtw[:, 0, :], ACT.Exp, scale=-1.0).then_inc(a_dt, 1)

                    def start(i):
                        act.wait_ge(t_in, NCH * q + i + 1)
                        need(act, v_cv, 3 * CH * (q - 1) + 3 * (i + 1))
                        ac.activation(taps[:, i, :], bP[i % 2][:, 0:T2], ACT.Copy).then_inc(a_cv, 1)
                        need(act, a_si, CH * (q - 1) + i + 1)
                        ac.activation(acc[:, i, :], bP[i % 2][:, 0:T2], ACT.Identity, bias=cb[:, i:i + 1],
                                      scale=cw[:, i, TAPS - 1:TAPS]).then_inc(a_cv, 1)

                    def silu(i):
                        act.wait_ge(v_cv, 3 * CH * q + 3 * (i + 1))
                        if i == 0:
                            need(act, t_sd, 4 * (q - 1) + 1)
                            need(act, c_C, 16 * q)
                        else:
                            need(act, t_sd, 4 * q)
                            need(act, v_gate, 4 * (q - 1) + 3)
                        ac.activation(BC[:, :] if i == 0 else xs[:, i - 1, :], acc[:, i, :], ACT.Silu)\
                          .then_inc(a_si, 1)

                    def gate(i):
                        act.wait_ge(t_in, NCH * q + CH + i + 1)
                        need(act, v_gate, 4 * q)
                        ac.activation(zs[:, i, :], bIn[CH + i][:, 0:T2], ACT.Silu).then_inc(a_z, 1)

                    start(0)
                    start(1)
                    start(2)
                    start(3)
                    silu(0)
                    gate(0)
                    silu(1)
                if live(g - 2):
                    u = g - 2
                    act.wait_ge(v_gate, 4 * u + 4)
                    need(act, t_out, u)
                    ac.activation(gsq[:, :, :], gated[:, :, :], ACT.Square).then_inc(a_sq, 1)
                if live(g - 1):
                    gate(1)
                    gate(2)
                    silu(2)
                    silu(3)
                    act.wait_ge(v_sp, SP * q + SP)
                    need(act, p_dt, 2 * q)
                    ac.activation(dec[:, :], dtA[:, :, :].rearrange("p u h -> p (u h)"), ACT.Exp,
                                  scale=-RATE_UNIT).then_inc(a_dt, 1)
                if live(g):
                    add_skip(g, 0)
                if live(g + 1):
                    high(2 * g + 3, 1)

            high(0, 0)
            act.wait_ge(c_wi, 16)
            ac.activation(WIh[:, :, :], wiraw[:, :, :], ACT.Copy).then_inc(a_wi, 1)
            high(1, 1)
            ac.activation(WDT[:, :, :], wiraw[:, :, WI - H:WI], ACT.Copy).then_inc(a_wi, 1)
            act.wait_ge(c_const, 16 * CONSTS)
            act.wait_ge(v_alog, 1)
            ac.activation(expa[:, :], alogc[:, :], ACT.Exp).then_inc(a_expa, 1)
            raw_weights_read(act)
            bodies(act, body, 3, NG - 1, NG + 1)
            stage_two_act(act)

        @block.vector
        def _(dve):
            ve = nc.vector
            dve.wait_ge(p_ident, 2)
            ve.tensor_reduce(eye[:, :], ident[0:T, 0:T].rearrange("p (n q) -> p n q", q=SB), AX.X, ALU.add)\
              .then_inc(v_mask, 1)
            ve.tensor_reduce(seq_of[:, :], ident[0:T, 0:T].rearrange("p (n q) -> p q n", q=SB), AX.X,
                             ALU.add)\
              .then_inc(v_mask, 1)
            dve.wait_ge(v_mask, 2)
            ve.tensor_copy(same[:, :].rearrange("p (n q) -> p n q", q=SB),
                           seq_of[:, :].unsqueeze(1).broadcast_to((T, NP, SB))).then_inc(v_mask, 1)
            ve.tensor_scalar(mean_of[:, :], seq_of[:, :], 1.0 / NP, None, ALU.mult).then_inc(v_mask, 1)
            dve.wait_ge(v_mask, 4)
            dve.wait_ge(p_idle, 1)
            dve.wait_ge(p_mask, 9)
            for r in range(PL // 2):
                dve.wait_ge(a_wt, r + 1)
                ve.tensor_tensor(WT[:, 2 * r:2 * r + 2, DM:2 * DM],
                                 bank[r][:, 0:2 * DM].rearrange("p (t d) -> p t d", t=2),
                                 WT[:, 2 * r:2 * r + 2, 0:DM].bitcast(F32), ALU.subtract).then_inc(v_wt, 1)
            def low(k, j):
                for h in range(2):
                    dve.wait_ge(a_xh, 2 * k + h + 1)
                    need(dve, t_emb, k - 1)
                    ve.tensor_tensor(xTl[:, j, h * 512:(h + 1) * 512], bT[h][:, :],
                                     xTh[:, j, h * 512:(h + 1) * 512].bitcast(F32), ALU.subtract)\
                      .then_inc(v_xl, 1)

            def resume(sem, per, index, done):
                st = Steps(dve, sem, per, index)
                st.n = done
                if done:
                    st.settle()
                return st

            def embedding(q, j, step):
                st = resume(v_emb, EMB, 2 * q + j, step)
                if step == 0:
                    dve.wait_ge(t_emb, 2 * q + j + 1)
                    need(dve, p_ln[j], LNP * (q - 1) + LNP_RS0)
                    st.did(ve.tensor_tensor(emb[:, j, :], bE[0:T, DM:2 * DM], tokb[:, :], ALU.add))
                elif step == 1:
                    st.did(ve.tensor_tensor(emb[:, j, :], bE[0:T, 0:DM], emb[:, j, :], ALU.add))
                elif step == 2:
                    st.did(ve.bn_stats(st0[:, j, :], emb[:, j, :]))
                else:
                    apart(dve)
                    st.did(ve.bn_aggr(mv0[:, j, :], st0[:, j, :]))

            def norm_a(q, j):
                st = Steps(dve, v_ln[j], VLN, q)
                dve.wait_ge(p_ln[j], LNP * q + LNP_RS0)
                need(dve, a_skip, 2 * (q - 1) + j + 1)
                st.did(ve.tensor_scalar(h0[:, j, :], emb[:, j, :], mv0[:, j, 0:1], rs0[:, j, 1:2],
                                        ALU.subtract, ALU.mult))
                assert st.n == VLN_H0

            def statistics_b(q, j, step):
                if step == 0:
                    dve.wait_ge(p_ln[j], LNP * q + LNP_H0)
                st = resume(v_ln[j], VLN, q, VLN_H0 + step)
                if step == 0:
                    st.did(ve.bn_stats(st1[:, j, :], h0[:, j, :]))
                else:
                    apart(dve)
                    st.did(ve.bn_aggr(mv1[:, j, :], st1[:, j, :]))
                    assert st.n == VLN_STAT

            def norm_b(q, j):
                st = Steps(dve, v_ln[j], VLN, q)
                st.n = VLN_STAT
                dve.wait_ge(p_ln[j], LNP * q + LNP_RS1)
                need(dve, t_xn, q)
                st.did(ve.tensor_scalar(xc[:, j, :], h0[:, j, :], mv1[:, j, 0:1], rs1[:, j, 3:4],
                                        ALU.subtract, ALU.mult))

            def mixing_a(u):
                st = Steps(dve, v_mix, 4, u)
                dve.wait_ge(t_sd, 4 * u + 1)
                need(dve, p_mix, u)
                st.did(ve.tensor_tensor(score[:, :, :], bX[0:T, 0:T2].rearrange("p (u t) -> p u t", u=2),
                                        same[:, :].unsqueeze(1).broadcast_to((T, 2, T)), ALU.mult))
                dve.wait_ge(t_sd, 4 * u + 2)
                st.then(ve.tensor_tensor(fade[:, :, :],
                                         bY[1][0:T, 0:2 * H * NP].rearrange("p (a t) -> p a t", t=NP),
                                         later[:, :].unsqueeze(1).broadcast_to((T, 2 * H, NP)), ALU.mult))
                dve.wait_ge(p_dt, 2 * u + 1)
                st.did(ve.tensor_tensor_scan(prod[:, :, :].rearrange("p a t -> p (a t)"),
                                              fade[:, :, :].rearrange("p a t -> p (a t)"),
                                              dteye[:, :, :].rearrange("p a t -> p (a t)"), 0.0,
                                              ALU.mult, ALU.add))

            def mixing_b(u):
                st = Steps(dve, v_mix, 4, u)
                st.n = 3
                st.settle()
                need(dve, t_y, 2 * u)
                st.did(ve.tensor_tensor(
                    mix[:, 0, :, :].rearrange("p h (n q) -> p h n q", q=SB),
                    score[:, 0, :].rearrange("p (n q) -> p n q", q=SB).unsqueeze(1)
                    .broadcast_to((T, H, NP, SB)),
                    prod[:, 0:H, :].unsqueeze(3).broadcast_to((T, H, NP, SB)), ALU.mult))

            def low_x(q):
                dve.wait_ge(a_xn, 3 * q + 3)
                need(dve, t_in, NCH * q)
                ve.tensor_tensor(xnl[:, :, :], xnf[:, :, :], xnh[:, :, :].bitcast(F32), ALU.subtract)\
                  .then_inc(v_xn, 1)

            def average(u):
                dve.wait_ge(t_mean, u + 1)
                ve.tensor_copy(means[:, :, ds(2 * SB * u, 2 * SB)],
                               bX[0:DH, 0:4 * SB].rearrange("p (c s) -> p c s", c=2))\
                  .then_inc(v_mean, 1)

            def gating_y(u):
                st = Steps(dve, v_gate, 4, u)
                need(dve, t_out, u)
                need(dve, a_sq, u)
                for c in range(NC):
                    dve.wait_ge(t_y, 2 * u + (1 if c < 2 else 2))
                    y = bY[0][:, c * T2:(c + 1) * T2] if c < 2 else bY[1][:, 0:T2]
                    st.did(ve.scalar_tensor_tensor(gated[:, c, :], xs[:, c, :], Dc[:, c:c + 1], y,
                                                   ALU.mult, ALU.add))

            def gating_z(u):
                st = Steps(dve, v_gate, 4, u)
                st.n = NC
                st.settle()
                dve.wait_ge(a_z, NC * u + NC)
                st.did(ve.tensor_tensor(gated[:, :, :], gated[:, :, :], zs[:, :, :], ALU.mult))

            def step_sizes(q):
                dve.wait_ge(t_dt, q + 1)
                need(dve, a_dt, 3 * q)
                need(dve, v_sp, SP * q)
                ve.tensor_tensor(dtv[:, :, :],
                                 bX[0:T, 2 * T2:2 * T2 + 2 * H].rearrange("p (u h) -> p u h", h=H),
                                 dtb[:, :].unsqueeze(1).broadcast_to((T, 2, H)), ALU.add).then_inc(v_dtv, 1)

            def softplus(q, n):
                st = Steps(dve, v_sp, SP, q)
                st.n = n
                u, w, rc, s, s2, p, lp, rl = (dtw[:, i, :] for i in range(1, 9))
                terms = len(LOG1P_TERMS)
                if n == 0:
                    dve.wait_ge(a_dt, 3 * q + 2)
                    st.did(ve.tensor_scalar(w, u, 2.0, None, ALU.add))
                    return
                st.settle()
                if n == 1:
                    st.did(ve.reciprocal(rc, w))
                elif n == 2:
                    st.did(ve.tensor_tensor(s, u, rc, ALU.mult))
                elif n == 3:
                    st.did(ve.tensor_tensor(s2, s, s, ALU.mult))
                elif n == 4:
                    st.did(ve.tensor_scalar(p, s2, LOG1P_TERMS[0], None, ALU.mult))
                elif n < 4 + terms:
                    st.did(ve.scalar_tensor_tensor(p, p, LOG1P_TERMS[n - 4], s2, ALU.add, ALU.mult))
                elif n == 4 + terms:
                    st.did(ve.scalar_tensor_tensor(lp, p, 1.0, s, ALU.add, ALU.mult))
                elif n == 5 + terms:
                    st.did(ve.tensor_scalar(rl, dtv[:, :, :].rearrange("p u h -> p (u h)"), 0.0, None,
                                            ALU.max))
                elif n == 6 + terms:
                    need(dve, p_dt, 2 * (q - 1) + 1)
                    st.did(ve.scalar_tensor_tensor(dt[:, :], lp, 2.0, rl, ALU.mult, ALU.add))
                    assert st.n == SP_DT
                elif n == 7 + terms:
                    st.did(ve.tensor_tensor(dtA[:, :, :], dt[:, :].rearrange("p (u h) -> p u h", u=2),
                                            rate[:, :].unsqueeze(1).broadcast_to((T, 2, H)), ALU.mult))
                else:
                    st.did(ve.tensor_scalar(dtA[:, :, :], dtA[:, :, :], DECAY_MAX / RATE_UNIT, None, ALU.min))

            def convolve(q, i):
                st = Steps(dve, v_cv, 3 * CH, q)
                st.n = 3 * i
                a = acc[:, i, :].rearrange("p (j t) -> p j t", t=T)
                p = taps[:, i, :].rearrange("p (j t) -> p j t", t=T)
                dve.wait_ge(a_cv, 2 * CH * q + 2 * (i + 1))
                for back in (1, 2, 3):
                    if back > 1:
                        st.settle()
                    st.did(ve.scalar_tensor_tensor(
                        a[:, :, back * SB:T], p[:, :, 0:T - back * SB], cw[:, i, TAPS - 1 - back:TAPS - back],
                        a[:, :, back * SB:T], ALU.mult, ALU.add))
                    softplus(q, 3 * i + back - 1)

            def mean_square(u):
                st = Steps(dve, v_o, OV, u)
                dve.wait_ge(t_out, u + 1)
                need(dve, p_o, PO * (u - 1) + PO_RR)
                st.did(ve.tensor_scalar(msq[:, :], bP[0][0:T, 2 * DM:2 * DM + 2], 1.0 / DI, EPS,
                                        ALU.mult, ALU.add))

            def mixed_rows(u, step):
                st = resume(v_o, OV, u, (OV_MS, OV_MS + 2, OV_MS + 4, OV_MS + 6)[step])
                if step == 0:
                    dve.wait_ge(p_o, PO * u + PO_RR)
                    dve.wait_ge(a_skip, 2 * u + 2)
                    need(dve, c_hid, 32 * u)
                    for j in range(2):
                        st.did(ve.scalar_tensor_tensor(
                            hrow[:, j:j + 1, 0:DM],
                            bP[0][0:T, j * DM:(j + 1) * DM].rearrange("p (a d) -> p a d", a=1),
                            rrms[:, j:j + 1], skip[:, ds(2 * u + j, 1), :], ALU.mult, ALU.add))
                elif step == 1:
                    for j in range(2):
                        st.did(ve.bn_stats(st2[:, j, :], hrow[:, j, 0:DM]))
                elif step == 2:
                    apart(dve)
                    for j in range(2):
                        st.did(ve.bn_aggr(mv2[:, j, :], st2[:, j, :]))
                else:
                    st.did(ve.tensor_copy(hrow[:, :, DM], mv2[:, :, 0]))
                    assert st.n == OV_STAT

            def normed_rows(u):
                st = Steps(dve, v_o, OV, u)
                st.n = OV_STAT
                dve.wait_ge(p_o, PO * u + PO_R)
                need(dve, t_mean, u)
                for j in range(2):
                    st.did(ve.tensor_scalar(bn[:, j, :], hrow[:, j, 0:DM], hrow[:, j, DM:DM + 1],
                                            hrow[:, j, DM + 1:DM + 2], ALU.subtract, ALU.mult))

            def body(g):
                if live(g - 1):
                    statistics_b(g - 1, 1, 0)
                if live(g - 3):
                    mean_square(g - 3)
                if live(g - 1):
                    statistics_b(g - 1, 1, 1)
                if live(g - 2):
                    mixing_a(g - 2)
                if live(g - 1):
                    norm_b(g - 1, 1)
                if live(g - 2):
                    mixing_b(g - 2)
                if live(g):
                    low(2 * g + 1, 1)
                for step in range(4):
                    if live(g - 3):
                        mixed_rows(g - 3, step)
                    if live(g):
                        embedding(g, 0, step)
                if live(g - 1):
                    low_x(g - 1)
                if live(g - 2):
                    gating_y(g - 2)
                if live(g - 1):
                    step_sizes(g - 1)
                if live(g - 3):
                    normed_rows(g - 3)
                if live(g + 1):
                    low(2 * g + 2, 0)
                if live(g):
                    norm_a(g, 0)
                if live(g - 1):
                    convolve(g - 1, 0)
                if live(g):
                    statistics_b(g, 0, 0)
                if live(g - 2):
                    gating_z(g - 2)
                if live(g):
                    statistics_b(g, 0, 1)
                if live(g - 1):
                    convolve(g - 1, 1)
                if live(g):
                    norm_b(g, 0)
                if live(g - 1):
                    convolve(g - 1, 2)
                    convolve(g - 1, 3)
                for step in range(4):
                    if live(g - 1) and 3 * CH + step < SP:
                        softplus(g - 1, 3 * CH + step)
                    if live(g):
                        embedding(g, 1, step)
                if live(g - 3):
                    average(g - 3)
                if live(g):
                    norm_a(g, 1)

            low(0, 0)
            dve.wait_ge(a_wi, 1)
            ve.tensor_tensor(WIl[:, :, :], wiraw[:, :, :], WIh[:, :, :].bitcast(F32), ALU.subtract)\
              .then_inc(v_wi, 1)
            dve.wait_ge(c_const, 16 * CONSTS)
            ve.tensor_scalar(alogc[:, :], alog[:, :], LOG_MAX, None, ALU.min).then_inc(v_alog, 1)
            for c in range(NC):
                ve.tensor_scalar(WO[:, c, :], woraw[:, c, :], rmsw[:, c:c + 1], None, ALU.mult)\
                  .then_inc(v_wo, 1)
            dve.wait_ge(a_expa, 1)
            ve.tensor_scalar(rate[:, :], expa[:, :], 1.0 / RATE_UNIT, None, ALU.mult).then_inc(v_wo, 1)
            raw_weights_read(dve)
            bodies(dve, body, 4, NG - 1, NG + 2)
            stage_two_dve(dve)

        @block.tensor
        def _(pe):
            te = nc.tensor
            pe.wait_ge(p_ident, 2)
            for c in range(2):
                pe.wait_ge(c_wt[c], 16)
                for r in range(PL // 2):
                    for t in range(2):
                        by_tap = wtraw[:, c, :].rearrange("p (f t) -> p t f", t=PL)
                        last = te.transpose(bank[r][:, (2 * t + c) * DH:(2 * t + c + 1) * DH],
                                            by_tap[:, 2 * r + t, :], ident[0:DH, 0:DH])
                    if c == 1:
                        last.then_inc(t_wt, 1)
            pe.wait_ge(v_wt, 2)

            def turn_x(k, j, g):
                pe.wait_ge(c_x[j], 16 * (g + 1))
                for h in range(2):
                    need(pe, v_xl, 2 * (k - 1) + h + 1)
                    for r in range(4):
                        last = te.transpose(bT[h][:, r * 128:(r + 1) * 128],
                                            xraw[:, j, (4 * h + r) * F:(4 * h + r + 1) * F], ident[:, :])
                    last.then_inc(t_x, 1)

            def embed(k, j, taps=(0, PL)):
                if isinstance(k, int) and k == 0:
                    pe.wait_ge(v_wt, PL // 2)
                if taps[0] == 0:
                    pe.wait_ge(v_xl, 2 * k + 2)
                    need(pe, v_emb, EMB * (k - 1) + EMB_READ)
                hi = xTh[:, j, :].rearrange("p (r s) -> p r s", s=128)
                lo = xTl[:, j, :].rearrange("p (r s) -> p r s", s=128)
                for t in range(*taps):
                    w = slice(t // ST * SB, t // ST * SB + T)
                    if t > 0:
                        te.matmul(bE[0:T, DM:2 * DM], lo[:, t % ST, w], WT[:, t, 0:DM],
                                  start=False, stop=False, skip_group_check=True)
                    last = te.matmul(bE[0:T, 0:2 * DM], hi[:, t % ST, w], WT[:, t, :],
                                     start=(t == 0), stop=(t == PL - 1), skip_group_check=True)
                    if t == 0:
                        te.matmul(bE[0:T, DM:2 * DM], lo[:, t % ST, w], WT[:, t, 0:DM],
                                  start=False, stop=False, skip_group_check=True)
                if taps[1] == PL:
                    last.then_inc(t_emb, 1)

            def turn_norms(q):
                for j in range(2):
                    pe.wait_ge(v_ln[j], VLN * q + VLN_XC)
                need(pe, v_mix, 4 * (q - 1) + 1)
                need(pe, v_dtv, q)
                for j in range(2):
                    for c in range(2):
                        last = te.transpose(bX[0:DH, c * T2 + j * T:c * T2 + (j + 1) * T],
                                            xc[:, j, c * DH:(c + 1) * DH], ident[0:T, 0:T])
                last.then_inc(t_xn, 1)

            def step_size_inputs(q):
                if isinstance(q, int) and q == 0:
                    pe.wait_ge(a_wi, 2)
                    pe.wait_ge(v_wi, 1)
                pe.wait_ge(a_xn, 3 * q + 3)
                for j in range(2):
                    for c in range(2):
                        last = te.matmul(bX[0:T, 2 * T2 + j * H:2 * T2 + (j + 1) * H],
                                         xnf[:, c, j * T:(j + 1) * T], WDT[:, c, :],
                                         start=(c == 0), stop=(c == 1))
                last.then_inc(t_dt, 1)

            def project(q, chunks):
                pe.wait_ge(v_xn, q + 1)
                cols = [2 * DI] + [DI + 128 * i for i in range(NC)] + [128 * i for i in range(NC)]
                for i in chunks:
                    col = cols[i]
                    if i == 0:
                        need(pe, v_o, OV * (q - 2) + OV_MS + 2)
                    elif i == 1:
                        need(pe, a_xt, 2 * (q - 1) + 1)
                    elif i < CH:
                        pe.wait_ge(a_cv, 2 * CH * q + 2 * (i - 1))
                    elif i == NCH - 1:
                        pe.wait_ge(a_cv, 2 * CH * q + 2 * (CH - 1))
                    else:
                        need(pe, v_gate, NC + (NC + 1) * (q - 1))
                    n = 0
                    for c in range(2):
                        for w, a in ((WIh, xnh), (WIh, xnl), (WIl, xnh)):
                            last = te.matmul(bIn[i][:, 0:T2], w[:, c, col:col + 128], a[:, c, :],
                                             start=(n == 0), stop=(n == 5))
                            n += 1
                    last.then_inc(t_in, 1)

            def prepare(u):
                pe.wait_ge(c_C, 16 * (u + 1))
                pe.wait_ge(v_dtv, u + 1)
                need(pe, v_mean, u - 1)
                for j in range(2):
                    last = te.matmul(bX[0:T, j * T:(j + 1) * T], BC[0:NS, j * T:(j + 1) * T],
                                     CT[:, j * T:(j + 1) * T], start=True, stop=True)
                last.then_inc(t_sd, 1)
                if isinstance(u, int) and u == 0:
                    pe.wait_ge(v_mask, 4)
                pe.wait_ge(p_dt, 2 * u + 2)
                need(pe, v_gate, 4 * (u - 1) + 3)
                te.matmul(bY[1][0:T, 0:2 * H * NP], same[:, :],
                          deceye[:, :, :].rearrange("p a t -> p (a t)"), start=True, stop=True)\
                  .then_inc(t_sd, 1)
                pe.wait_ge(a_si, CH * u + CH)
                pe.wait_ge(a_z, NC * u + 2)
                for j, b in enumerate((bP[1], bY[0])):
                    for c in range(NC):
                        last = te.transpose(b[0:T, c * 128:(c + 1) * 128], xs[:, c, j * T:(j + 1) * T],
                                            ident[:, :])
                    last.then_inc(t_sd, 1)

            def blend(u):
                pe.wait_ge(v_mix, 4 * u + 4)
                pe.wait_ge(p_mix, u + 1)
                pe.wait_ge(a_xt, 2 * u + 2)
                for c in range(NC):
                    y = bY[0][:, c * T2:(c + 1) * T2] if c < 2 else bY[1][:, 0:T2]
                    for j in range(2):
                        for half in range(2):
                            h = 2 * c + half
                            last = te.matmul(y[half * HD:(half + 1) * HD, j * T:(j + 1) * T],
                                             xtok[:, j, h * HD:(h + 1) * HD], mix[:, j, h, :],
                                             start=True, stop=True)
                    if c > 0:
                        last.then_inc(t_y, 1)

            def average(u):
                if isinstance(u, int) and u == 0:
                    pe.wait_ge(v_mask, 4)
                pe.wait_ge(v_o, OV * u + OV)
                pe.wait_ge(v_dtv, min(u + 3, NG) if isinstance(u, int) else u + 3)
                need(pe, v_mean, u)
                for j in range(2):
                    for c in range(2):
                        col = c * 2 * SB + j * SB
                        last = te.matmul(bX[0:DH, col:col + SB], bn[:, j, c * DH:(c + 1) * DH],
                                         mean_of[:, :], start=True, stop=True)
                last.then_inc(t_mean, 1)

            def emit(u):
                if isinstance(u, int) and u == 0:
                    pe.wait_ge(v_wo, NC + 1)
                pe.wait_ge(v_gate, 4 * u + 4)
                for j in range(2):
                    for c in range(NC):
                        te.matmul(bP[0][0:T, j * DM:(j + 1) * DM], gated[:, c, j * T:(j + 1) * T],
                                  WO[:, c, :], start=(c == 0), stop=(c == NC - 1))
                pe.wait_ge(a_sq, u + 1)
                for j in range(2):
                    for c in range(NC):
                        last = te.matmul(bP[0][0:T, 2 * DM + j:2 * DM + j + 1],
                                         gsq[:, c, j * T:(j + 1) * T], ones[:, 0:1],
                                         start=(c == 0), stop=(c == NC - 1))
                last.then_inc(t_out, 1)

            def body(g):
                if live(g - 2):
                    prepare(g - 2)
                if live(g):
                    embed(2 * g, 0)
                if live(g - 1):
                    turn_norms(g - 1)
                if live(g - 2):
                    blend(g - 2)
                if live(g + 1):
                    turn_x(2 * g + 2, 0, g + 1)
                if live(g - 1):
                    step_size_inputs(g - 1)
                cuts = (0, 4, 7, 9, PL)
                if live(g):
                    embed(2 * g + 1, 1, (cuts[0], cuts[1]))
                if live(g - 1):
                    project(g - 1, (0, 1))
                if live(g):
                    embed(2 * g + 1, 1, (cuts[1], cuts[2]))
                if live(g - 1):
                    project(g - 1, (2, 3))
                if live(g):
                    embed(2 * g + 1, 1, (cuts[2], cuts[3]))
                if live(g - 1):
                    project(g - 1, (4, 5, 6))
                if live(g - 3):
                    average(g - 3)
                if live(g):
                    embed(2 * g + 1, 1, (cuts[3], cuts[4]))
                if live(g - 2):
                    pe.wait_ge(a_z, NC * (min(g, NG) if isinstance(g, int) else g))
                    emit(g - 2)
                if live(g + 1):
                    turn_x(2 * g + 3, 1, g + 1)

            turn_x(0, 0, 0)
            turn_x(1, 1, 0)
            bodies(pe, body, 4, NG - 1, NG + 2)
            stage_two_pe(pe)


_INS = ['x', 'L0_tok_W', 'L0_tok_b', 'L0_tok_gamma', 'L0_tok_beta', 'L0_attn_ln_w', 'L0_attn_ln_b',
        'L0_attn_W_in', 'L0_attn_conv_w', 'L0_attn_conv_b', 'L0_attn_dt_bias', 'L0_attn_A_log', 'L0_attn_D',
        'L0_attn_rms_w', 'L0_attn_W_out', 'L0_ffn_Wg', 'L0_ffn_W1', 'L0_ffn_b1', 'L0_ffn_W2', 'L0_ffn_b2']


def kernel(**inputs):
    import numpy as _np
    import concourse.bacc as _bacc
    from concourse import mybir as _mybir
    from concourse.bass_utils import run_bass_kernel_spmd as _run

    nc = _bacc.Bacc("TRN2", target_bir_lowering=False, num_devices=1)
    arrays, args = {}, []
    for name in _INS:
        a = _np.ascontiguousarray(inputs[name])
        arrays[f"in_{name}"] = a
        args.append(nc.dram_tensor(f"in_{name}", a.shape, _mybir.dt.from_np(a.dtype),
                                   kind="ExternalInput").ap())
    nseq, samples, _ = inputs['x'].shape
    width = inputs['L0_tok_W'].shape[0]
    shape = (nseq, (samples - 16) // 8 + 1, width)
    args.append(nc.dram_tensor("out_0", shape, _mybir.dt.float32, kind="ExternalOutput").ap())
    audio_tower(nc, *args)
    r = _run(nc, [arrays], core_ids=[0])
    return r.results[0]["out_0"]
```
